# Optimizing a Trainium2 kernel written in Bass

```python
import numpy as np
import jax
import jax.numpy as jnp

def _softmax(x, axis=-1):
    return jax.nn.softmax(x, axis=axis)

def _gelu(x):
    return jax.nn.gelu(x, approximate=True)

def _silu(x):
    return jax.nn.silu(x)

def _sigmoid(x):
    return jax.nn.sigmoid(x)

def _layernorm(x, axis=-1, eps=1e-05):
    m = jnp.mean(x, axis=axis, keepdims=True)
    v = jnp.var(x, axis=axis, keepdims=True)
    return (x - m) / jnp.sqrt(v + eps)

def _scatter_add(tgt, idx, src, axis=0):
    return tgt.at[idx].add(src)

def _segment_sum(src, seg, n):
    return jax.ops.segment_sum(src, seg, n)
kernel_name = 'mk_gnn_resnorm_d4_gnn_r32_29faef'

def setup_inputs(seed: int=0):
    np.random.seed(seed)
    _w = jnp.asarray

    def _rec_inputs():
        import jax
        import jax.numpy as jnp
        _gk = jax.random.key(seed)
        x = -0.000202 + 1 * jax.random.normal(jax.random.fold_in(_gk, 1), (50000, 128), jnp.float32)
        src = jax.random.randint(jax.random.fold_in(_gk, 2), (25000,), 0, 50000, jnp.int32)
        dst = jnp.minimum((50000 * jax.random.uniform(jax.random.fold_in(_gk, 3), (25000,)) ** 2.0).astype(jnp.int32), 49999)
        _o = jnp.argsort(dst, stable=True)
        src = src[_o]
        dst = dst[_o]
        edge_attr_64 = -9.77346e-05 + 0.999888 * jax.random.normal(jax.random.fold_in(_gk, 12), (25000, 64), jnp.float32)
        return (x, src, dst, edge_attr_64)
    x, src, dst, edge_attr_64 = _rec_inputs()

    def _L0_gnn_setup():
        import jax, jax.numpy as jnp
        import numpy as np
        N_NODES = 50000
        N_EDGES = 25000
        H = 128
        B = 64
        NEG_SLOPE = 0.01
        key = jax.random.key(seed)
        k1, k2, k3, k4, k5 = jax.random.split(key, 5)
        feat = jax.random.normal(k1, (N_NODES, H), dtype=jnp.float32)
        gdf_feat = jax.random.normal(k2, (N_EDGES, B), dtype=jnp.float32)
        W = jax.random.normal(k3, (H, 2 * H + B), dtype=jnp.float32) * 0.05
        b = jnp.zeros((H,), dtype=jnp.float32)
        src = jax.random.randint(k4, (N_EDGES,), 0, N_NODES, dtype=jnp.int64)
        dst = jax.random.randint(k5, (N_EDGES,), 0, N_NODES, dtype=jnp.int64)
        return {'feat': feat, 'gdf_feat': gdf_feat, 'W': W, 'b': b, 'src': src, 'dst': dst}
    _L0_gnn_all = _L0_gnn_setup()
    _L0_gnn_in = {k: v for k, v in _L0_gnn_all.items() if k in ('W', 'b')}
    del _L0_gnn_all

    def _L1_gnn_setup():
        import jax, jax.numpy as jnp
        import numpy as np
        N_NODES = 50000
        N_EDGES = 50000
        F_IN = 128
        UNITS = 128
        LEAKY_SLOPE = 0.2
        key = jax.random.key(seed)
        k1, k2, k3, k4 = jax.random.split(key, 4)
        node_states = jax.random.normal(k1, (N_NODES, F_IN), dtype=jnp.float32)
        edges = jax.random.randint(k2, (N_EDGES, 2), 0, N_NODES, dtype=jnp.int32)
        kernel = jax.random.normal(k3, (F_IN, UNITS), dtype=jnp.float32) * (1.0 / np.sqrt(F_IN))
        kernel_attention = jax.random.normal(k4, (2 * UNITS, 1), dtype=jnp.float32) * (1.0 / np.sqrt(2 * UNITS))
        return {'node_states': node_states, 'edges': edges, 'kernel': kernel, 'kernel_attention': kernel_attention}
    _L1_gnn_all = _L1_gnn_setup()
    _L1_gnn_in = {k: v for k, v in _L1_gnn_all.items() if k in ('kernel', 'kernel_attention')}
    del _L1_gnn_all

    def _L2_gnn_setup():
        import jax, jax.numpy as jnp
        import numpy as np
        N_NODES = 50000
        N_EDGES = 25000
        IN_F = 128
        HID = 128
        OUT_F = 128

        def _mean_aggr(x, src, dst, n):
            s = jax.ops.segment_sum(x[src], dst, num_segments=n)
            cnt = jax.ops.segment_sum(jnp.ones((src.shape[0],), x.dtype), dst, num_segments=n)
            return s / jnp.maximum(cnt, 1.0)[:, None]

        def _sage(x, src, dst, Wl, b, Wr):
            m = _mean_aggr(x, src, dst, x.shape[0])
            return m @ Wl.T + b + x @ Wr.T
        key = jax.random.key(seed)
        ks = jax.random.split(key, 8)
        x = jax.random.normal(ks[0], (N_NODES, IN_F), dtype=jnp.float32)
        edge_index = jax.random.randint(ks[1], (2, N_EDGES), 0, N_NODES, dtype=jnp.int64)
        s1 = 1.0 / np.sqrt(IN_F)
        s2 = 1.0 / np.sqrt(HID)
        return {'x': x, 'edge_index': edge_index, 'layer': 0, 'W1l': jax.random.uniform(ks[2], (HID, IN_F), jnp.float32, -s1, s1), 'b1': jnp.zeros((HID,), jnp.float32), 'W1r': jax.random.uniform(ks[3], (HID, IN_F), jnp.float32, -s1, s1), 'W2l': jax.random.uniform(ks[4], (OUT_F, HID), jnp.float32, -s2, s2), 'b2': jnp.zeros((OUT_F,), jnp.float32), 'W2r': jax.random.uniform(ks[5], (OUT_F, HID), jnp.float32, -s2, s2)}
    _L2_gnn_all = _L2_gnn_setup()
    _L2_gnn_in = {k: v for k, v in _L2_gnn_all.items() if k in ('W1l', 'b1', 'W1r', 'W2l', 'b2', 'W2r')}
    del _L2_gnn_all

    def _L3_gnn_setup():
        import jax, jax.numpy as jnp
        import numpy as np
        import math
        N_NODES = 625
        N_EDGES = 20000
        IN_F = 128
        HID = 32
        HEADS = 4
        OUT_F = 128
        EPS = 1e-05

        def _gat_forward(x, edge_index, qw, kw, ln_gamma, ln_beta, out_w, out_b):
            n = x.shape[0]
            row, col = (edge_index[0], edge_index[1])
            scale = jnp.float32(math.sqrt(HID))
            Q = jnp.einsum('nf,hfd->hnd', x, qw)
            K = jnp.einsum('nf,hfd->hnd', x, kw)
            Qr = Q[:, row]
            alpha = jnp.einsum('hed,hed->he', Qr, K[:, col]) / scale
            seg_max = jax.vmap(lambda a: jax.ops.segment_max(a, col, num_segments=n))(alpha)
            a = jnp.exp(alpha - seg_max[:, col])
            denom = jax.vmap(lambda e: jax.ops.segment_sum(e, col, num_segments=n))(a)
            a = a / denom[:, col]
            msg = Qr * a[..., None]
            agg = jax.vmap(lambda m: jax.ops.segment_sum(m, col, num_segments=n))(msg)
            h = jnp.transpose(agg, (1, 0, 2)).reshape(n, HEADS * HID)
            mu = jnp.mean(h, axis=-1, keepdims=True)
            var = jnp.mean((h - mu) ** 2, axis=-1, keepdims=True)
            h = (h - mu) / jnp.sqrt(var + EPS) * ln_gamma + ln_beta
            h = h * jax.nn.sigmoid(h)
            return h @ out_w + out_b
        key = jax.random.key(seed)
        ks = jax.random.split(key, 8)
        s_in = 1.0 / math.sqrt(IN_F)
        s_cat = 1.0 / math.sqrt(HID * HEADS)
        x = jax.random.normal(ks[0], (N_NODES, IN_F), dtype=jnp.float32)
        edge_index = jax.random.randint(ks[1], (2, N_EDGES), 0, N_NODES, dtype=jnp.int32)
        qw = jax.random.uniform(ks[2], (HEADS, IN_F, HID), jnp.float32, -s_in, s_in)
        kw = jax.random.uniform(ks[3], (HEADS, IN_F, HID), jnp.float32, -s_in, s_in)
        ln_gamma = jnp.ones((HID * HEADS,), jnp.float32)
        ln_beta = jnp.zeros((HID * HEADS,), jnp.float32)
        out_w = jax.random.uniform(ks[4], (HID * HEADS, OUT_F), jnp.float32, -s_cat, s_cat)
        out_b = jax.random.uniform(ks[5], (OUT_F,), jnp.float32, -s_cat, s_cat)
        return {'x': x, 'edge_index': edge_index, 'qw': qw, 'kw': kw, 'ln_gamma': ln_gamma, 'ln_beta': ln_beta, 'out_w': out_w, 'out_b': out_b}
    _L3_gnn_all = _L3_gnn_setup()
    _L3_gnn_in = {k: v for k, v in _L3_gnn_all.items() if k in ('qw', 'kw', 'ln_gamma', 'ln_beta', 'out_w', 'out_b')}
    del _L3_gnn_all
    return {'x': x, 'src': src, 'dst': dst, 'edge_attr_64': edge_attr_64, 'L0_gnn_W': _L0_gnn_in['W'], 'L0_gnn_b': _L0_gnn_in['b'], 'L1_gnn_kernel': _L1_gnn_in['kernel'], 'L1_gnn_kernel_attention': _L1_gnn_in['kernel_attention'], 'L2_gnn_W1l': _L2_gnn_in['W1l'], 'L2_gnn_b1': _L2_gnn_in['b1'], 'L2_gnn_W1r': _L2_gnn_in['W1r'], 'L2_gnn_W2l': _L2_gnn_in['W2l'], 'L2_gnn_b2': _L2_gnn_in['b2'], 'L2_gnn_W2r': _L2_gnn_in['W2r'], 'L3_gnn_qw': _L3_gnn_in['qw'], 'L3_gnn_kw': _L3_gnn_in['kw'], 'L3_gnn_ln_gamma': _L3_gnn_in['ln_gamma'], 'L3_gnn_ln_beta': _L3_gnn_in['ln_beta'], 'L3_gnn_out_w': _L3_gnn_in['out_w'], 'L3_gnn_out_b': _L3_gnn_in['out_b']}

def reference(x, src, dst, edge_attr_64, L0_gnn_W, L0_gnn_b, L1_gnn_kernel, L1_gnn_kernel_attention, L2_gnn_W1l, L2_gnn_b1, L2_gnn_W1r, L2_gnn_W2l, L2_gnn_b2, L2_gnn_W2r, L3_gnn_qw, L3_gnn_kw, L3_gnn_ln_gamma, L3_gnn_ln_beta, L3_gnn_out_w, L3_gnn_out_b):
    import jax
    import jax.numpy as jnp

    def _L0_gnn_ref(feat, gdf_feat, W, b, src, dst):
        import jax, jax.numpy as jnp
        import numpy as np
        N_NODES = 50000
        N_EDGES = 25000
        H = 128
        B = 64
        NEG_SLOPE = 0.01
        n_nodes = feat.shape[0]
        z = jnp.concatenate([feat[src], feat[dst], gdf_feat], axis=-1)
        z = z @ W.T + b
        msg = jax.nn.sigmoid(z) * jnp.where(z > 0, z, NEG_SLOPE * z)
        return jax.ops.segment_sum(msg, dst, num_segments=n_nodes)

    def _L1_gnn_ref(node_states, edges, kernel, kernel_attention):
        import jax, jax.numpy as jnp
        import numpy as np
        N_NODES = 50000
        N_EDGES = 50000
        F_IN = 128
        UNITS = 128
        LEAKY_SLOPE = 0.2
        n_nodes = node_states.shape[0]
        units = kernel.shape[1]
        dst = edges[:, 0]
        src = edges[:, 1]
        h = jnp.matmul(node_states, kernel)
        a_dst = kernel_attention[:units, 0]
        a_src = kernel_attention[units:, 0]
        score_dst = jnp.matmul(h, a_dst)
        score_src = jnp.matmul(h, a_src)
        scores = jax.nn.leaky_relu(score_dst[dst] + score_src[src], negative_slope=LEAKY_SLOPE)
        scores = jnp.exp(jnp.clip(scores, -2.0, 2.0))
        scores_sum = jax.ops.segment_sum(scores, dst, num_segments=n_nodes)
        attention_norm = scores / scores_sum[dst]
        out = jax.ops.segment_sum(h[src] * attention_norm[:, None], dst, num_segments=n_nodes)
        return out

    def _L2_gnn_ref(x, edge_index, layer, W1l, b1, W1r, W2l, b2, W2r):
        import jax, jax.numpy as jnp
        import numpy as np
        N_NODES = 50000
        N_EDGES = 25000
        IN_F = 128
        HID = 128
        OUT_F = 128

        def _mean_aggr(x, src, dst, n):
            s = jax.ops.segment_sum(x[src], dst, num_segments=n)
            cnt = jax.ops.segment_sum(jnp.ones((src.shape[0],), x.dtype), dst, num_segments=n)
            return s / jnp.maximum(cnt, 1.0)[:, None]

        def _sage(x, src, dst, Wl, b, Wr):
            m = _mean_aggr(x, src, dst, x.shape[0])
            return m @ Wl.T + b + x @ Wr.T
        src, dst = (edge_index[0], edge_index[1])
        h = jax.nn.relu(_sage(x, src, dst, W1l, b1, W1r))
        out = _sage(h, src, dst, W2l, b2, W2r)
        return out

    def _L3_gnn_ref(x, edge_index, qw, kw, ln_gamma, ln_beta, out_w, out_b):
        import jax, jax.numpy as jnp
        import numpy as np
        import math
        N_NODES = 625
        N_EDGES = 20000
        IN_F = 128
        HID = 32
        HEADS = 4
        OUT_F = 128
        EPS = 1e-05

        def _gat_forward(x, edge_index, qw, kw, ln_gamma, ln_beta, out_w, out_b):
            n = x.shape[0]
            row, col = (edge_index[0], edge_index[1])
            scale = jnp.float32(math.sqrt(HID))
            Q = jnp.einsum('nf,hfd->hnd', x, qw)
            K = jnp.einsum('nf,hfd->hnd', x, kw)
            Qr = Q[:, row]
            alpha = jnp.einsum('hed,hed->he', Qr, K[:, col]) / scale
            seg_max = jax.vmap(lambda a: jax.ops.segment_max(a, col, num_segments=n))(alpha)
            a = jnp.exp(alpha - seg_max[:, col])
            denom = jax.vmap(lambda e: jax.ops.segment_sum(e, col, num_segments=n))(a)
            a = a / denom[:, col]
            msg = Qr * a[..., None]
            agg = jax.vmap(lambda m: jax.ops.segment_sum(m, col, num_segments=n))(msg)
            h = jnp.transpose(agg, (1, 0, 2)).reshape(n, HEADS * HID)
            mu = jnp.mean(h, axis=-1, keepdims=True)
            var = jnp.mean((h - mu) ** 2, axis=-1, keepdims=True)
            h = (h - mu) / jnp.sqrt(var + EPS) * ln_gamma + ln_beta
            h = h * jax.nn.sigmoid(h)
            return h @ out_w + out_b
        return _gat_forward(x, edge_index, qw, kw, ln_gamma, ln_beta, out_w, out_b)
    edge_index = jnp.stack([src, dst])
    edge_index_t = jnp.stack([src, dst], axis=1)
    x = _layernorm(x + _L0_gnn_ref(x, edge_attr_64, L0_gnn_W, L0_gnn_b, src, dst), axis=-1)
    x = _layernorm(x + _L1_gnn_ref(x, edge_index_t, L1_gnn_kernel, L1_gnn_kernel_attention), axis=-1)
    x = _layernorm(x + _L2_gnn_ref(x, edge_index, 0, L2_gnn_W1l, L2_gnn_b1, L2_gnn_W1r, L2_gnn_W2l, L2_gnn_b2, L2_gnn_W2r), axis=-1)
    x = _layernorm(x + _L3_gnn_ref(x, edge_index, L3_gnn_qw, L3_gnn_kw, L3_gnn_ln_gamma, L3_gnn_ln_beta, L3_gnn_out_w, L3_gnn_out_b), axis=-1)
    return x

_drawn_inputs = setup_inputs


def setup_inputs(seed=0):
    import zlib

    import numpy as np

    out = dict(_drawn_inputs(seed))
    spreads = {'L0_gnn_b': (0.0, 0.1),
     'L2_gnn_b1': (0.0, 0.1),
     'L2_gnn_b2': (0.0, 0.1),
     'L3_gnn_ln_gamma': (1.0, 0.2),
     'L3_gnn_ln_beta': (0.0, 0.288)}
    factors = {'L3_gnn_kw': 3.931}
    for name, (base, spread) in spreads.items():
        noise = np.random.default_rng([zlib.crc32(name.encode()), seed]).standard_normal(out[name].shape)
        drawn = base * np.exp(spread * noise) if base else spread * noise
        out[name] = jnp.asarray(drawn.astype(out[name].dtype))
    for name, factor in factors.items():
        out[name] = (out[name] * factor).astype(out[name].dtype)
    return out
```

```python
import concourse.bass as bass
from concourse import mybir
from contextlib import ExitStack

P = 128
F = 128
FE = 64
N_NODES = 50000
N_EDGES = 25000
EP = 125
T = N_EDGES // EP
SLOTS = P * T
J = 4
STEPS = T // J
DENSE_FULL = N_NODES // (P * J)
DENSE_DONE = DENSE_FULL * P * J
TAIL_P, TAIL_J = 112, 3
DENSE_STEPS = DENSE_FULL + 1
MAP_P = 125
HEADS, HID = 4, 32
EPS = 1e-5
FAR = 1 << 20
PAD_NODE = 65535
LOW = 1e30
DOUBLINGS = [1, 2, 4, 8, 16, 32, 64, 128]

assert EP * T == N_EDGES and T % J == 0 and DENSE_DONE + TAIL_P * TAIL_J == N_NODES


class Step:

    def __init__(self, k, b):
        self.k, self.b = k, b

    def first_use(self):
        return isinstance(self.k, int) and self.k == 0

    def index(self):
        return 2 * self.k + self.b


class Signal:

    def __init__(self, sem, base, per):
        self.sem, self.base, self.per = sem, base, per

    def at(self, steps):
        return self.base + self.per * steps


class Ring:

    def __init__(self, sems, base, n, rounds):
        self.sems, self.base, self.n = sems, base, n
        self.end = base + 16 * n * rounds


def wait_done(eng, signal, g):
    eng.wait_ge(signal.sem, signal.per * g.index() + (signal.base + signal.per))


def wait_part(eng, signal, g, part):
    eng.wait_ge(signal.sem, signal.per * g.index() + (signal.base + part))


def wait_free(eng, signal, g):
    if not g.first_use():
        eng.wait_ge(signal.sem, signal.per * g.index() + (signal.base - signal.per))


def wait_previous(eng, signal, g):
    if not (isinstance(g.k, int) and g.index() == 0):
        eng.wait_ge(signal.sem, signal.per * g.index() + signal.base)


def wait_landed(eng, ring, g):
    eng.wait_ge(ring.sems[g.b], 16 * ring.n * g.k + (ring.base + 16 * ring.n))


def wait_drained(eng, ring, g):
    if not g.first_use():
        eng.wait_ge(ring.sems[g.b], 16 * ring.n * g.k + ring.base)


def wait_all(eng, ring):
    for b in range(2):
        eng.wait_ge(ring.sems[b], ring.end)


def settle(eng):
    eng.nop(nofuse=True)


def pipeline(eng, count, looped, stages):
    longest = max(lag for lag, _ in stages)

    def at(s):
        for lag, stage in stages:
            if 0 <= s - lag < count:
                stage(Step((s - lag) // 2, (s - lag) % 2))

    first = (longest + 3) // 2 * 2
    loops = (looped - first) // 2
    for s in range(first):
        at(s)
    with eng.Fori(0, loops) as i:
        for h in range(2):
            for lag, stage in stages:
                stage(Step(i + (first + h - lag) // 2, (h - lag) % 2))
    for s in range(first + 2 * loops, count + longest):
        at(s)


def gnn_program(nc, x, src, dst, edge_attr, w0, b0, w_gat, att, w1l, b1, w1r, w2l, b2, w2r,
                qw, kw, gamma, beta, out_w, out_b, out):
    fp32 = mybir.dt.float32
    i32 = mybir.dt.int32
    ALU = mybir.AluOpType
    ACT = mybir.ActivationFunctionType
    AX = mybir.AxisListType.X

    ctx = ExitStack()
    with ctx:
        def sb(name, shape, dt=fp32):
            return ctx.enter_context(nc.sbuf_tensor(name, shape, dt))

        def sem(name):
            return ctx.enter_context(nc.semaphore(name))

        def sem2(name):
            return [sem(f"{name}{b}") for b in range(2)]

        def table(name, rows):
            return nc.dram_tensor(name, (rows, F), fp32, kind="Internal").ap()

        x1_nodes, x2_nodes = (table(n, N_NODES) for n in ("x1_nodes", "x2_nodes"))
        h1_table, x3_table = (table(n, SLOTS + N_NODES) for n in ("h1_table", "x3_table"))
        x2_slots = table("x2_slots", SLOTS)
        q_rows = table("q_rows", SLOTS)
        ACC_W = F + HEADS
        gat_sums = nc.dram_tensor("gat_sums", (DENSE_STEPS * P * J, ACC_W), fp32, kind="Internal").ap()
        acc_dump = nc.dram_tensor("acc_dump", (SLOTS, ACC_W), fp32, kind="Internal").ap()
        node_map = nc.dram_tensor("node_map", (N_NODES, 1), i32, kind="Internal").ap()

        def slot_rows(tab, g):
            v = tab[0:SLOTS, :].rearrange("(p t) f -> p (t f)", p=P)
            return v[:, bass.ds(g.index() * (J * F), J * F)]

        def acc_rows(g):
            v = acc_dump.rearrange("(p t) f -> p (t f)", p=P)
            return v[:, bass.ds(g.index() * (J * ACC_W), J * ACC_W)]

        def is_tail(g):
            return isinstance(g.k, int) and g.index() == DENSE_FULL

        def dense_shape(g):
            return (TAIL_P, TAIL_J) if is_tail(g) else (P, J)

        def node_rows(tab, base, g):
            pn, jn = dense_shape(g)
            rows = tab[bass.ds(g.index() * (P * J) + base, pn * jn), :]
            return rows.rearrange("(p j) f -> p j f", p=pn)

        def sums_rows(g):
            rows = gat_sums[bass.ds(g.index() * (P * J), P * J), :]
            return rows.rearrange("(p j) f -> p (j f)", p=P)

        ident = sb("ident", [P, P])
        ones = sb("ones", [P, P])
        upper = sb("upper", [P, P])
        lower = sb("lower", [P, P])
        w0_sb = sb("w0_sb", [P, 2 * F + FE])
        natural = {n: sb(f"{n}_sb", [P, F]) for n in ("w_gat", "w1l", "w1r", "w2l", "w2r")}
        w0s_t, w0d_t, wgat_t, w1l_t, w1r_t, w2l_t, w2r_t = (sb(n, [P, F]) for n in ("w0s_t", "w0d_t", "wgat_t", "w1l_t", "w1r_t", "w2l_t", "w2r_t"))
        w0e_t = sb("w0e_t", [FE + 1, F])
        qw_sb, kw_sb = sb("qw_sb", [P, HEADS, HID]), sb("kw_sb", [P, HEADS, HID])
        outw_sb = sb("outw_sb", [P, F])
        outb_bc = sb("outb_bc", [P, F])
        b2_row = sb("b2_row", [1, J, F])
        cols = sb("cols", [P, 8])
        b1_col, gamma_col, beta_col, adst_col, asrc_col, sbeta_col = (cols[:, i:i + 1] for i in range(6))
        col_bc = sb("col_bc", [P, 3, P])
        vdst_bc, vsrc_bc, local3_bc = sb("vdst_bc", [P, F]), sb("vsrc_bc", [P, F]), sb("local3_bc", [P, F])

        dst_i = sb("dst_i", [P, T + 2], i32)
        d = sb("d", [P, T + 2])
        src_i = sb("src_i", [P, T], i32)
        dst_safe_i = sb("dst_safe_i", [P, T], i32)
        table_index = sb("table_index", [P, T], i32)
        canon_slot_i = sb("canon_slot_i", [P, T], i32)
        map_index = sb("map_index", [P, T], i32)
        out_index = sb("out_index", [P, T], i32)
        slot_i = sb("slot_i", [P, T], i32)
        slot = sb("slot", [P, T])
        keep, canon, in_first, in_open, first_done = (sb(n, [P, T]) for n in ("keep", "canon", "in_first", "in_open", "first_done"))
        canon_inner = sb("canon_inner", [P, T])
        undone = sb("undone", [P, len(DOUBLINGS), T])
        spread = sb("spread", [P, T])
        tmp_t = sb("tmp_t", [P, T])
        tmp_t2 = sb("tmp_t2", [P, T])
        source_key = sb("source_key", [P, T])
        dummy_row = sb("dummy_row", [P, 2])
        alpha = sb("alpha", [P, T, HEADS])
        seg_max = sb("seg_max", [P, T, HEADS])
        tmp_a = sb("tmp_a", [P, T, HEADS])
        neg_half = sb("neg_half", [P, J])
        one_p = sb("one_p", [P, 16])
        has_first, fix_slot, open_last, carry_p, score_fix = (one_p[:, i:i + 1] for i in range(5))
        fix_idx = sb("fix_idx", [P, 4], i32)
        fix_read, fix_write, fix_out, fix_node = (fix_idx[:, i:i + 1] for i in range(4))
        fix_f = sb("fix_f", [P, 4])
        diag = sb("diag", [P, 2 + 2 * HEADS, P])
        sum_carry = sb("sum_carry", [P, P])
        back_carry = sb("back_carry", [P, P])
        max_pen = sb("max_pen", [P, 4, P])
        max_row = sb("max_row", [P, 2, HEADS, P])
        max_extra = sb("max_extra", [P, 4, HEADS])

        def ring(name, width=F, dt=fp32):
            return sb(name, [P, 2, J, width], dt)

        zeros = sb("zeros", [P, J * ACC_W])
        nsums = ring("n_sums", ACC_W)
        npre = ring("n_pre")
        nsumst = sb("n_sumst", [P, 2, J * F])
        nrecip = sb("n_recip", [P, 2, 2, J])
        nx, nx1, nx2, nh1, nx3, ny, nw, nx4 = (ring(f"n_{n}") for n in ("x", "x1", "x2", "h1", "x3", "y", "w", "x4"))
        nx2t, nh1t = sb("n_x2t", [P, 2, J * F]), sb("n_h1t", [P, 2, J * F])
        src_rows = ring("src_rows", ACC_W)
        own_rows, own2_rows = ring("own_rows"), ring("own2_rows")
        ea_rows = ring("ea_rows", FE)
        msg = ring("msg", ACC_W)
        acc = ring("acc", ACC_W)
        gate = ring("gate")
        bc = ring("bc")
        pre = ring("pre")
        new_rows = ring("new_rows")
        same = sb("same", [P, 2, J, P])
        sums = ring("sums", ACC_W)
        key4 = sb("key4", [P, 2, 5, J])
        add_idx = sb("add_idx", [P, 2, J], i32)
        junk = sb("junk", [P, 3, J, F])
        t_a, t_b, t_c = (sb(n, [P, 2, J * F]) for n in ("t_a", "t_b", "t_c"))
        t_e = sb("t_e", [FE + 1, 2, J * P])
        stats, mv, rstd = (sb(n, [P, 2, J, w]) for n, w in (("stats", 6), ("mv", 2), ("rstd", 1)))
        mv2 = sb("mv2", [P, 2, J, 2])
        rstd2 = sb("rstd2", [P, 2, J, 1])
        nstats, nmv, nr = sb("nstats", [P, 2, 3, J, 6]), sb("nmv", [P, 2, 3, J, 2]), sb("nr", [P, 2, 8, J])
        edge4 = sb("edge4", [P, 2, 6, J])
        recip = sb("recip", [P, 2, J, HEADS])
        out_stage = sb("out_stage", [P, 2, J], i32)
        idx_stage = sb("idx_stage", [P, 2, 2, J], i32)
        val_stage = sb("val_stage", [P, 2, J], i32)
        map_init = sb("map_init", [MAP_P, N_NODES // MAP_P], i32)
        fix_acc = sb("fix_acc", [P, ACC_W])

        ps = [[ctx.enter_context(nc.psum_tensor(f"ps{i}{b}", [P, J * F], fp32)) for b in range(2)] for i in range(4)]

        weights_in, cols_in, dst_in, src_in = sem("weights_in"), sem("cols_in"), sem("dst_in"), sem("src_in")
        consts_made, dst_set, slots_made = sem("consts_made"), sem("dst_set"), sem("slots_made")
        pe_prep, dve_prep, act_prep = sem("pe_prep"), sem("dve_prep"), sem("act_prep")
        map_start, map_index_made, index_made = sem("map_start"), sem("map_index_made"), sem("index_made")
        spread_at, carried, max_at, fix_in, fix_out_sem = (sem(n) for n in ("spread_at", "carried", "max_at", "fix_in", "fix_out_sem"))
        fix_ready = sem("fix_ready")

        PER = {"accd": J}
        LAYERS = {
            "dense0": dict(front=["n_bn0", "n_ag0", "n_ve0", "n_sd0", "n_r0", "n_x"], back=[], rings=dict(n_in=1, n_out=1, n_zero=1),
                           steps=DENSE_STEPS),
            "msg": dict(front=["idxd", "idx2", "tr_a", "cp_a", "tr_b", "cp_b", "tr_e", "cp_e", "mm", "sig", "msg0", "msgd"],
                        back=["accd", "pre", "bn", "ag", "ve", "rs", "newd"],
                        rings=dict(gathered=2 * J, eain=2, dumped=1, scattered=J)),
            "gat": dict(front=["idxd", "score", "e0", "e1", "e2", "expd", "msgd", "keyd", "bcd", "tr_a", "samed", "rep0", "rep1",
                               "rep2", "rep3", "mm", "cp_a"],
                        back=[], rings=dict(gathered=2 * J), parts=dict(added=16 * J)),
            "dense1": dict(front=["n_tr_s", "n_cp_s", "n_mm_s", "n_rc0", "n_rc1", "n_pre",
                                  "n_bn0", "n_ag0", "n_ve0", "n_sd0", "n_r0", "n_x", "x2tp", "x2tc", "h1p", "h1tc", "h1tp",
                                  "h1c", "yp", "y", "bn1", "ag1", "ve1", "sd1", "r1", "x3", "w", "bn2", "ag2", "ve2", "sd2", "r2", "x4"],
                           back=[], rings=dict(n_in=2, n_out=1, n_h1=1, n_x34=2), steps=DENSE_STEPS),
            "map": dict(front=["idxd", "idx2", "mapd"], back=[], rings=dict(marked=J, mapped=J)),
            "sage1": dict(front=["idxd"], back=["accd", "rcp", "msgd", "tr_a", "cp_a", "tr_b", "cp_b", "mm", "cp_c", "mm2", "newd"],
                          rings=dict(gathered=2 * J, kept=1, dumped=1, stored=1)),
            "sage2": dict(front=["idxd"], back=["accd", "rcp", "msgd", "tr_a", "cp_a", "tr_b", "cp_b", "mm", "pre", "bn", "ag", "ve", "rs", "newd"],
                          rings=dict(gathered=J, own=1, own2=1, dumped=1, stored=1)),
            "att1": dict(front=["idxd", "tr_a", "cp_a", "tr_b", "cp_b", "mm", "mm2", "newd", "cp_c", "pre", "score"],
                         back=[], rings=dict(gathered=2 * J, stored=1)),
            "att2": dict(front=["idxd", "msgd"],
                         back=["accd", "rcp", "rcp2", "pre", "bn", "ag", "ve", "rs", "msg0", "tr_a", "cp_a", "mm",
                               "pre2", "pre3", "bn2", "ag2", "ve2", "rs2", "newd"],
                         rings=dict(qin=1, own=1, dumped=1, scattered=J)),
        }
        sems, counts, flow = {}, {}, {}
        for layer, use in LAYERS.items():
            flow[layer] = {}
            steps = use.get("steps", STEPS)
            for kind, total in (("front", steps), ("back", steps + 1)):
                for n in use[kind]:
                    if n not in sems:
                        sems[n], counts[n] = sem(n), 0
                    per = PER.get(n, 1)
                    flow[layer][n] = Signal(sems[n], counts[n], per)
                    counts[n] += per * total
            for n, m in use["rings"].items():
                if n not in sems:
                    sems[n], counts[n] = sem2(n), 0
                flow[layer][n] = Ring(sems[n], counts[n], m, steps // 2)
                counts[n] = flow[layer][n].end
            for n, per in use.get("parts", {}).items():
                flow[layer][n] = Signal(sem(n), 0, per)
        LAYER_NO = {n: i for i, n in enumerate(("msg", "sage1", "sage2", "att2"))}
        FIX = Step(STEPS // 2, 0)

        block = ctx.enter_context(nc.Block())

        def fours(ap, g):
            return ap[:, bass.ds(g.index() * J, J)]

        def nothing(g):
            pass

        @block.sync
        def _(sp):
            sp.wait_ge(dst_set, 1)
            by_p = dst.rearrange("(p t) -> p t", t=T)
            sp.dma_start(dst_i[0:EP, 1:T + 1], by_p).then_inc(dst_in, 16)
            with nc.allow_non_contiguous_dma(reason="one value a partition"):
                sp.dma_start(dst_i[1:EP, 0:1], by_p[0:EP - 1, T - 1:T]).then_inc(dst_in, 16)
                sp.dma_start(dst_i[0:EP - 1, T + 1:T + 2], by_p[1:EP, 0:1]).then_inc(dst_in, 16)
            sp.dma_start(src_i[0:EP, :], src.rearrange("(p t) -> p t", t=T)).then_inc(src_in, 16)
            sp.dma_start(w0_sb[:, :], w0).then_inc(weights_in, 16)
            for n, a in (("w_gat", w_gat), ("w1l", w1l), ("w1r", w1r), ("w2l", w2l), ("w2r", w2r)):
                sp.dma_start(natural[n][:, :], a).then_inc(weights_in, 16)
            sp.dma_start(outw_sb[:, :], out_w).then_inc(weights_in, 16)
            sp.dma_start(w0e_t[FE:FE + 1, :], b0.rearrange("(a n) -> a n", a=1)).then_inc(weights_in, 16)
            sp.dma_start(qw_sb[:, :, :], qw.rearrange("h f d -> f h d")).then_inc(weights_in, 16)
            sp.dma_start(kw_sb[:, :, :], kw.rearrange("h f d -> f h d")).then_inc(weights_in, 16)
            sp.dma_start(b2_row[:, 0, :], b2.rearrange("(a n) -> a n", a=1)).then_inc(weights_in, 16)
            sp.dma_start(outb_bc[:, :], out_b.partition_broadcast(P)).then_inc(weights_in, 16)
            with nc.allow_non_contiguous_dma(reason="one value a partition"):
                for i, a in enumerate((b1, gamma, beta)):
                    sp.dma_start(cols[:, i:i + 1], a.rearrange("(n a) -> n a", a=1)).then_inc(cols_in, 16)
                sp.dma_start(cols[:, 3:4], att[0:F, :]).then_inc(cols_in, 16)
                sp.dma_start(cols[:, 4:5], att[F:2 * F, :]).then_inc(cols_in, 16)

            D = flow["dense0"]

            def dense0_load(g):
                wait_free(sp, D["n_x"], g)
                pn, jn = dense_shape(g)
                sp.dma_start(nx[0:pn, g.b, 0:jn, :], node_rows(x, 0, g)).then_inc(D["n_in"].sems[g.b], 16)

            def dense0_store(g):
                pn, jn = dense_shape(g)
                wait_drained(sp, D["n_zero"], g)
                sp.dma_start(sums_rows(g), zeros[:, :]).then_inc(D["n_zero"].sems[g.b], 16)
                wait_done(sp, D["n_x"], g)
                sp.dma_start(node_rows(x1_nodes, 0, g), nx1[0:pn, g.b, 0:jn, :]).then_inc(D["n_out"].sems[g.b], 16)

            pipeline(sp, DENSE_STEPS, DENSE_FULL, [(3, dense0_store), (0, dense0_load)])

            def dump_and_store(L, tab):
                def dump(g):
                    wait_done(sp, L["accd"], g)
                    sp.dma_start(acc_rows(g), acc[:, g.b, :, :]).then_inc(L["dumped"].sems[g.b], 16)

                def store(g):
                    wait_done(sp, L["newd"], g)
                    sp.dma_start(slot_rows(tab, g), new_rows[:, g.b, :, :]).then_inc(L["stored"].sems[g.b], 16)

                return dump, store

            L = flow["msg"]
            ea_v = edge_attr.rearrange("(p t) f -> p (t f)", p=EP)

            def load_ea(g):
                wait_free(sp, L["tr_e"], g)
                for lo, hi in ((0, 112), (112, EP)):
                    sp.dma_start(ea_rows[lo:hi, g.b, :, :],
                                 ea_v[lo:hi, bass.ds(g.index() * (J * FE), J * FE)]).then_inc(L["eain"].sems[g.b], 16)

            dump, _ = dump_and_store(L, None)
            pipeline(sp, STEPS, STEPS, [(3, dump), (0, load_ea)])

            def load_own(L, signal, tab, to, ring):
                def load(g):
                    wait_free(sp, signal, g)
                    sp.dma_start(to[:, g.b, :, :], slot_rows(tab, g)).then_inc(ring.sems[g.b], 16)
                return load

            D = flow["dense1"]
            sp.wait_ge(flow["gat"]["added"].sem, flow["gat"]["added"].at(STEPS))

            def dense1_load(g):
                wait_free(sp, D["n_pre"], g)
                pn, jn = dense_shape(g)
                sp.dma_start(nx[0:pn, g.b, 0:jn, :], node_rows(x1_nodes, 0, g)).then_inc(D["n_in"].sems[g.b], 16)
                sp.dma_start(nsums[0:pn, g.b, 0:jn, :], node_rows(gat_sums, 0, g)).then_inc(D["n_in"].sems[g.b], 16)

            def dense1_store_x2(g):
                pn, jn = dense_shape(g)
                wait_done(sp, D["n_x"], g)
                sp.dma_start(node_rows(x2_nodes, 0, g), nx2[0:pn, g.b, 0:jn, :]).then_inc(D["n_out"].sems[g.b], 16)

            def dense1_store_h1(g):
                pn, jn = dense_shape(g)
                wait_done(sp, D["h1c"], g)
                sp.dma_start(node_rows(h1_table, SLOTS, g), nh1[0:pn, g.b, 0:jn, :]).then_inc(D["n_h1"].sems[g.b], 16)

            def dense1_store_x34(g):
                pn, jn = dense_shape(g)
                wait_done(sp, D["x3"], g)
                sp.dma_start(node_rows(x3_table, SLOTS, g), nx3[0:pn, g.b, 0:jn, :]).then_inc(D["n_x34"].sems[g.b], 16)
                wait_done(sp, D["x4"], g)
                sp.dma_start(node_rows(out, 0, g), nx4[0:pn, g.b, 0:jn, :]).then_inc(D["n_x34"].sems[g.b], 16)

            pipeline(sp, DENSE_STEPS, DENSE_FULL,
                     [(9, dense1_store_x34), (7, dense1_store_h1), (5, dense1_store_x2), (0, dense1_load)])

            L = flow["sage1"]

            def keep_x2(g):
                wait_landed(sp, L["gathered"], g)
                sp.dma_start(slot_rows(x2_slots, g), own_rows[:, g.b, :, :]).then_inc(L["kept"].sems[g.b], 16)

            dump, store = dump_and_store(L, h1_table)
            pipeline(sp, STEPS, STEPS, [(5, store), (2, dump), (0, keep_x2)])
            L = flow["sage2"]
            wait_all(sp, flow["sage1"]["kept"])
            sp.wait_ge(fix_out_sem, 16 * 2)
            dump, store = dump_and_store(L, x3_table)
            h1_own = load_own(L, L["tr_b"], h1_table, own_rows, L["own"])
            x2_own = load_own(L, L["pre"], x2_slots, own2_rows, L["own2"])

            def both(g):
                h1_own(g)
                x2_own(g)

            pipeline(sp, STEPS, STEPS, [(6, store), (2, dump), (0, both)])
            L = flow["att1"]
            _, store = dump_and_store(dict(L, accd=L["newd"]), q_rows)
            pipeline(sp, STEPS, STEPS, [(2, store)])
            L = flow["att2"]
            wait_all(sp, flow["att1"]["stored"])
            sp.wait_ge(fix_out_sem, 16 * 3)

            def load_q(g):
                wait_free(sp, L["msgd"], g)
                sp.dma_start(src_rows[:, g.b, :, 0:F], slot_rows(q_rows, g).rearrange("p (j f) -> p j f", f=F))\
                    .then_inc(L["qin"].sems[g.b], 16)

            dump, _ = dump_and_store(L, None)
            pipeline(sp, STEPS, STEPS, [(2, dump), (0, load_q), (3, load_own(L, L["pre3"], x3_table, own_rows, L["own"]))])
            sp.wait_ge(fix_out_sem, 16 * 4)
            wait_all(sp, L["scattered"])

        @block.gpsimd
        def _(pool):
            g_ = nc.gpsimd
            g_.memset(dst_i[:, :], PAD_NODE)
            g_.memset(src_i[:, :], 0)
            g_.memset(ident[:, :], 0.0)
            g_.memset(ones[:, :], 1.0)
            g_.memset(upper[:, :], 1.0)
            g_.memset(neg_half[:, :], -0.5)
            g_.memset(lower[:, :], 1.0).then_inc(consts_made, 1)
            pool.wait_ge(consts_made, 1)
            g_.memset(dst_i[:, 0:1], -1)
            g_.memset(dst_i[:, T + 1:T + 2], -1).then_inc(dst_set, 1)
            g_.affine_select(out=ident[:, :], in_=ident[:, :], compare_op=ALU.not_equal, fill=1.0, base=0,
                             pattern=[[-1, P]], channel_multiplier=1)
            g_.affine_select(out=upper[:, :], in_=upper[:, :], compare_op=ALU.is_gt, fill=0.0, base=0,
                             pattern=[[1, P]], channel_multiplier=-1)
            g_.affine_select(out=lower[:, :], in_=lower[:, :], compare_op=ALU.is_gt, fill=0.0, base=0,
                             pattern=[[-1, P]], channel_multiplier=1)
            g_.iota(slot_i[:, :], pattern=[[1, T]], base=0, channel_multiplier=T)
            g_.iota(map_init[:, :], pattern=[[1, N_NODES // MAP_P]], base=SLOTS, channel_multiplier=N_NODES // MAP_P)
            g_.memset(src_rows[:, :, :, :], 0.0)
            g_.memset(msg[:, :, :, :], 0.0)
            g_.memset(acc[:, :, :, :], 0.0)
            g_.memset(zeros[:, :], 0.0)
            g_.iota(dummy_row[:, 0:1], pattern=[[0, 1]], base=N_NODES, channel_multiplier=1,
                    allow_small_or_imprecise_dtypes=True)
            g_.memset(ea_rows[:, :, :, :], 0.0).then_inc(consts_made, 1)
            pool.wait_ge(consts_made, 2)
            g_.memset(src_rows[:, :, :, F:F + 1], 1.0).then_inc(consts_made, 1)

            def mark_and_look_up():
                pool.dma_start(node_map.rearrange("(p t) a -> p (t a)", p=MAP_P), map_init[:, :]).then_inc(map_start, 16)
                pool.wait_ge(map_start, 16)
                L = flow["map"]
                pool.wait_ge(map_index_made, 1)

                def mark(g):
                    wait_drained(pool, L["marked"], g)
                    g_.tensor_copy(idx_stage[:, g.b, 0, :], fours(map_index, g))
                    g_.tensor_copy(val_stage[:, g.b, :], fours(slot_i, g)).then_inc(L["idxd"].sem, 1)
                    wait_done(pool, L["idxd"], g)
                    settle(pool)
                    for j in range(J):
                        g_.indirect_dma_start(
                            out=node_map[:, :], out_offset=bass.IndirectOffsetOnAxis(ap=idx_stage[:, g.b, 0, j:j + 1], axis=0),
                            in_=val_stage[:, g.b, j:j + 1], in_offset=None,
                            bounds_check=N_NODES - 1, oob_is_err=False).then_inc(L["marked"].sems[g.b], 16)

                pipeline(pool, STEPS, STEPS, [(0, mark)])
                wait_all(pool, L["marked"])

                def look_up(g):
                    wait_free(pool, L["mapd"], g)
                    g_.tensor_copy(idx_stage[:, g.b, 1, :], fours(src_i, g)).then_inc(L["idx2"].sem, 1)
                    wait_done(pool, L["idx2"], g)
                    settle(pool)
                    for j in range(J):
                        g_.indirect_dma_start(
                            out=val_stage[:, g.b, j:j + 1], out_offset=None, in_=node_map[:, :],
                            in_offset=bass.IndirectOffsetOnAxis(ap=idx_stage[:, g.b, 1, j:j + 1], axis=0))\
                            .then_inc(L["mapped"].sems[g.b], 16)

                def keep_looked_up(g):
                    wait_landed(pool, L["mapped"], g)
                    g_.tensor_copy(fours(table_index, g), val_stage[:, g.b, :]).then_inc(L["mapd"].sem, 1)

                pipeline(pool, STEPS, STEPS, [(0, look_up), (1, keep_looked_up)])
                pool.wait_ge(L["mapd"].sem, L["mapd"].at(STEPS))

            def inv_root(L, g, jn=J, before="ve", after="rs", at=rstd):
                wait_done(pool, L[before], g)
                g_.tensor_tensor(at[:, g.b, 0:jn, 0], at[:, g.b, 0:jn, 0], neg_half[:, 0:jn], ALU.pow).then_inc(L[after].sem, 1)

            def inv_root2(L, g, jn=J):
                inv_root(L, g, jn, "ve2", "rs2", rstd2)

            def stage_indices(L, g, arrays):
                for i, a in enumerate(arrays):
                    last = g_.tensor_copy(idx_stage[:, g.b, i, :], fours(a, g))
                last.then_inc(L["idxd"].sem, 1)
                wait_done(pool, L["idxd"], g)
                settle(pool)

            def gather(L, g, i, tab, to, width=F):
                for j in range(J):
                    g_.indirect_dma_start(
                        out=to[:, g.b, j, 0:width], out_offset=None, in_=tab,
                        in_offset=bass.IndirectOffsetOnAxis(ap=idx_stage[:, g.b, i, j:j + 1], axis=0))\
                        .then_inc(L["gathered"].sems[g.b], 16)

            def fix_gather(L, own, idx, own_used, more=()):
                n = LAYER_NO["att2" if L is flow["att2"] else next(k for k in flow if flow[k] is L)]
                wait_all(pool, L["dumped"])
                pool.wait_ge(own_used.sem, own_used.at(STEPS))
                g_.indirect_dma_start(out=fix_acc[:, :], out_offset=None, in_=acc_dump[:, :],
                                      in_offset=bass.IndirectOffsetOnAxis(ap=fix_read, axis=0)).then_inc(fix_in, 16)
                g_.indirect_dma_start(out=own_rows[:, 0, 0, :], out_offset=None, in_=own,
                                      in_offset=bass.IndirectOffsetOnAxis(ap=idx, axis=0)).then_inc(fix_in, 16)
                g_.indirect_dma_start(out=own2_rows[:, 0, 0, :], out_offset=None, in_=more[0] if more else own,
                                      in_offset=bass.IndirectOffsetOnAxis(ap=idx, axis=0)).then_inc(fix_in, 16)
                pool.wait_ge(fix_in, 48 * (n + 1))
                return n

            def fix_scatter(L, tab, idx, rows, n, out_ring="stored"):
                wait_all(pool, L[out_ring])
                pool.wait_ge(L["newd"].sem, L["newd"].at(STEPS + 1))
                g_.indirect_dma_start(out=tab, out_offset=bass.IndirectOffsetOnAxis(ap=idx, axis=0),
                                      in_=new_rows[:, 0, 0, :], in_offset=None,
                                      bounds_check=rows - 1, oob_is_err=False).then_inc(fix_out_sem, 16)
                pool.wait_ge(fix_out_sem, 16 * (n + 1))

            pool.wait_ge(index_made, 1)
            L = flow["msg"]

            def gather_ends(g):
                wait_free(pool, L["pre"], g)
                stage_indices(L, g, (src_i, dst_safe_i))
                gather(L, g, 0, x[:, :], src_rows)
                gather(L, g, 1, x[:, :], own_rows)

            def scatter_rows(L, tab, stage):
                def scatter(g):
                    wait_drained(pool, L["scattered"], g)
                    g_.tensor_copy(out_stage[:, g.b, :], fours(out_index, g)).then_inc(L[stage].sem, 1)
                    wait_done(pool, L[stage], g)
                    wait_done(pool, L["newd"], g)
                    settle(pool)
                    for j in range(J):
                        g_.indirect_dma_start(
                            out=tab, out_offset=bass.IndirectOffsetOnAxis(ap=out_stage[:, g.b, j:j + 1], axis=0),
                            in_=new_rows[:, g.b, j, :], in_offset=None,
                            bounds_check=N_NODES - 1, oob_is_err=False).then_inc(L["scattered"].sems[g.b], 16)
                return scatter

            scatter_x1 = scatter_rows(L, x1_nodes[:, :], "idx2")

            def scatter_x1_after_local(g):
                if isinstance(g.k, int) and g.index() == 0:
                    wait_all(pool, flow["dense0"]["n_out"])
                    wait_all(pool, flow["dense0"]["n_zero"])
                scatter_x1(g)

            pipeline(pool, STEPS, STEPS, [(0, gather_ends), (2, lambda g: inv_root(L, g)), (4, scatter_x1_after_local)])
            n = fix_gather(L, x[:, :], fix_node, L["pre"])
            inv_root(L, FIX, 1)
            fix_scatter(L, x1_nodes[:, :], fix_out, N_NODES, n, "scattered")

            G = flow["gat"]

            def gather_x1(g):
                wait_free(pool, G["msgd"], g)
                wait_free(pool, G["score"], g)
                stage_indices(G, g, (src_i, dst_safe_i))
                gather(G, g, 0, x1_nodes[:, :], own_rows)
                gather(G, g, 1, x1_nodes[:, :], src_rows)

            def add_sums(g):
                wait_done(pool, G["cp_a"], g)
                wait_done(pool, G["rep2"], g)
                for j in range(J):
                    pool.wait_ge(G["added"].sem, (G["added"].per * g.index()) + 16 * j)
                    settle(pool)
                    g_.indirect_dma_start(
                        out=gat_sums[:, :], out_offset=bass.IndirectOffsetOnAxis(ap=add_idx[:, g.b, j:j + 1], axis=0),
                        in_=sums[:, g.b, j, :], in_offset=None, compute_op=ALU.add).then_inc(G["added"].sem, 16)

            pipeline(pool, STEPS, STEPS, [(0, gather_x1), (3, add_sums)])
            mark_and_look_up()

            def gather_layer(name, tabs, own, own_idx, own_used, new, lag, more=()):
                L = flow[name]
                idx = (src_i, dst_safe_i) if len(tabs) > 1 else (table_index,)

                def gather_sources(g):
                    wait_free(pool, L["accd"], g)
                    if len(tabs) > 1:
                        wait_free(pool, L["tr_b"], g)
                        wait_drained(pool, L["kept"], g)
                    stage_indices(L, g, idx)
                    for i, (tab, to) in enumerate(zip(tabs, (src_rows, own_rows))):
                        gather(L, g, i, tab, to)

                pipeline(pool, STEPS, STEPS, [(0, gather_sources)] + ([(lag, lambda g: inv_root(L, g))] if lag else []))
                n = fix_gather(L, own, own_idx, L[own_used], more)
                if lag:
                    inv_root(L, FIX, 1)
                fix_scatter(L, new, fix_write, SLOTS, n)

            for r in ("n_out", "n_h1", "n_x34"):
                wait_all(pool, flow["dense1"][r])
            gather_layer("sage1", (x2_nodes[:, :], x2_nodes[:, :]), x2_nodes[:, :], fix_node, "tr_b", h1_table[:, :], 0)
            gather_layer("sage2", (h1_table[:, :],), h1_table[:, :], fix_read, "pre", x3_table[:, :], 3, more=(x2_slots[:, :],))

            L = flow["att1"]

            def gather_x3(g):
                wait_free(pool, L["tr_b"], g)
                stage_indices(L, g, (table_index, canon_slot_i))
                gather(L, g, 0, x3_table[:, :], src_rows)
                gather(L, g, 1, x3_table[:, :], own_rows)

            pipeline(pool, STEPS, STEPS, [(0, gather_x3)])

            L = flow["att2"]

            pipeline(pool, STEPS, STEPS, [(5, lambda g: inv_root2(L, g)), (1, lambda g: inv_root(L, g)),
                                          (7, scatter_rows(L, out[:, :], "idxd"))])
            n = fix_gather(L, x3_table[:, :], fix_read, L["pre3"])
            inv_root(L, FIX, 1)
            inv_root2(L, FIX, 1)
            fix_scatter(L, out[:, :], fix_out, N_NODES, n, "scattered")

        @block.tensor
        def _(pe):
            te = nc.tensor
            pe.wait_ge(consts_made, 3)
            pe.wait_ge(weights_in, 16 * 12)
            w0s, w0d, w0e = w0_sb[:, 0:F], w0_sb[:, F:2 * F], w0_sb[:, 2 * F:2 * F + FE]
            for i, w in enumerate((w0s, w0d, natural["w_gat"][:, :], natural["w1l"][:, :],
                                   natural["w1r"][:, :], natural["w2l"][:, :], natural["w2r"][:, :])):
                te.transpose(ps[i // 4][0][:, (i % 4) * F:(i % 4 + 1) * F], w, ident[:, :])
            te.transpose(ps[1][0][0:FE, 3 * F:4 * F], w0e, ident[:, :]).then_inc(pe_prep, 1)
            pe.wait_ge(fix_ready, 1)
            for i in range(2):
                last = te.matmul(ps[2][0][:, i * P:(i + 1) * P], ones[:, :], diag[:, i, :], start=True, stop=True)
            last.then_inc(pe_prep, 1)
            pe.wait_ge(spread_at, 1)
            te.matmul(ps[2][0][:, 256:257], back_carry[:, :], fix_f[:, 0:1], start=True, stop=True).then_inc(carried, 1)
            pe.wait_ge(fix_ready, 2)
            te.matmul(ps[3][0][:, 0:F], col_bc[:, 0, :], wgat_t[:, :], start=True, stop=True)
            te.matmul(ps[3][0][:, F:2 * F], col_bc[:, 1, :], wgat_t[:, :], start=True, stop=True)
            te.matmul(ps[3][0][:, 2 * F:3 * F], col_bc[:, 2, :], outw_sb[:, :], start=True, stop=True).then_inc(pe_prep, 1)
            pe.wait_ge(dve_prep, 1)

            def tiles(pn, jn):
                return [(j, slice(j * F, j * F + pn)) for j in range(jn)]

            def transpose_step(L, g, bank, rows, done, copied, jn=J):
                wait_free(pe, L[copied], g)
                for j in range(jn):
                    last = te.transpose(ps[bank][g.b][:, j * F:(j + 1) * F], rows[:, g.b, j, 0:F], ident[:, :])
                last.then_inc(L[done].sem, 1)

            def carry(L, width, used):
                pe.wait_ge(L["accd"].sem, L["accd"].at(STEPS))
                pe.wait_ge(used.sem, used.at(STEPS))
                te.matmul(ps[0][0][:, 0:width], sum_carry[:, :], acc[:, 1, J - 1, 0:width],
                          start=True, stop=True).then_inc(carried, 1)

            L = flow["msg"]

            def transpose_ends(g):
                wait_landed(pe, L["gathered"], g)
                transpose_step(L, g, 0, src_rows, "tr_a", "cp_a")
                transpose_step(L, g, 1, own_rows, "tr_b", "cp_b")
                wait_landed(pe, L["eain"], g)
                wait_free(pe, L["cp_e"], g)
                settle(pe)
                for j in range(J):
                    last = te.transpose(ps[2][g.b][0:FE, j * P:(j + 1) * P], ea_rows[:, g.b, j, :], ident[:, :])
                last.then_inc(L["tr_e"].sem, 1)

            def messages(g):
                wait_done(pe, L["cp_a"], g)
                wait_done(pe, L["cp_b"], g)
                wait_done(pe, L["cp_e"], g)
                wait_free(pe, L["msg0"], g)
                for j in range(J):
                    c = slice(j * F, (j + 1) * F)
                    te.matmul(ps[3][g.b][:, c], t_a[:, g.b, c], w0s_t[:, :], start=True, stop=False)
                    te.matmul(ps[3][g.b][:, c], t_b[:, g.b, c], w0d_t[:, :], start=False, stop=False)
                    last = te.matmul(ps[3][g.b][:, c], t_e[:, g.b, c], w0e_t[:, :], start=False, stop=True)
                last.then_inc(L["mm"].sem, 1)

            pipeline(pe, STEPS, STEPS, [(1, messages), (0, transpose_ends)])
            carry(L, F, L["cp_a"])

            L = flow["gat"]

            def gat_keys(g):
                wait_done(pe, L["bcd"], g)
                transpose_step(L, g, 0, bc, "tr_a", "samed")

            def gat_tile_sums(g):
                wait_done(pe, L["samed"], g)
                wait_done(pe, L["msgd"], g)
                wait_free(pe, L["cp_a"], g)
                for j in range(J):
                    last = te.matmul(ps[2 + j // 2][g.b][:, (j % 2) * ACC_W:(j % 2 + 1) * ACC_W], same[:, g.b, j, :],
                                     msg[:, g.b, j, :], start=True, stop=True)
                last.then_inc(L["mm"].sem, 1)

            pipeline(pe, STEPS, STEPS, [(1, gat_tile_sums), (0, gat_keys)])
            for n in ("samed", "cp_a"):
                pe.wait_ge(L[n].sem, L[n].at(STEPS))

            D = flow["dense1"]

            def dense_transpose_sums(g):
                pn, jn = dense_shape(g)
                wait_landed(pe, D["n_in"], g)
                wait_previous(pe, D["n_cp_s"], g)
                for j, c in tiles(pn, jn):
                    last = te.transpose(ps[0][0][:, c], nsums[0:pn, g.b, j, 0:F], ident[0:pn, 0:pn])
                last.then_inc(D["n_tr_s"].sem, 1)

            def dense_project(g):
                pn, jn = dense_shape(g)
                wait_done(pe, D["n_cp_s"], g)
                wait_free(pe, D["n_pre"], g)
                for j, c in tiles(pn, jn):
                    last = te.matmul(ps[2][g.b][0:pn, j * F:(j + 1) * F], nsumst[:, g.b, c], natural["w_gat"][:, :], start=True, stop=True)
                last.then_inc(D["n_mm_s"].sem, 1)

            def dense_transpose_x2(g):
                pn, jn = dense_shape(g)
                wait_done(pe, D["n_x"], g)
                wait_previous(pe, D["x2tc"], g)
                for j, c in tiles(pn, jn):
                    last = te.transpose(ps[0][1][:, c], nx2[0:pn, g.b, j, :], ident[0:pn, 0:pn])
                last.then_inc(D["x2tp"].sem, 1)

            def dense_h1(g):
                pn, jn = dense_shape(g)
                wait_done(pe, D["x2tc"], g)
                wait_previous(pe, D["h1tc"], g)
                for j, c in ([(0, slice(0, J * F))] if jn == J else tiles(pn, jn)):
                    last = te.matmul(ps[1][0][:, c], w1r_t[:, :], nx2t[:, g.b, c], start=True, stop=True)
                last.then_inc(D["h1p"].sem, 1)

            def dense_y(g):
                pn, jn = dense_shape(g)
                wait_done(pe, D["h1tc"], g)
                wait_previous(pe, D["h1c"], g)
                for j, c in tiles(pn, jn):
                    last = te.transpose(ps[1][1][0:pn, j * F:(j + 1) * F], nh1t[:, g.b, c], ident[:, :])
                last.then_inc(D["h1tp"].sem, 1)
                wait_free(pe, D["y"], g)
                for j, c in tiles(pn, jn):
                    to = ps[3][g.b][0:pn, j * F:(j + 1) * F]
                    te.matmul(to, ones[0:1, 0:pn], b2_row[0:1, 0, :], start=True, stop=False)
                    last = te.matmul(to, nh1t[:, g.b, c], w2r_t[:, :], start=False, stop=True)
                last.then_inc(D["yp"].sem, 1)

            pipeline(pe, DENSE_STEPS, DENSE_FULL, [(6, dense_y), (5, dense_h1), (4, dense_transpose_x2), (1, dense_project),
                                                   (0, dense_transpose_sums)])
            for n in ("n_cp_s", "n_pre", "x2tc", "h1tc", "h1c", "y"):
                pe.wait_ge(D[n].sem, D[n].at(DENSE_STEPS))

            L = flow["sage1"]

            def sage_transpose(g, jn=J):
                wait_done(pe, L["msgd"], g)
                transpose_step(L, g, 0, msg, "tr_a", "cp_a", jn)
                if g is FIX:
                    pe.wait_ge(fix_in, 48 * (LAYER_NO["sage1" if L is flow["sage1"] else "sage2"] + 1))
                else:
                    wait_landed(pe, L["gathered" if L is flow["sage1"] else "own"], g)
                transpose_step(L, g, 1, own_rows, "tr_b", "cp_b", jn)

            def sage_h1(g, jn=J):
                wait_done(pe, L["cp_a"], g)
                wait_done(pe, L["cp_b"], g)
                wait_free(pe, L["cp_c"], g)
                c = slice(0, jn * F)
                te.matmul(ps[2][g.b][:, c], w1l_t[:, :], t_a[:, g.b, c], start=True, stop=False)
                te.matmul(ps[2][g.b][:, c], w1r_t[:, :], t_b[:, g.b, c], start=False, stop=True).then_inc(L["mm"].sem, 1)

            def sage_h1_rows(g, jn=J):
                wait_done(pe, L["cp_c"], g)
                wait_free(pe, L["newd"], g)
                for j in range(jn):
                    c = slice(j * F, (j + 1) * F)
                    last = te.transpose(ps[3][g.b][:, c], t_c[:, g.b, c], ident[:, :])
                last.then_inc(L["mm2"].sem, 1)

            pipeline(pe, STEPS, STEPS, [(2, sage_h1_rows), (1, sage_h1), (0, sage_transpose)])
            carry(L, F + 1, L["cp_a"])
            sage_transpose(FIX, 1)
            sage_h1(FIX, 1)
            sage_h1_rows(FIX, 1)

            L = flow["sage2"]

            def sage_out(g, jn=J):
                wait_done(pe, L["cp_a"], g)
                wait_done(pe, L["cp_b"], g)
                wait_free(pe, L["pre"], g)
                for j in range(jn):
                    c = slice(j * F, (j + 1) * F)
                    te.matmul(ps[3][g.b][:, c], ones[0:1, :], b2_row[0:1, 0, :], start=True, stop=False)
                    te.matmul(ps[3][g.b][:, c], t_a[:, g.b, c], w2l_t[:, :], start=False, stop=False)
                    last = te.matmul(ps[3][g.b][:, c], t_b[:, g.b, c], w2r_t[:, :], start=False, stop=True)
                last.then_inc(L["mm"].sem, 1)

            pipeline(pe, STEPS, STEPS, [(1, sage_out), (0, sage_transpose)])
            carry(L, F + 1, L["cp_a"])
            sage_transpose(FIX, 1)
            sage_out(FIX, 1)

            L = flow["att1"]

            def att_transpose(g):
                wait_landed(pe, L["gathered"], g)
                transpose_step(L, g, 0, src_rows, "tr_a", "cp_a")
                transpose_step(L, g, 1, own_rows, "tr_b", "cp_b")

            def queries_keys(g):
                wait_done(pe, L["cp_a"], g)
                wait_free(pe, L["newd"], g)
                for j in range(J):
                    c = slice(j * F, (j + 1) * F)
                    last = te.matmul(ps[2][g.b][:, c], t_a[:, g.b, c], qw_sb[:, :, :].rearrange("f h d -> f (h d)"), start=True, stop=True)
                last.then_inc(L["mm"].sem, 1)
                wait_done(pe, L["cp_b"], g)
                wait_free(pe, L["cp_c"], g)
                for j in range(J):
                    c = slice(j * F, (j + 1) * F)
                    last = te.matmul(ps[3][g.b][:, c], t_b[:, g.b, c], kw_sb[:, :, :].rearrange("f h d -> f (h d)"), start=True, stop=True)
                last.then_inc(L["mm2"].sem, 1)

            pipeline(pe, STEPS, STEPS, [(1, queries_keys), (0, att_transpose)])
            pe.wait_ge(max_at, 1)
            for i in range(2):
                last = te.matmul(ps[i][0][:, :], ones[:, :],
                                 diag[:, 2 + i * HEADS:2 + (i + 1) * HEADS, :].rearrange("p h q -> p (h q)"), start=True, stop=True)
            last.then_inc(max_at, 1)

            L = flow["att2"]
            pe.wait_ge(max_at, 3)

            def att_back_transpose(g, jn=J):
                wait_done(pe, L["msg0"], g)
                transpose_step(L, g, 0, gate, "tr_a", "cp_a", jn)

            def att_project(g, jn=J):
                wait_done(pe, L["cp_a"], g)
                wait_free(pe, L["pre2"], g)
                for j in range(jn):
                    c = slice(j * F, (j + 1) * F)
                    last = te.matmul(ps[3][g.b][:, c], t_a[:, g.b, c], outw_sb[:, :], start=True, stop=True)
                last.then_inc(L["mm"].sem, 1)

            pipeline(pe, STEPS, STEPS, [(1, att_project), (0, att_back_transpose)])
            pe.wait_ge(L["accd"].sem, L["accd"].at(STEPS))
            carry(L, ACC_W, L["cp_a"])
            att_back_transpose(FIX, 1)
            att_project(FIX, 1)

        @block.scalar
        def _(act):
            sc = nc.scalar
            act.wait_ge(cols_in, 16 * 5)
            sc.activation(sbeta_col, beta_col, ACT.Silu).then_inc(act_prep, 1)

            def roots(D, i, before, after):
                def root(g):
                    pn, jn = dense_shape(g)
                    wait_done(act, D[before], g)
                    at = nr[0:pn, g.b, i, 0:jn]
                    sc.activation(at, at, ACT.Sqrt).then_inc(D[after].sem, 1)
                return root

            pipeline(act, DENSE_STEPS, DENSE_FULL, [(0, roots(flow["dense0"], 0, "n_ve0", "n_sd0"))])

            def copy_out(L, g, bank, to, produced, copied, free, jn=J):
                wait_done(act, L[produced], g)
                wait_free(act, L[free], g)
                sc.activation(to[:, g.b, 0:jn * F], ps[bank][g.b][:, 0:jn * F], ACT.Copy).then_inc(L[copied].sem, 1)

            L = flow["msg"]

            def copy_ends(g):
                copy_out(L, g, 0, t_a, "tr_a", "cp_a", "mm")
                wait_done(act, L["tr_e"], g)
                sc.activation(t_e[0:FE, g.b, :], ps[2][g.b][0:FE, :], ACT.Copy).then_inc(L["cp_e"].sem, 1)

            def sigmoid(g):
                wait_done(act, L["mm"], g)
                wait_free(act, L["msg0"], g)
                sc.activation(gate[:, g.b, :, :].rearrange("p j f -> p (j f)"), ps[3][g.b][:, :], ACT.Sigmoid)\
                    .then_inc(L["sig"].sem, 1)

            pipeline(act, STEPS, STEPS, [(1, sigmoid), (0, copy_ends)])

            L = flow["gat"]

            def exp_scores(g):
                wait_done(act, L["e2"], g)
                wait_free(act, L["msgd"], g)
                sc.activation(edge4[:, g.b, 4, :], edge4[:, g.b, 3, :], ACT.Exp).then_inc(L["expd"].sem, 1)

            def gat_copy(g):
                wait_done(act, L["mm"], g)
                if not g.first_use():
                    act.wait_ge(L["added"].sem, L["added"].per * (g.index() - 1))
                for h in range(2):
                    last = sc.activation(sums[:, g.b, 2 * h:2 * h + 2, :].rearrange("p j f -> p (j f)"),
                                         ps[2 + h][g.b][:, 0:2 * ACC_W], ACT.Copy)
                last.then_inc(L["cp_a"].sem, 1)

            pipeline(act, STEPS, STEPS, [(1, gat_copy), (0, exp_scores)])

            D = flow["dense1"]

            def halves(pn, jn):
                return [slice(0, J * F)] if jn == J else [slice(j * F, j * F + pn) for j in range(jn)]

            def dense_copy_sums(g):
                wait_done(act, D["n_tr_s"], g)
                wait_free(act, D["n_mm_s"], g)
                for c in halves(*dense_shape(g)):
                    last = sc.activation(nsumst[:, g.b, c], ps[0][0][:, c], ACT.Copy)
                last.then_inc(D["n_cp_s"].sem, 1)

            def dense_copy_x2t(g):
                wait_done(act, D["x2tp"], g)
                wait_free(act, D["h1p"], g)
                for c in halves(*dense_shape(g)):
                    last = sc.activation(nx2t[:, g.b, c], ps[0][1][:, c], ACT.Copy)
                last.then_inc(D["x2tc"].sem, 1)

            def dense_relu(g):
                wait_done(act, D["h1p"], g)
                wait_free(act, D["yp"], g)
                for c in halves(*dense_shape(g)):
                    last = sc.activation(nh1t[:, g.b, c], ps[1][0][:, c], ACT.Relu, bias=b1_col)
                last.then_inc(D["h1tc"].sem, 1)

            def dense_copy_h1(g):
                pn, jn = dense_shape(g)
                wait_done(act, D["h1tp"], g)
                wait_drained(act, D["n_h1"], g)
                sc.activation(nh1[0:pn, g.b, 0:jn, :].rearrange("p j f -> p (j f)"), ps[1][1][0:pn, 0:jn * F], ACT.Copy)\
                    .then_inc(D["h1c"].sem, 1)

            pipeline(act, DENSE_STEPS, DENSE_FULL, [
                (8, roots(D, 4, "ve2", "sd2")), (7, roots(D, 2, "ve1", "sd1")), (6, dense_copy_h1), (5, dense_relu),
                (4, dense_copy_x2t), (3, roots(D, 0, "n_ve0", "n_sd0")), (0, dense_copy_sums)])

            L = flow["sage1"]

            def sage_copies(g, jn=J):
                copy_out(L, g, 0, t_a, "tr_a", "cp_a", "mm", jn)
                copy_out(L, g, 1, t_b, "tr_b", "cp_b", "mm", jn)

            def sage_relu(g, jn=J):
                wait_done(act, L["mm"], g)
                wait_free(act, L["mm2"], g)
                sc.activation(t_c[:, g.b, 0:jn * F], ps[2][g.b][:, 0:jn * F], ACT.Relu, bias=b1_col).then_inc(L["cp_c"].sem, 1)

            pipeline(act, STEPS, STEPS, [(1, sage_relu), (0, sage_copies)])
            sage_copies(FIX, 1)
            sage_relu(FIX, 1)

            L = flow["sage2"]
            pipeline(act, STEPS, STEPS, [(0, sage_copies)])
            sage_copies(FIX, 1)

            L = flow["att1"]

            def att_copies(g):
                copy_out(L, g, 0, t_a, "tr_a", "cp_a", "mm")
                copy_out(L, g, 1, t_b, "tr_b", "cp_b", "mm2")

            def queries_keys_out(g):
                wait_done(act, L["mm"], g)
                wait_drained(act, L["stored"], g)
                wait_free(act, L["pre"], g)
                sc.activation(new_rows[:, g.b, :, :].rearrange("p j f -> p (j f)"), ps[2][g.b][:, :], ACT.Copy)\
                    .then_inc(L["newd"].sem, 1)
                wait_done(act, L["mm2"], g)
                sc.activation(gate[:, g.b, :, :].rearrange("p j f -> p (j f)"), ps[3][g.b][:, :], ACT.Copy,
                              scale=float(HID) ** -0.5).then_inc(L["cp_c"].sem, 1)

            pipeline(act, STEPS, STEPS, [(1, queries_keys_out), (0, att_copies)])
            act.wait_ge(max_at, 4)
            sc.activation(alpha[:, :, :].rearrange("p t h -> p (t h)"), tmp_a[:, :, :].rearrange("p t h -> p (t h)"),
                          ACT.Exp).then_inc(max_at, 1)

            L = flow["att2"]

            def silu(g, jn=J):
                wait_done(act, L["tr_a"], g)
                wait_free(act, L["mm"], g)
                sc.activation(t_a[:, g.b, 0:jn * F], ps[0][g.b][:, 0:jn * F], ACT.Silu, bias=beta_col, scale=gamma_col)\
                    .then_inc(L["cp_a"].sem, 1)

            pipeline(act, STEPS, STEPS, [(0, silu)])
            silu(FIX, 1)

        @block.vector
        def _(dve):
            v = nc.vector
            linked = [0]

            def link(ins):
                linked[0] += 1
                ins.then_inc(slots_made, 1)
                dve.wait_ge(slots_made, linked[0])

            first, last_ = d[:, 1:2], d[:, T:T + 1]
            dve.wait_ge(consts_made, 3)
            dve.wait_ge(dst_in, 48)
            dve.wait_ge(src_in, 16)
            v.memset(t_e[FE:FE + 1, :, :], 1.0)
            link(v.tensor_copy(d[:, :], dst_i[:, :]))
            v.tensor_copy(slot[:, :], slot_i[:, :])
            v.tensor_tensor(keep[:, :], d[:, 1:T + 1], d[:, 0:T], ALU.is_equal)
            v.tensor_tensor(canon[:, :], d[:, 1:T + 1], d[:, 2:T + 2], ALU.not_equal)
            v.tensor_scalar(in_first[:, :], d[:, 1:T + 1], first, None, ALU.is_equal)
            v.tensor_scalar(in_open[:, :], d[:, 1:T + 1], last_, None, ALU.is_equal)
            link(v.tensor_scalar_min(dst_safe_i[:, :], d[:, 1:T + 1], float(N_NODES - 1)))
            v.memset(keep[:, 0:1], 0.0)
            link(v.tensor_scalar(tmp_t[:, :], canon[:, :], -float(FAR), float(FAR), ALU.mult, ALU.add))
            link(v.tensor_tensor(map_index[:, :], tmp_t[:, :], d[:, 1:T + 1], ALU.add))
            v.tensor_scalar(open_last, canon[:, T - 1:T], -1.0, 1.0, ALU.mult, ALU.add).then_inc(map_index_made, 1)
            link(v.tensor_tensor(first_done[:, :], in_first[:, :], canon[:, :], ALU.mult))
            link(v.reduce_sum(has_first, first_done[:, :], axis=AX))
            link(v.tensor_tensor(tmp_t[:, :], first_done[:, :], slot[:, :], ALU.mult))
            link(v.reduce_sum(fix_slot, tmp_t[:, :], axis=AX))
            v.tensor_copy(fix_f[:, 0:1], fix_slot)
            link(v.tensor_copy(fix_read, fix_slot))
            link(v.tensor_scalar(fix_f[:, 1:2], has_first, -float(FAR), float(FAR), ALU.mult, ALU.add))
            link(v.tensor_tensor(fix_write, fix_f[:, 1:2], fix_slot, ALU.add))
            v.tensor_tensor(fix_out, fix_f[:, 1:2], first, ALU.add)
            v.tensor_copy(fix_node, dst_safe_i[:, 0:1])
            link(v.tensor_tensor(canon_inner[:, :], canon[:, :], first_done[:, :], ALU.subtract))
            link(v.tensor_scalar(tmp_t[:, :], canon_inner[:, :], -float(FAR), float(FAR), ALU.mult, ALU.add))
            link(v.tensor_tensor(out_index[:, :], tmp_t[:, :], d[:, 1:T + 1], ALU.add))
            link(v.tensor_scalar(tmp_t[:, 0:1], first, float(N_NODES - 1), None, ALU.is_gt))
            link(v.tensor_tensor(dummy_row[:, 1:2], tmp_t[:, 0:1], dummy_row[:, 0:1], ALU.mult))
            link(v.tensor_scalar(source_key[:, :], src_i[:, :], dummy_row[:, 1:2], None, ALU.add))
            link(v.tensor_scalar(in_open[:, :], in_open[:, :], open_last, None, ALU.mult))
            link(v.tensor_scalar(first_done[:, :], in_first[:, :], has_first, None, ALU.mult))
            v.tensor_scalar(diag[:, 0, :], ident[:, :], first, None, ALU.mult)
            v.tensor_scalar(diag[:, 1, :], ident[:, :], last_, None, ALU.mult).then_inc(fix_ready, 1)
            dve.wait_ge(pe_prep, 2)
            first_row, last_row = ps[2][0][:, 0:P], ps[2][0][:, P:2 * P]
            link(v.scalar_tensor_tensor(sum_carry[:, :], first_row, last_, upper[:, :], ALU.is_equal, ALU.mult))
            link(v.scalar_tensor_tensor(back_carry[:, :], last_row, first, lower[:, :], ALU.is_equal, ALU.mult))
            link(v.tensor_scalar(back_carry[:, :], back_carry[:, :], has_first, None, ALU.mult))
            for i, (row, col) in enumerate(((first_row, first), (last_row, first), (first_row, last_), (last_row, last_))):
                link(v.tensor_scalar(max_pen[:, i, :], row, col, None, ALU.is_equal))
            link(v.tensor_scalar(max_pen[:, :, :], max_pen[:, :, :], 1.0, LOW, ALU.subtract, ALU.mult))
            link(v.tensor_scalar(undone[:, 0, :], canon[:, :], -1.0, 1.0, ALU.mult, ALU.add))
            for k in range(1, len(DOUBLINGS)):
                s = DOUBLINGS[k - 1]
                v.tensor_copy(undone[:, k, T - s:T], undone[:, k - 1, T - s:T])
                link(v.tensor_tensor(undone[:, k, 0:T - s], undone[:, k - 1, 0:T - s], undone[:, k - 1, s:T], ALU.mult))

            def spread_back(value, fix, times):
                link(v.tensor_tensor(spread[:, :], value, canon_inner[:, :], ALU.mult))
                for k, s in enumerate(DOUBLINGS):
                    link(v.tensor_tensor(tmp_t[:, 0:T - s], spread[:, s:T], undone[:, k, 0:T - s], ALU.mult))
                    link(v.tensor_tensor(spread[:, 0:T - s], spread[:, 0:T - s], tmp_t[:, 0:T - s], ALU.add))
                link(v.scalar_tensor_tensor(spread[:, :], first_done[:, :], fix, spread[:, :], ALU.mult, ALU.add))
                dve.wait_ge(carried, times)
                link(v.tensor_copy(carry_p, ps[2][0][:, 256:257]))
                link(v.scalar_tensor_tensor(spread[:, :], in_open[:, :], carry_p, spread[:, :], ALU.mult, ALU.add))

            v.memset(junk[:, 0, 0, 0:1], 0.0).then_inc(spread_at, 1)
            spread_back(slot[:, :], fix_slot, 1)
            v.tensor_copy(canon_slot_i[:, :], spread[:, :]).then_inc(index_made, 1)
            dve.wait_ge(pe_prep, 1)
            for i, w in enumerate((w0s_t, w0d_t, wgat_t, w1l_t, w1r_t, w2l_t, w2r_t)):
                v.tensor_copy(w[:, :], ps[i // 4][0][:, (i % 4) * F:(i % 4 + 1) * F])
            v.tensor_copy(w0e_t[0:FE, :], ps[1][0][0:FE, 3 * F:4 * F])
            dve.wait_ge(cols_in, 16 * 5)
            dve.wait_ge(act_prep, 1)
            for i, col in enumerate((adst_col, asrc_col, sbeta_col)):
                last = v.tensor_scalar(col_bc[:, i, :], ones[:, :], col, None, ALU.mult)
            last.then_inc(fix_ready, 1)
            dve.wait_ge(pe_prep, 3)
            dve.wait_ge(weights_in, 16 * 12)
            v.tensor_copy(vdst_bc[:, :], ps[3][0][:, 0:F])
            v.tensor_copy(vsrc_bc[:, :], ps[3][0][:, F:2 * F])
            v.tensor_tensor(local3_bc[:, :], ps[3][0][:, 2 * F:3 * F], outb_bc[:, :], ALU.add).then_inc(dve_prep, 1)
            dve.wait_ge(dve_prep, 1)

            def dense_norm(D, g, rows, i, bn, ag, ve):
                pn, jn = dense_shape(g)
                for j in range(jn):
                    last = v.bn_stats(nstats[0:pn, g.b, i, j, :], rows[0:pn, g.b, j, :])
                last.then_inc(D[bn].sem, 1)
                wait_done(dve, D[bn], g)
                settle(dve)
                for j in range(jn):
                    last = v.bn_aggr(nmv[0:pn, g.b, i, j, :], nstats[0:pn, g.b, i, j, :])
                last.then_inc(D[ag].sem, 1)
                wait_done(dve, D[ag], g)
                v.tensor_scalar_add(nr[0:pn, g.b, 2 * i, 0:jn], nmv[0:pn, g.b, i, 0:jn, 1], EPS).then_inc(D[ve].sem, 1)

            def dense_rows(D, g, rows, to, i, sd, r, made):
                pn, jn = dense_shape(g)
                wait_done(dve, D[sd], g)
                at = nr[0:pn, g.b, 2 * i, 0:jn]
                v.reciprocal(at, at).then_inc(D[r].sem, 1)
                wait_done(dve, D[r], g)
                for j in range(jn):
                    last = v.tensor_scalar(to[0:pn, g.b, j, :], rows[0:pn, g.b, j, :], nmv[0:pn, g.b, i, j, 0:1],
                                           nr[0:pn, g.b, 2 * i, j:j + 1], ALU.subtract, ALU.mult)
                last.then_inc(D[made].sem, 1)

            D0 = flow["dense0"]

            def dense0_stats(g):
                wait_landed(dve, D0["n_in"], g)
                dense_norm(D0, g, nx, 0, "n_bn0", "n_ag0", "n_ve0")

            def dense0_rows(g):
                wait_drained(dve, D0["n_out"], g)
                dense_rows(D0, g, nx, nx1, 0, "n_sd0", "n_r0", "n_x")

            pipeline(dve, DENSE_STEPS, DENSE_FULL, [(1, dense0_rows), (0, dense0_stats)])

            def norm_stats(L, g, rows, jn=J, names=("bn", "ag", "ve"), root=rstd, moments=mv):
                bn, ag, ve = names
                for j in range(jn):
                    last = v.bn_stats(stats[:, g.b, j, :], rows[:, g.b, j, 0:F])
                last.then_inc(L[bn].sem, 1)
                wait_done(dve, L[bn], g)
                settle(dve)
                for j in range(jn):
                    last = v.bn_aggr(moments[:, g.b, j, :], stats[:, g.b, j, :])
                last.then_inc(L[ag].sem, 1)
                wait_done(dve, L[ag], g)
                v.tensor_scalar_add(root[:, g.b, 0:jn, 0], moments[:, g.b, 0:jn, 1], EPS).then_inc(L[ve].sem, 1)

            def norm_rows(L, g, rows, to, jn=J, rs="rs", made="newd", root=rstd, moments=mv):
                if to is new_rows:
                    wait_drained(dve, L["scattered" if "scattered" in L else "stored"], g)
                wait_done(dve, L[rs], g)
                for j in range(jn):
                    last = v.tensor_scalar(to[:, g.b, j, :], rows[:, g.b, j, 0:F], moments[:, g.b, j, 0:1], root[:, g.b, j, :],
                                           ALU.subtract, ALU.mult)
                last.then_inc(L[made].sem, 1)

            def running_sums(L, g, rows, width):
                wait_drained(dve, L["dumped"], g)
                for j in range(J):
                    wait_part(dve, L["accd"], g, j)
                    before = acc[:, g.b, j - 1, 0:width] if j else acc[:, 1 - g.b, J - 1, 0:width]
                    v.scalar_tensor_tensor(acc[:, g.b, j, 0:width], before, keep[:, bass.ds(g.index() * J + j, 1)],
                                           rows[:, g.b, j, 0:width], ALU.mult, ALU.add).then_inc(L["accd"].sem, 1)

            def fix_sums(L, width, times):
                n = LAYER_NO[next(k for k in flow if flow[k] is L)]
                dve.wait_ge(fix_in, 48 * (n + 1))
                dve.wait_ge(carried, times)
                v.tensor_tensor(acc[:, 0, 0, 0:width], fix_acc[:, 0:width], ps[0][0][:, 0:width], ALU.add)\
                    .then_inc(L["accd"].sem, J)

            L = flow["msg"]

            def copy_dst(g):
                wait_done(dve, L["tr_b"], g)
                wait_free(dve, L["mm"], g)
                v.tensor_copy(t_b[:, g.b, :], ps[1][g.b][:, :]).then_inc(L["cp_b"].sem, 1)

            def message_sums(g):
                wait_done(dve, L["sig"], g)
                v.tensor_tensor(msg[:, g.b, :, 0:F], ps[3][g.b][:, :].rearrange("p (j f) -> p j f", f=F), gate[:, g.b, :, :], ALU.mult)\
                    .then_inc(L["msg0"].sem, 1)
                wait_done(dve, L["msg0"], g)
                v.scalar_tensor_tensor(msg[:, g.b, :, 0:F], msg[:, g.b, :, 0:F], 0.01, msg[:, g.b, :, 0:F], ALU.mult, ALU.max)\
                    .then_inc(L["msgd"].sem, 1)
                wait_done(dve, L["msgd"], g)
                running_sums(L, g, msg, F)

            def x1_sums(g, jn=J):
                wait_free(dve, L["newd"], g)
                wait_done(dve, L["accd"], g)
                v.tensor_tensor(pre[:, g.b, 0:jn, :], own_rows[:, g.b, 0:jn, :], acc[:, g.b, 0:jn, 0:F], ALU.add).then_inc(L["pre"].sem, 1)
                wait_done(dve, L["pre"], g)
                norm_stats(L, g, pre, jn)

            def x1_rows(g, jn=J):
                norm_rows(L, g, pre, new_rows, jn)

            pipeline(dve, STEPS, STEPS, [(3, x1_rows), (1, message_sums), (1, x1_sums), (0, copy_dst)])
            fix_sums(L, F, 2)
            x1_sums(FIX, 1)
            x1_rows(FIX, 1)
            L = flow["gat"]

            def edge_scores(g):
                wait_landed(dve, L["gathered"], g)
                for i, (rows, vec) in enumerate(((own_rows, vdst_bc), (src_rows, vsrc_bc))):
                    for j in range(J):
                        last = v.tensor_tensor_reduce(out=junk[:, i, j, :], in0=rows[:, g.b, j, 0:F], in1=vec[:, :], scale=1.0,
                                                      scalar=0.0, op0=ALU.mult, op1=ALU.add, accum_out=edge4[:, g.b, i, j:j + 1])
                last.then_inc(L["score"].sem, 1)
                wait_done(dve, L["score"], g)
                v.tensor_tensor(edge4[:, g.b, 2, :], edge4[:, g.b, 0, :], edge4[:, g.b, 1, :], ALU.add).then_inc(L["e0"].sem, 1)
                wait_done(dve, L["e0"], g)
                v.scalar_tensor_tensor(edge4[:, g.b, 5, :], edge4[:, g.b, 2, :], 0.2, edge4[:, g.b, 2, :], ALU.mult, ALU.max)\
                    .then_inc(L["e1"].sem, 1)
                wait_free(dve, L["expd"], g)
                wait_done(dve, L["e1"], g)
                v.tensor_scalar(edge4[:, g.b, 3, :], edge4[:, g.b, 5, :], -2.0, 2.0, ALU.max, ALU.min).then_inc(L["e2"].sem, 1)

            def edge_keys(g):
                v.tensor_copy(key4[:, g.b, 0, :], fours(source_key, g)).then_inc(L["keyd"].sem, 1)
                wait_free(dve, L["tr_a"], g)
                wait_done(dve, L["keyd"], g)
                for j in range(J):
                    last = v.tensor_scalar(bc[:, g.b, j, :], ones[:, :], key4[:, g.b, 0, j:j + 1], None, ALU.mult)
                last.then_inc(L["bcd"].sem, 1)

            def same_sources(g):
                wait_done(dve, L["tr_a"], g)
                wait_free(dve, L["mm"], g)
                for j in range(J):
                    last = v.tensor_scalar(same[:, g.b, j, :], ps[0][g.b][:, j * P:(j + 1) * P], key4[:, g.b, 0, j:j + 1], None, ALU.is_equal)
                last.then_inc(L["samed"].sem, 1)
                wait_done(dve, L["samed"], g)
                for j in range(J):
                    last = v.tensor_tensor_reduce(out=junk[:, 2, j, :], in0=same[:, g.b, j, :], in1=lower[:, :], scale=1.0,
                                                  scalar=0.0, op0=ALU.mult, op1=ALU.add, accum_out=key4[:, g.b, 1, j:j + 1])
                last.then_inc(L["rep0"].sem, 1)
                v.tensor_scalar(key4[:, g.b, 2, :], key4[:, g.b, 0, :], dummy_row[:, 0:1], None, ALU.subtract)
                wait_done(dve, L["rep0"], g)
                v.tensor_scalar(key4[:, g.b, 3, :], key4[:, g.b, 1, :], 0.0, None, ALU.is_equal).then_inc(L["rep1"].sem, 1)
                wait_done(dve, L["rep1"], g)
                v.tensor_tensor(key4[:, g.b, 4, :], key4[:, g.b, 2, :], key4[:, g.b, 3, :], ALU.mult).then_inc(L["rep3"].sem, 1)
                if not g.first_use():
                    dve.wait_ge(L["added"].sem, L["added"].per * (g.index() - 1))
                wait_done(dve, L["rep3"], g)
                v.tensor_scalar(add_idx[:, g.b, :], key4[:, g.b, 4, :], dummy_row[:, 0:1], None, ALU.add).then_inc(L["rep2"].sem, 1)

            def weighted_rows(g):
                wait_done(dve, L["expd"], g)
                wait_free(dve, L["mm"], g)
                for j in range(J):
                    last = v.tensor_scalar(msg[:, g.b, j, 0:F + 1], src_rows[:, g.b, j, 0:F + 1], edge4[:, g.b, 4, j:j + 1], None, ALU.mult)
                last.then_inc(L["msgd"].sem, 1)

            pipeline(dve, STEPS, STEPS, [(1, weighted_rows), (1, same_sources), (0, edge_keys), (0, edge_scores)])

            D = flow["dense1"]

            def dense_x2_sums(g):
                pn, jn = dense_shape(g)
                wait_landed(dve, D["n_in"], g)
                v.tensor_scalar_max(nrecip[0:pn, g.b, 0, 0:jn], nsums[0:pn, g.b, 0:jn, F], 1e-30).then_inc(D["n_rc0"].sem, 1)
                wait_done(dve, D["n_rc0"], g)
                v.reciprocal(nrecip[0:pn, g.b, 1, 0:jn], nrecip[0:pn, g.b, 0, 0:jn]).then_inc(D["n_rc1"].sem, 1)
                wait_done(dve, D["n_mm_s"], g)
                wait_free(dve, D["n_x"], g)
                wait_done(dve, D["n_rc1"], g)
                for j in range(jn):
                    last = v.scalar_tensor_tensor(npre[0:pn, g.b, j, :], ps[2][g.b][0:pn, j * F:(j + 1) * F], nrecip[0:pn, g.b, 1, j:j + 1],
                                                  nx[0:pn, g.b, j, :], ALU.mult, ALU.add)
                last.then_inc(D["n_pre"].sem, 1)
                wait_done(dve, D["n_pre"], g)
                dense_norm(D, g, npre, 0, "n_bn0", "n_ag0", "n_ve0")

            def dense_x2_rows(g):
                wait_drained(dve, D["n_out"], g)
                wait_free(dve, D["x2tp"], g)
                wait_free(dve, D["y"], g)
                dense_rows(D, g, npre, nx2, 0, "n_sd0", "n_r0", "n_x")

            def dense_y(g):
                pn, jn = dense_shape(g)
                wait_done(dve, D["yp"], g)
                wait_free(dve, D["x3"], g)
                v.tensor_tensor(ny[0:pn, g.b, 0:jn, :].rearrange("p j f -> p (j f)"), ps[3][g.b][0:pn, 0:jn * F],
                                nx2[0:pn, g.b, 0:jn, :].rearrange("p j f -> p (j f)"), ALU.add).then_inc(D["y"].sem, 1)
                wait_done(dve, D["y"], g)
                dense_norm(D, g, ny, 1, "bn1", "ag1", "ve1")

            def dense_x3(g):
                pn, jn = dense_shape(g)
                wait_drained(dve, D["n_x34"], g)
                dense_rows(D, g, ny, nx3, 1, "sd1", "r1", "x3")
                wait_done(dve, D["x3"], g)
                wait_free(dve, D["x4"], g)
                v.tensor_tensor(nw[0:pn, g.b, 0:jn, :], nx3[0:pn, g.b, 0:jn, :],
                                local3_bc[0:pn, None, :].to_broadcast([pn, jn, F]), ALU.add).then_inc(D["w"].sem, 1)
                wait_done(dve, D["w"], g)
                dense_norm(D, g, nw, 2, "bn2", "ag2", "ve2")

            def dense_x4(g):
                dense_rows(D, g, nw, nx4, 2, "sd2", "r2", "x4")

            pipeline(dve, DENSE_STEPS, DENSE_FULL, [(8, dense_x4), (7, dense_x3), (6, dense_y), (4, dense_x2_rows), (2, dense_x2_sums)])

            def new_node_rows(g, jn=J):
                norm_rows(L, g, pre, new_rows, jn)

            def plain_sums(g):
                wait_landed(dve, L["gathered"], g)
                running_sums(L, g, src_rows, F + 1)

            def means(g, jn=J):
                wait_done(dve, L["accd"], g)
                v.reciprocal(edge4[:, g.b, 5, 0:jn], acc[:, g.b, 0:jn, F]).then_inc(L["rcp"].sem, 1)
                wait_free(dve, L["tr_a"], g)
                wait_done(dve, L["rcp"], g)
                for j in range(jn):
                    last = v.tensor_scalar(msg[:, g.b, j, 0:F], acc[:, g.b, j, 0:F], edge4[:, g.b, 5, j:j + 1], None, ALU.mult)
                last.then_inc(L["msgd"].sem, 1)

            def sums_and_means(g):
                plain_sums(g)
                means(g)

            L = flow["sage1"]

            def h1_rows(g, jn=J):
                wait_done(dve, L["mm2"], g)
                wait_drained(dve, L["stored"], g)
                v.tensor_copy(new_rows[:, g.b, 0:jn, :].rearrange("p j f -> p (j f)"), ps[3][g.b][:, 0:jn * F]).then_inc(L["newd"].sem, 1)

            pipeline(dve, STEPS, STEPS, [(3, h1_rows), (0, sums_and_means)])
            fix_sums(L, F + 1, 3)
            means(FIX, 1)
            h1_rows(FIX, 1)

            L = flow["sage2"]

            def x3_sums(g, jn=J):
                if g is FIX:
                    dve.wait_ge(fix_in, 48 * 3)
                else:
                    wait_landed(dve, L["own2"], g)
                wait_done(dve, L["mm"], g)
                wait_free(dve, L["newd"], g)
                v.tensor_tensor(pre[:, g.b, 0:jn, :].rearrange("p j f -> p (j f)"), ps[3][g.b][:, 0:jn * F],
                                own2_rows[:, g.b, 0:jn, :].rearrange("p j f -> p (j f)"), ALU.add).then_inc(L["pre"].sem, 1)
                wait_done(dve, L["pre"], g)
                norm_stats(L, g, pre, jn)

            pipeline(dve, STEPS, STEPS, [(4, new_node_rows), (2, x3_sums), (0, sums_and_means)])
            fix_sums(L, F + 1, 4)
            means(FIX, 1)
            x3_sums(FIX, 1)
            new_node_rows(FIX, 1)

            L = flow["att1"]

            def products(g):
                wait_done(dve, L["newd"], g)
                wait_done(dve, L["cp_c"], g)
                wait_free(dve, L["score"], g)
                v.tensor_tensor(pre[:, g.b, :, :], new_rows[:, g.b, :, :], gate[:, g.b, :, :], ALU.mult).then_inc(L["pre"].sem, 1)
                wait_done(dve, L["pre"], g)
                v.tensor_reduce(alpha[:, bass.ds(g.index() * J, J), :], pre[:, g.b, :, :].rearrange("p j (h e) -> p j h e", e=HID),
                                axis=AX, op=ALU.add).then_inc(L["score"].sem, 1)

            pipeline(dve, STEPS, STEPS, [(2, products)])
            dve.wait_ge(L["score"].sem, L["score"].at(STEPS))
            link(v.tensor_copy(seg_max[:, :, :], alpha[:, :, :]))

            def hop(s, ahead):
                n = T - s
                a, b = (seg_max[:, s:T, :], seg_max[:, 0:n, :]) if ahead else (seg_max[:, 0:n, :], seg_max[:, s:T, :])
                link(v.tensor_tensor(tmp_t[:, 0:n], d[:, 1:1 + n], d[:, 1 + s:1 + T], ALU.is_equal))
                link(v.tensor_scalar(tmp_t[:, 0:n], tmp_t[:, 0:n], 1.0, LOW, ALU.subtract, ALU.mult))
                link(v.tensor_tensor(tmp_a[:, 0:n, :], a, tmp_t[:, 0:n, None].to_broadcast([P, n, HEADS]), ALU.add))
                link(v.tensor_tensor(b, b, tmp_a[:, 0:n, :], ALU.max))

            for s in DOUBLINGS:
                hop(s, False)
            for s in DOUBLINGS:
                hop(s, True)
            for i, t in enumerate((0, T - 1)):
                for h in range(HEADS):
                    last = v.tensor_scalar(diag[:, 2 + i * HEADS + h, :], ident[:, :], seg_max[:, t, h:h + 1], None, ALU.mult)
            last.then_inc(max_at, 1)
            dve.wait_ge(max_at, 2)
            for i in range(4):
                row = ps[i % 2][0][:, :].rearrange("p (h q) -> p h q", q=P)
                link(v.tensor_tensor(max_row[:, 0, :, :], row, max_pen[:, i:i + 1, :].to_broadcast([P, HEADS, P]), ALU.add))
                link(v.tensor_reduce(max_extra[:, i, :], max_row[:, 0, :, :], axis=AX, op=ALU.max))
            v.tensor_tensor(max_extra[:, 0, :], max_extra[:, 0, :], max_extra[:, 1, :], ALU.max)
            link(v.tensor_tensor(max_extra[:, 2, :], max_extra[:, 2, :], max_extra[:, 3, :], ALU.max))
            for i, at in ((0, first), (2, last_)):
                link(v.tensor_scalar(tmp_t[:, :], d[:, 1:T + 1], at, None, ALU.is_equal))
                link(v.tensor_scalar(tmp_t[:, :], tmp_t[:, :], 1.0, LOW, ALU.subtract, ALU.mult))
                link(v.tensor_tensor(tmp_a[:, :, :], tmp_t[:, :, None].to_broadcast([P, T, HEADS]),
                                     max_extra[:, i:i + 1, :].to_broadcast([P, T, HEADS]), ALU.add))
                link(v.tensor_tensor(seg_max[:, :, :], seg_max[:, :, :], tmp_a[:, :, :], ALU.max))
            v.tensor_tensor(tmp_a[:, :, :], alpha[:, :, :], seg_max[:, :, :], ALU.subtract).then_inc(max_at, 2)
            dve.wait_ge(max_at, 5)

            L = flow["att2"]

            def attended_sums(g):
                wait_landed(dve, L["qin"], g)
                a = fours(alpha, g)
                v.tensor_tensor(msg[:, g.b, :, 0:F].rearrange("p j (h e) -> p j h e", e=HID),
                                src_rows[:, g.b, :, 0:F].rearrange("p j (h e) -> p j h e", e=HID),
                                a[:, :, :, None].to_broadcast([P, J, HEADS, HID]), ALU.mult)
                v.tensor_copy(msg[:, g.b, :, F:F + HEADS], a).then_inc(L["msgd"].sem, 1)
                wait_done(dve, L["msgd"], g)
                running_sums(L, g, msg, ACC_W)

            def attended(g, jn=J):
                wait_done(dve, L["accd"], g)
                v.tensor_scalar_max(recip[:, g.b, 0:jn, :], acc[:, g.b, 0:jn, F:ACC_W], 1e-30).then_inc(L["rcp"].sem, 1)
                wait_done(dve, L["rcp"], g)
                v.reciprocal(recip[:, g.b, 0:jn, :], recip[:, g.b, 0:jn, :]).then_inc(L["rcp2"].sem, 1)
                wait_done(dve, L["rcp2"], g)
                wait_free(dve, L["msg0"], g)
                v.tensor_tensor(pre[:, g.b, 0:jn, :].rearrange("p j (h e) -> p j h e", e=HID),
                                acc[:, g.b, 0:jn, 0:F].rearrange("p j (h e) -> p j h e", e=HID),
                                recip[:, g.b, 0:jn, :, None].to_broadcast([P, jn, HEADS, HID]), ALU.mult).then_inc(L["pre"].sem, 1)
                wait_done(dve, L["pre"], g)
                norm_stats(L, g, pre, jn)

            def normed(g, jn=J):
                wait_free(dve, L["tr_a"], g)
                norm_rows(L, g, pre, gate, jn, made="msg0")

            def x4_sums(g, jn=J):
                wait_done(dve, L["mm"], g)
                rows = ps[3][g.b][:, 0:jn * F].rearrange("p (j f) -> p j f", f=F)
                wait_free(dve, L["newd"], g)
                v.tensor_tensor(ny[:, g.b, 0:jn, :], rows, outb_bc[:, None, :].to_broadcast([P, jn, F]), ALU.add).then_inc(L["pre2"].sem, 1)
                if g is FIX:
                    dve.wait_ge(fix_in, 48 * 4)
                else:
                    wait_landed(dve, L["own"], g)
                wait_done(dve, L["pre2"], g)
                v.tensor_tensor(ny[:, g.b, 0:jn, :], ny[:, g.b, 0:jn, :], own_rows[:, g.b, 0:jn, :], ALU.add).then_inc(L["pre3"].sem, 1)
                wait_done(dve, L["pre3"], g)
                norm_stats(L, g, ny, jn, ("bn2", "ag2", "ve2"), rstd2, mv2)

            def x4_rows(g, jn=J):
                norm_rows(L, g, ny, new_rows, jn, "rs2", "newd", rstd2, mv2)

            def sums_then_attended(g):
                attended_sums(g)
                attended(g)

            pipeline(dve, STEPS, STEPS, [(6, x4_rows), (4, x4_sums), (2, normed), (0, sums_then_attended)])
            fix_sums(L, ACC_W, 5)
            attended(FIX, 1)
            normed(FIX, 1)
            x4_sums(FIX, 1)
            x4_rows(FIX, 1)


_INS = ["x", "src", "dst", "edge_attr_64", "L0_gnn_W", "L0_gnn_b", "L1_gnn_kernel", "L1_gnn_kernel_attention",
        "L2_gnn_W1l", "L2_gnn_b1", "L2_gnn_W1r", "L2_gnn_W2l", "L2_gnn_b2", "L2_gnn_W2r", "L3_gnn_qw", "L3_gnn_kw",
        "L3_gnn_ln_gamma", "L3_gnn_ln_beta", "L3_gnn_out_w", "L3_gnn_out_b"]


def kernel(**inputs):
    import numpy as _np
    import concourse.bacc as _bacc
    from concourse import mybir as _mybir
    from concourse.bass_utils import run_bass_kernel_spmd as _run

    nc = _bacc.Bacc("TRN2", target_bir_lowering=False, num_devices=1)
    arrays, args = {}, []
    for name in _INS:
        a = _np.ascontiguousarray(inputs[name])
        arrays[f"in_{name}_dram"] = a
        args.append(nc.dram_tensor(f"in_{name}_dram", a.shape, _mybir.dt.from_np(a.dtype), kind="ExternalInput").ap())
    out = nc.dram_tensor("out_0_dram", (N_NODES, F), _mybir.dt.float32, kind="ExternalOutput").ap()
    gnn_program(nc, *args, out)
    r = _run(nc, [arrays], core_ids=[0])
    return r.results[0]["out_0_dram"]
```

```python
import concourse.bass as bass
from concourse import mybir
from contextlib import ExitStack

P = 128
F = 128
FE = 64
N_NODES = 50000
N_EDGES = 25000
EP = 125
T = N_EDGES // EP
SLOTS = P * T
J = 4
STEPS = T // J
DJ = 8
DENSE_FULL = N_NODES // (P * DJ)
TAIL_P = (N_NODES - DENSE_FULL * P * DJ) // DJ
DENSE_STEPS = DENSE_FULL + 1
MAP_P = 125
HEADS, HID = 4, 32
EPS = 1e-5
FAR = 1 << 20
PAD_NODE = 65535
LOW = 1e30
DOUBLINGS = [1, 2, 4, 8, 16, 32, 64, 128]

assert EP * T == N_EDGES and T % J == 0 and DENSE_FULL * P * DJ + TAIL_P * DJ == N_NODES


class Step:

    def __init__(self, k, b):
        self.k, self.b = k, b

    def first_use(self):
        return isinstance(self.k, int) and self.k == 0

    def index(self):
        return 2 * self.k + self.b


class Signal:

    def __init__(self, sem, base, per):
        self.sem, self.base, self.per = sem, base, per

    def at(self, steps):
        return self.base + self.per * steps


class Ring:

    def __init__(self, sems, base, n, steps):
        self.sems, self.base, self.n = sems, base, n
        self.end = [base[0] + 16 * n * ((steps + 1) // 2), base[1] + 16 * n * (steps // 2)]


def wait_done(eng, signal, g):
    eng.wait_ge(signal.sem, signal.per * g.index() + (signal.base + signal.per))


def wait_part(eng, signal, g, part):
    eng.wait_ge(signal.sem, signal.per * g.index() + (signal.base + part))


def wait_free(eng, signal, g):
    if not g.first_use():
        eng.wait_ge(signal.sem, signal.per * g.index() + (signal.base - signal.per))
    elif signal.base:
        eng.wait_ge(signal.sem, signal.base)


def wait_previous(eng, signal, g):
    if not (isinstance(g.k, int) and g.index() == 0 and signal.base == 0):
        eng.wait_ge(signal.sem, signal.per * g.index() + signal.base)


def wait_landed(eng, ring, g):
    eng.wait_ge(ring.sems[g.b], 16 * ring.n * g.k + (ring.base[g.b] + 16 * ring.n))


def wait_drained(eng, ring, g):
    if not g.first_use() or ring.base[g.b]:
        eng.wait_ge(ring.sems[g.b], 16 * ring.n * g.k + ring.base[g.b])


def wait_all(eng, ring):
    for b in range(2):
        eng.wait_ge(ring.sems[b], ring.end[b])


def settle(eng):
    eng.nop(nofuse=True)


def pipeline(eng, looped, stages):
    longest = max(lag for lag, _, _ in stages)

    def at(s):
        for lag, stage, count in stages:
            if 0 <= s - lag < count:
                stage(Step((s - lag) // 2, (s - lag) % 2))

    first = (longest + 3) // 2 * 2
    loops = (looped - first) // 2
    for s in range(first):
        at(s)
    with eng.Fori(0, loops) as i:
        for h in range(2):
            for lag, stage, _ in stages:
                stage(Step(i + (first + h - lag) // 2, (h - lag) % 2))
    for s in range(first + 2 * loops, max(lag + count for lag, _, count in stages)):
        at(s)


def edges(*stages):
    return [(lag, stage, STEPS) for lag, stage in stages]


def nodes(lag, stage):
    return (lag, stage, DENSE_STEPS)


def gnn_program(nc, x, src, dst, edge_attr, w0, b0, w_gat, att, w1l, b1, w1r, w2l, b2, w2r,
                qw, kw, gamma, beta, out_w, out_b, out):
    fp32 = mybir.dt.float32
    bf16 = mybir.dt.bfloat16
    i32 = mybir.dt.int32
    ALU = mybir.AluOpType
    ACT = mybir.ActivationFunctionType
    AX = mybir.AxisListType.X

    ctx = ExitStack()
    with ctx:
        def sb(name, shape, dt=fp32):
            return ctx.enter_context(nc.sbuf_tensor(name, shape, dt))

        def sem(name):
            return ctx.enter_context(nc.semaphore(name))

        def sem2(name):
            return [sem(f"{name}{b}") for b in range(2)]

        def table(name, rows):
            return nc.dram_tensor(name, (rows, F), fp32, kind="Internal").ap()

        x1_table, x2_table, h1_table, x3_table = (table(f"{n}_table", SLOTS + N_NODES) for n in ("x1", "x2", "h1", "x3"))
        y_nodes = table("y_nodes", N_NODES)
        q_rows = table("q_rows", SLOTS)
        ACC_W = F + HEADS
        gat_sums = nc.dram_tensor("gat_sums", (DENSE_STEPS * P * DJ + J * P, ACC_W), fp32, kind="Internal").ap()
        acc_dump = nc.dram_tensor("acc_dump", (SLOTS, ACC_W), fp32, kind="Internal").ap()
        node_map = nc.dram_tensor("node_map", (N_NODES, 1), i32, kind="Internal").ap()

        def slot_rows(tab, g):
            v = tab[0:SLOTS, :].rearrange("(p t) f -> p (t f)", p=P)
            return v[:, bass.ds(g.index() * (J * F), J * F)]

        def acc_rows(g):
            v = acc_dump.rearrange("(p t) f -> p (t f)", p=P)
            return v[:, bass.ds(g.index() * (J * ACC_W), J * ACC_W)]

        def is_tail(g):
            return isinstance(g.k, int) and g.index() == DENSE_FULL

        def dense_p(g):
            return TAIL_P if is_tail(g) else P

        def node_rows(tab, base, g):
            pn = dense_p(g)
            rows = tab[bass.ds(g.index() * (P * DJ) + base, pn * DJ), :]
            return rows.rearrange("(p j) f -> p j f", p=pn)

        def sums_rows(g):
            rows = gat_sums[bass.ds(g.index() * (P * DJ), P * DJ), :]
            return rows.rearrange("(p j) f -> p (j f)", p=P)

        ident = sb("ident", [P, P])
        ones = sb("ones", [P, P])
        upper = sb("upper", [P, P])
        lower = sb("lower", [P, P])
        w0_sb = sb("w0_sb", [P, 2 * F + FE])
        natural = {n: sb(f"{n}_sb", [P, F]) for n in ("w_gat", "w1l", "w1r", "w2l", "w2r")}
        w0s_t, w0d_t, wgat_t, w1l_t, w1r_t, w2l_t, w2r_t = (sb(n, [P, F]) for n in ("w0s_t", "w0d_t", "wgat_t", "w1l_t", "w1r_t", "w2l_t", "w2r_t"))
        w0e_t = sb("w0e_t", [FE + 1, F])
        qw_sb, kw_sb = sb("qw_sb", [P, HEADS, HID]), sb("kw_sb", [P, HEADS, HID])
        outw_sb = sb("outw_sb", [P, F])
        outb_bc = sb("outb_bc", [P, F])
        b2_rows = sb("b2_rows", [3, F])
        b2_hi, b2_mid, b2_lo = (sb(n, [3, F], bf16) for n in ("b2_hi", "b2_mid", "b2_lo"))
        b2_parts = sb("b2_parts", [3, J, F], bf16)
        ones_bf = sb("ones_bf", [3, P], bf16)
        cols = sb("cols", [P, 8])
        b1_col, gamma_col, beta_col, adst_col, asrc_col, sbeta_col = (cols[:, i:i + 1] for i in range(6))
        col_bc = sb("col_bc", [P, 3, P])
        vdst_bc, vsrc_bc, local3_bc = sb("vdst_bc", [P, F]), sb("vsrc_bc", [P, F]), sb("local3_bc", [P, F])

        dst_i = sb("dst_i", [P, T + 2], i32)
        d = sb("d", [P, T + 2])
        src_i = sb("src_i", [P, T], i32)
        dst_safe_i = sb("dst_safe_i", [P, T], i32)
        table_index = sb("table_index", [P, T], i32)
        canon_slot_i = sb("canon_slot_i", [P, T], i32)
        map_index = sb("map_index", [P, T], i32)
        out_index = sb("out_index", [P, T], i32)
        slot_i = sb("slot_i", [P, T], i32)
        slot = sb("slot", [P, T])
        keep, canon, in_first, in_open, first_done = (sb(n, [P, T]) for n in ("keep", "canon", "in_first", "in_open", "first_done"))
        canon_inner = sb("canon_inner", [P, T])
        undone = sb("undone", [P, len(DOUBLINGS), T])
        spread = sb("spread", [P, T])
        tmp_t = sb("tmp_t", [P, T])
        tmp_t2 = sb("tmp_t2", [P, T])
        source_key = sb("source_key", [P, T])
        dummy_row = sb("dummy_row", [P, 2])
        dummy_rows = sb("dummy_rows", [P, J])
        alpha = sb("alpha", [P, T, HEADS])
        seg_max = sb("seg_max", [P, T, HEADS])
        tmp_a = sb("tmp_a", [P, T, HEADS])
        neg_half = sb("neg_half", [P, J])
        one_p = sb("one_p", [P, 16])
        has_first, fix_slot, open_last, carry_p, score_fix = (one_p[:, i:i + 1] for i in range(5))
        fix_idx = sb("fix_idx", [P, 4], i32)
        fix_read, fix_write, fix_out, fix_node = (fix_idx[:, i:i + 1] for i in range(4))
        fix_f = sb("fix_f", [P, 4])
        diag = sb("diag", [P, 2 + 2 * HEADS, P])
        sum_carry = sb("sum_carry", [P, P])
        back_carry = sb("back_carry", [P, P])
        max_pen = sb("max_pen", [P, 4, P])
        max_row = sb("max_row", [P, 2, HEADS, P])
        max_extra = sb("max_extra", [P, 4, HEADS])

        def ring(name, width=F, dt=fp32):
            return sb(name, [P, 2, J, width], dt)

        def dense_ring(name, width=F):
            return sb(name, [P, 2, DJ, width])

        zeros = sb("zeros", [P, DJ * ACC_W])
        node_in, node_sums, node_out, node_h1, node_y = (dense_ring(f"node_{n}", w) for n, w in (
            ("in", F), ("sums", ACC_W), ("out", F), ("h1", F), ("y", F)))
        node_x2t, node_h1t = sb("node_x2t", [P, 2, DJ * F]), sb("node_h1t", [P, 2, DJ * F])
        node_recip = sb("node_recip", [P, 2, 2, DJ])
        src_rows = ring("src_rows", ACC_W)
        own_rows, own2_rows, ny = ring("own_rows"), ring("own2_rows"), ring("att_pre")
        ea_rows = ring("ea_rows", FE)
        msg = ring("msg", ACC_W)
        acc = ring("acc", ACC_W)
        gate = ring("gate")
        bc = ring("bc")
        pre = ring("pre")
        new_rows = ring("new_rows")
        same = [t[:, :, :, :].rearrange("p b j f -> p (b j f)").rearrange("p (j i) -> p j i", j=J) for t in (node_h1, node_y)]
        junk2 = node_x2t[:, :, :].rearrange("p b c -> p (b c)").rearrange("p (j i) -> p j i", j=J)
        same_bf = sb("same_bf", [P, 2, J, J * P], bf16)
        w_parts = sb("w_parts", [P, 2, 3, J], bf16)
        w_left = sb("w_left", [P, 2, 2, J])
        earlier = sb("earlier", [P, (J - 1) * P + P])
        sums = ring("sums", ACC_W)
        key4 = sb("key4", [P, 2, 5, J])
        add_idx = sb("add_idx", [P, 2, J], i32)
        junk = sb("junk", [P, 2, J, F])
        t_a, t_b, t_c = (sb(n, [P, 2, J * F]) for n in ("t_a", "t_b", "t_c"))
        t_e = sb("t_e", [FE + 1, 2, J * P])
        NORM = {k: (sb(f"{k}_stats", [P, 2, n, 6]), sb(f"{k}_moments", [P, 2, n, 2]), sb(f"{k}_root", [P, 2, n]),
                    sb(f"{k}_shift", [P, 2, n])) for k, n in (("e", J), ("a", J), ("n", DJ))}
        edge4 = sb("edge4", [P, 2, 6, J])
        recip = sb("recip", [P, 2, J, HEADS])
        out_stage = sb("out_stage", [P, 2, J], i32)
        idx_stage = sb("idx_stage", [P, 2, 2, J], i32)
        val_stage = sb("val_stage", [P, 2, J], i32)
        map_init = sb("map_init", [MAP_P, N_NODES // MAP_P], i32)
        fix_acc = sb("fix_acc", [P, ACC_W])

        ps = [[ctx.enter_context(nc.psum_tensor(f"ps{i}{b}", [P, J * F], fp32)) for b in range(2)] for i in range(4)]

        weights_in, cols_in, dst_in, src_in = sem("weights_in"), sem("cols_in"), sem("dst_in"), sem("src_in")
        consts_made, dst_set, slots_made = sem("consts_made"), sem("dst_set"), sem("slots_made")
        pe_prep, dve_prep, act_prep = sem("pe_prep"), sem("dve_prep"), sem("act_prep")
        map_start, map_index_made, index_made = sem("map_start"), sem("map_index_made"), sem("index_made")
        spread_at, carried, max_at, fix_in, fix_out_sem = (sem(n) for n in ("spread_at", "carried", "max_at", "fix_in", "fix_out_sem"))
        fix_ready, dummies_zero = sem("fix_ready"), sem("dummies_zero")

        PER = {"accd": J}

        def norm(k, inverted=True):
            return [f"{k}_{n}" for n in ("bn", "ag", "ve", "rt", "nm")] + [f"{k}_rc"] * inverted

        LAYERS = {
            "map": dict(front=["idxd", "idx2", "mapd"], rings=dict(marked=J, mapped=J)),
            "nodes1": dict(front=norm("n") + ["n_row"], rings=dict(n_in=1, n_out=1, n_zero=1), steps=DENSE_STEPS),
            "msg": dict(front=["idxd", "tr_a", "cp_a", "tr_b", "cp_b", "tr_e", "cp_e", "mm", "sig", "msg0", "msgd"],
                        back=["accd", "pre", "newd"] + norm("e", False),
                        rings=dict(gathered=2 * J, eain=2, dumped=1, stored=1)),
            "gat": dict(front=["idxd", "score", "e0", "e1", "e2", "expd", "msgd", "keyd", "bcd", "tr_a", "samed", "rep0", "rep1",
                               "rep2", "rep3", "mm", "cp_a", "mm2", "cp_b", "w_hi", "w_r1", "w_mid", "w_r2", "w_lo", "same_bf"],
                        rings=dict(gathered=2 * J), parts=dict(added=16 * J)),
            "x2": dict(front=["idxd", "rcs", "rc0", "rc1", "pre", "newd"] + norm("e"), rings=dict(gathered=J, own=1, stored=1)),
            "nodes2": dict(front=["n_rcs", "n_rc0", "n_rc1", "n_pre", "x2tp", "x2tc", "h1p", "h1tc", "h1tp", "h1c", "yp", "y", "n_row"] + norm("n"),
                           rings=dict(n_in=2, n_out=1, n_h1=1, n_y=1), steps=DENSE_STEPS),
            "sage1": dict(front=["idxd"], back=["accd", "rcp", "msgd", "tr_a", "cp_a", "tr_b", "cp_b", "mm", "cp_c", "mm2", "newd"],
                          rings=dict(gathered=J, own=1, dumped=1, stored=1)),
            "nodes3": dict(front=norm("n") + ["n_row"], rings=dict(n_in=1, n_out=1), steps=DENSE_STEPS),
            "sage2": dict(front=["idxd"], back=["accd", "rcp", "msgd", "tr_a", "cp_a", "tr_b", "cp_b", "mm", "pre", "newd"] + norm("e"),
                          rings=dict(gathered=J, own=1, own2=1, dumped=1, stored=1)),
            "att1": dict(front=["idxd", "tr_a", "cp_a", "tr_b", "cp_b", "mm", "mm2", "newd", "cp_c", "pre", "score"],
                         rings=dict(gathered=2 * J, stored=1)),
            "nodes4": dict(front=norm("n") + ["n_pre", "n_row"], rings=dict(n_in=1, n_out=1), steps=DENSE_STEPS),
            "att2": dict(front=["idxd", "msgd"],
                         back=["accd", "rcp", "rcp2", "pre", "msg0", "tr_a", "cp_a", "mm", "pre2", "pre3", "newd"]
                         + norm("e", False) + norm("a", False),
                         rings=dict(qin=1, own=1, dumped=1, scattered=J)),
        }
        sems, counts, flow = {}, {}, {}
        for layer, use in LAYERS.items():
            flow[layer] = {}
            steps = use.get("steps", STEPS)
            for kind, total in (("front", steps), ("back", steps + 1)):
                for n in use.get(kind, []):
                    if n not in sems:
                        sems[n], counts[n] = sem(n), 0
                    per = PER.get(n, 1)
                    flow[layer][n] = Signal(sems[n], counts[n], per)
                    counts[n] += per * total
            for n, m in use["rings"].items():
                if n not in sems:
                    sems[n], counts[n] = sem2(n), [0, 0]
                flow[layer][n] = Ring(sems[n], counts[n], m, steps)
                counts[n] = flow[layer][n].end
            for n, per in use.get("parts", {}).items():
                flow[layer][n] = Signal(sem(n), 0, per)
        LAYER_NO = {n: i for i, n in enumerate(("msg", "sage1", "sage2", "att2"))}
        FIX = Step(STEPS // 2, 0)

        block = ctx.enter_context(nc.Block())

        def fours(ap, g):
            return ap[:, bass.ds(g.index() * J, J)]

        def nothing(g):
            pass

        @block.sync
        def _(sp):
            sp.wait_ge(dst_set, 1)
            by_p = dst.rearrange("(p t) -> p t", t=T)
            sp.dma_start(dst_i[0:EP, 1:T + 1], by_p).then_inc(dst_in, 16)
            with nc.allow_non_contiguous_dma(reason="one value a partition"):
                sp.dma_start(dst_i[1:EP, 0:1], by_p[0:EP - 1, T - 1:T]).then_inc(dst_in, 16)
                sp.dma_start(dst_i[0:EP - 1, T + 1:T + 2], by_p[1:EP, 0:1]).then_inc(dst_in, 16)
            sp.dma_start(src_i[0:EP, :], src.rearrange("(p t) -> p t", t=T)).then_inc(src_in, 16)
            sp.dma_start(w0_sb[:, :], w0).then_inc(weights_in, 16)
            for n, a in (("w_gat", w_gat), ("w1l", w1l), ("w1r", w1r), ("w2l", w2l), ("w2r", w2r)):
                sp.dma_start(natural[n][:, :], a).then_inc(weights_in, 16)
            sp.dma_start(outw_sb[:, :], out_w).then_inc(weights_in, 16)
            sp.dma_start(w0e_t[FE:FE + 1, :], b0.rearrange("(a n) -> a n", a=1)).then_inc(weights_in, 16)
            sp.dma_start(qw_sb[:, :, :], qw.rearrange("h f d -> f h d")).then_inc(weights_in, 16)
            sp.dma_start(kw_sb[:, :, :], kw.rearrange("h f d -> f h d")).then_inc(weights_in, 16)
            sp.dma_start(b2_rows[:, :], b2.partition_broadcast(3)).then_inc(weights_in, 16)
            sp.dma_start(outb_bc[:, :], out_b.partition_broadcast(P)).then_inc(weights_in, 16)
            with nc.allow_non_contiguous_dma(reason="one value a partition"):
                for i, a in enumerate((b1, gamma, beta)):
                    sp.dma_start(cols[:, i:i + 1], a.rearrange("(n a) -> n a", a=1)).then_inc(cols_in, 16)
                sp.dma_start(cols[:, 3:4], att[0:F, :]).then_inc(cols_in, 16)
                sp.dma_start(cols[:, 4:5], att[F:2 * F, :]).then_inc(cols_in, 16)

            def dump_and_store(L, tab):
                def dump(g):
                    wait_done(sp, L["accd"], g)
                    sp.dma_start(acc_rows(g), acc[:, g.b, :, :]).then_inc(L["dumped"].sems[g.b], 16)

                def store(g):
                    wait_done(sp, L["newd"], g)
                    sp.dma_start(slot_rows(tab, g), new_rows[:, g.b, :, :]).then_inc(L["stored"].sems[g.b], 16)

                return dump, store

            def load_nodes(D, tab, base, used):
                def load(g):
                    wait_free(sp, D[used], g)
                    sp.dma_start(node_in[0:dense_p(g), g.b, :, :], node_rows(tab, base, g)).then_inc(D["n_in"].sems[g.b], 16)
                return load

            def store_nodes(D, tab, base):
                def store(g):
                    wait_done(sp, D["n_row"], g)
                    sp.dma_start(node_rows(tab, base, g), node_out[0:dense_p(g), g.b, :, :]).then_inc(D["n_out"].sems[g.b], 16)
                return store

            D = flow["nodes1"]

            def zero_sums(g):
                wait_drained(sp, D["n_zero"], g)
                sp.dma_start(sums_rows(g), zeros[:, :]).then_inc(D["n_zero"].sems[g.b], 16)

            sp.wait_ge(consts_made, 3)
            sp.dma_start(gat_sums[DENSE_STEPS * P * DJ:, :].rearrange("(p j) f -> p (j f)", p=P), zeros[:, 0:J * ACC_W])\
                .then_inc(dummies_zero, 16)
            pipeline(sp, DENSE_FULL, [nodes(2, store_nodes(D, x1_table, SLOTS)), nodes(0, load_nodes(D, x, 0, "n_row")), nodes(0, zero_sums)])

            L = flow["msg"]
            ea_v = edge_attr.rearrange("(p t) f -> p (t f)", p=EP)

            def load_ea(g):
                wait_free(sp, L["tr_e"], g)
                for lo, hi in ((0, 112), (112, EP)):
                    sp.dma_start(ea_rows[lo:hi, g.b, :, :],
                                 ea_v[lo:hi, bass.ds(g.index() * (J * FE), J * FE)]).then_inc(L["eain"].sems[g.b], 16)

            dump, store = dump_and_store(L, x1_table)
            pipeline(sp, STEPS, edges((0, load_ea), (1, dump), (4, store)))

            def load_own(L, signal, tab, to, ring):
                def load(g):
                    wait_free(sp, signal, g)
                    sp.dma_start(to[:, g.b, :, :], slot_rows(tab, g)).then_inc(ring.sems[g.b], 16)
                return load

            L, D = flow["x2"], flow["nodes2"]
            wait_all(sp, flow["nodes1"]["n_out"])
            wait_all(sp, flow["msg"]["stored"])
            sp.wait_ge(fix_out_sem, 16 * 1)
            sp.wait_ge(flow["gat"]["added"].sem, flow["gat"]["added"].at(STEPS))
            load_x1 = load_nodes(D, x1_table, SLOTS, "n_row")

            def load_x1_sums(g):
                wait_free(sp, D["n_pre"], g)
                sp.dma_start(node_sums[0:dense_p(g), g.b, :, :], node_rows(gat_sums, 0, g)).then_inc(D["n_in"].sems[g.b], 16)
                load_x1(g)

            def store_h1(g):
                wait_done(sp, D["h1c"], g)
                sp.dma_start(node_rows(h1_table, SLOTS, g), node_h1[0:dense_p(g), g.b, :, :]).then_inc(D["n_h1"].sems[g.b], 16)

            def store_y(g):
                wait_done(sp, D["y"], g)
                sp.dma_start(node_rows(y_nodes, 0, g), node_y[0:dense_p(g), g.b, :, :]).then_inc(D["n_y"].sems[g.b], 16)

            _, store = dump_and_store(L, x2_table)
            pipeline(sp, DENSE_FULL, [nodes(5, store_h1), nodes(5, store_y), nodes(3, store_nodes(D, x2_table, SLOTS))]
                     + edges((3, store), (0, load_own(L, L["pre"], x1_table, own_rows, L["own"]))) + [nodes(0, load_x1_sums)])

            L, D = flow["sage1"], flow["nodes3"]
            wait_all(sp, flow["x2"]["stored"])
            wait_all(sp, flow["nodes2"]["n_out"])
            wait_all(sp, flow["nodes2"]["n_y"])
            dump, store = dump_and_store(L, h1_table)
            pipeline(sp, DENSE_FULL, edges((0, load_own(L, L["tr_b"], x2_table, own_rows, L["own"])))
                     + [nodes(0, load_nodes(D, y_nodes, 0, "n_row"))] + edges((1, dump))
                     + [nodes(2, store_nodes(D, x3_table, SLOTS))] + edges((3, store)))
            L = flow["sage2"]
            wait_all(sp, flow["sage1"]["stored"])
            sp.wait_ge(fix_out_sem, 16 * 2)
            dump, store = dump_and_store(L, x3_table)
            h1_own = load_own(L, L["tr_b"], h1_table, own_rows, L["own"])
            x2_own = load_own(L, L["pre"], x2_table, own2_rows, L["own2"])

            def both(g):
                h1_own(g)
                x2_own(g)

            pipeline(sp, STEPS, edges((0, both), (1, dump), (4, store)))
            L, D = flow["att1"], flow["nodes4"]
            wait_all(sp, flow["nodes3"]["n_out"])
            _, store = dump_and_store(L, q_rows)
            pipeline(sp, DENSE_FULL, edges((2, store)) + [nodes(2, store_nodes(D, out, 0)), nodes(0, load_nodes(D, x3_table, SLOTS, "n_row"))])
            L = flow["att2"]
            wait_all(sp, flow["att1"]["stored"])
            sp.wait_ge(fix_out_sem, 16 * 3)

            def load_q(g):
                wait_free(sp, L["msgd"], g)
                sp.dma_start(src_rows[:, g.b, :, 0:F], slot_rows(q_rows, g).rearrange("p (j f) -> p j f", f=F))\
                    .then_inc(L["qin"].sems[g.b], 16)

            dump, _ = dump_and_store(L, None)
            pipeline(sp, STEPS, edges((0, load_q), (1, dump), (3, load_own(L, L["pre3"], x3_table, own_rows, L["own"]))))
            sp.wait_ge(fix_out_sem, 16 * 4)
            wait_all(sp, L["scattered"])

        @block.gpsimd
        def _(pool):
            g_ = nc.gpsimd
            g_.memset(dst_i[:, :], PAD_NODE)
            g_.memset(src_i[:, :], 0)
            g_.memset(ident[:, :], 0.0)
            g_.memset(ones[:, :], 1.0)
            g_.memset(upper[:, :], 1.0)
            g_.memset(neg_half[:, :], -0.5)
            g_.memset(lower[:, :], 1.0).then_inc(consts_made, 1)
            pool.wait_ge(consts_made, 1)
            g_.memset(dst_i[:, 0:1], -1)
            g_.memset(dst_i[:, T + 1:T + 2], -1).then_inc(dst_set, 1)
            g_.affine_select(out=ident[:, :], in_=ident[:, :], compare_op=ALU.not_equal, fill=1.0, base=0,
                             pattern=[[-1, P]], channel_multiplier=1)
            g_.affine_select(out=upper[:, :], in_=upper[:, :], compare_op=ALU.is_gt, fill=0.0, base=0,
                             pattern=[[1, P]], channel_multiplier=-1)
            g_.affine_select(out=lower[:, :], in_=lower[:, :], compare_op=ALU.is_gt, fill=0.0, base=0,
                             pattern=[[-1, P]], channel_multiplier=1)
            g_.iota(slot_i[:, :], pattern=[[1, T]], base=0, channel_multiplier=T)
            g_.iota(map_init[:, :], pattern=[[1, N_NODES // MAP_P]], base=SLOTS, channel_multiplier=N_NODES // MAP_P)
            g_.memset(src_rows[:, :, :, :], 0.0)
            g_.memset(msg[:, :, :, :], 0.0)
            g_.memset(acc[:, :, :, :], 0.0)
            g_.memset(zeros[:, :], 0.0)
            g_.memset(sums[:, :, :, :], 0.0)
            g_.iota(dummy_rows[:, :], pattern=[[P, J]], base=DENSE_STEPS * P * DJ, channel_multiplier=1,
                    allow_small_or_imprecise_dtypes=True)
            g_.iota(dummy_row[:, 0:1], pattern=[[0, 1]], base=N_NODES, channel_multiplier=1,
                    allow_small_or_imprecise_dtypes=True)
            g_.memset(ea_rows[:, :, :, :], 0.0).then_inc(consts_made, 1)
            pool.wait_ge(consts_made, 2)
            g_.memset(src_rows[:, :, :, F:F + 1], 1.0).then_inc(consts_made, 1)

            def mark_and_look_up():
                pool.dma_start(node_map.rearrange("(p t) a -> p (t a)", p=MAP_P), map_init[:, :]).then_inc(map_start, 16)
                pool.wait_ge(map_start, 16)
                L = flow["map"]
                pool.wait_ge(map_index_made, 1)

                def mark(g):
                    wait_drained(pool, L["marked"], g)
                    g_.tensor_copy(idx_stage[:, g.b, 0, :], fours(map_index, g))
                    g_.tensor_copy(val_stage[:, g.b, :], fours(slot_i, g)).then_inc(L["idxd"].sem, 1)
                    wait_done(pool, L["idxd"], g)
                    settle(pool)
                    for j in range(J):
                        g_.indirect_dma_start(
                            out=node_map[:, :], out_offset=bass.IndirectOffsetOnAxis(ap=idx_stage[:, g.b, 0, j:j + 1], axis=0),
                            in_=val_stage[:, g.b, j:j + 1], in_offset=None,
                            bounds_check=N_NODES - 1, oob_is_err=False).then_inc(L["marked"].sems[g.b], 16)

                pipeline(pool, STEPS, edges((0, mark)))
                wait_all(pool, L["marked"])

                def look_up(g):
                    wait_free(pool, L["mapd"], g)
                    g_.tensor_copy(idx_stage[:, g.b, 1, :], fours(src_i, g)).then_inc(L["idx2"].sem, 1)
                    wait_done(pool, L["idx2"], g)
                    settle(pool)
                    for j in range(J):
                        g_.indirect_dma_start(
                            out=val_stage[:, g.b, j:j + 1], out_offset=None, in_=node_map[:, :],
                            in_offset=bass.IndirectOffsetOnAxis(ap=idx_stage[:, g.b, 1, j:j + 1], axis=0))\
                            .then_inc(L["mapped"].sems[g.b], 16)

                def keep_looked_up(g):
                    wait_landed(pool, L["mapped"], g)
                    g_.tensor_copy(fours(table_index, g), val_stage[:, g.b, :]).then_inc(L["mapd"].sem, 1)

                pipeline(pool, STEPS, edges((0, look_up), (1, keep_looked_up)))
                pool.wait_ge(L["mapd"].sem, L["mapd"].at(STEPS))

            def inverse_root(L, k):
                def root(g, jn=J):
                    wait_done(pool, L[f"{k}_ve"], g)
                    at = NORM[k][2][:, g.b, 0:jn]
                    g_.tensor_tensor(at, at, neg_half[:, 0:jn], ALU.pow).then_inc(L[f"{k}_rt"].sem, 1)
                return root

            def stage_indices(L, g, arrays):
                for i, a in enumerate(arrays):
                    last = g_.tensor_copy(idx_stage[:, g.b, i, :], fours(a, g))
                last.then_inc(L["idxd"].sem, 1)
                wait_done(pool, L["idxd"], g)
                settle(pool)

            def gather(L, g, i, tab, to, width=F, only=None):
                for j in range(J) if only is None else [only]:
                    g_.indirect_dma_start(
                        out=to[:, g.b, j, 0:width], out_offset=None, in_=tab,
                        in_offset=bass.IndirectOffsetOnAxis(ap=idx_stage[:, g.b, i, j:j + 1], axis=0))\
                        .then_inc(L["gathered"].sems[g.b], 16)

            def fix_gather(L, own, idx, own_used, more=()):
                n = LAYER_NO["att2" if L is flow["att2"] else next(k for k in flow if flow[k] is L)]
                wait_all(pool, L["dumped"])
                pool.wait_ge(own_used.sem, own_used.at(STEPS))
                g_.indirect_dma_start(out=fix_acc[:, :], out_offset=None, in_=acc_dump[:, :],
                                      in_offset=bass.IndirectOffsetOnAxis(ap=fix_read, axis=0)).then_inc(fix_in, 16)
                g_.indirect_dma_start(out=own_rows[:, 0, 0, :], out_offset=None, in_=own,
                                      in_offset=bass.IndirectOffsetOnAxis(ap=idx, axis=0)).then_inc(fix_in, 16)
                g_.indirect_dma_start(out=own2_rows[:, 0, 0, :], out_offset=None, in_=more[0] if more else own,
                                      in_offset=bass.IndirectOffsetOnAxis(ap=idx, axis=0)).then_inc(fix_in, 16)
                pool.wait_ge(fix_in, 48 * (n + 1))
                return n

            def fix_scatter(L, tab, idx, rows, n, out_ring="stored"):
                wait_all(pool, L[out_ring])
                pool.wait_ge(L["newd"].sem, L["newd"].at(STEPS + 1))
                g_.indirect_dma_start(out=tab, out_offset=bass.IndirectOffsetOnAxis(ap=idx, axis=0),
                                      in_=new_rows[:, 0, 0, :], in_offset=None,
                                      bounds_check=rows - 1, oob_is_err=False).then_inc(fix_out_sem, 16)
                pool.wait_ge(fix_out_sem, 16 * (n + 1))

            mark_and_look_up()
            pool.wait_ge(index_made, 1)
            L = flow["msg"]

            def gather_ends(g):
                wait_free(pool, L["tr_b"], g)
                stage_indices(L, g, (src_i, dst_safe_i))
                gather(L, g, 0, x[:, :], src_rows)
                wait_free(pool, L["pre"], g)
                settle(pool)
                gather(L, g, 1, x[:, :], own_rows)

            def scatter_rows(L, tab, stage):
                def scatter(g):
                    wait_drained(pool, L["scattered"], g)
                    g_.tensor_copy(out_stage[:, g.b, :], fours(out_index, g)).then_inc(L[stage].sem, 1)
                    wait_done(pool, L[stage], g)
                    wait_done(pool, L["newd"], g)
                    settle(pool)
                    for j in range(J):
                        g_.indirect_dma_start(
                            out=tab, out_offset=bass.IndirectOffsetOnAxis(ap=out_stage[:, g.b, j:j + 1], axis=0),
                            in_=new_rows[:, g.b, j, :], in_offset=None,
                            bounds_check=N_NODES - 1, oob_is_err=False).then_inc(L["scattered"].sems[g.b], 16)
                return scatter

            pipeline(pool, STEPS, edges((0, gather_ends), (2, inverse_root(L, "e"))))
            n = fix_gather(L, x[:, :], fix_node, L["pre"])
            inverse_root(L, "e")(FIX, 1)
            fix_scatter(L, x1_table[:, :], fix_write, SLOTS, n)

            G = flow["gat"]
            wait_all(pool, flow["nodes1"]["n_out"])
            wait_all(pool, flow["nodes1"]["n_zero"])
            pool.wait_ge(dummies_zero, 16)

            def stage_x1(g):
                wait_free(pool, G["score"], g)
                wait_free(pool, G["msgd"], g)
                stage_indices(G, g, (table_index, canon_slot_i))

            def gather_x1(j):
                return lambda g: [gather(G, g, i, x1_table[:, :], to, only=j) for i, to in enumerate((own_rows, src_rows))]

            def add_sums(j):
                def add(g):
                    if j == 0:
                        wait_done(pool, G["cp_b"], g)
                        wait_done(pool, G["rep2"], g)
                        if not (isinstance(g.k, int) and g.index() == 0):
                            pool.wait_ge(G["added"].sem, G["added"].per * g.index())
                        settle(pool)
                    g_.indirect_dma_start(
                        out=gat_sums[:, :], out_offset=bass.IndirectOffsetOnAxis(ap=add_idx[:, g.b, j:j + 1], axis=0),
                        in_=sums[:, g.b, j, :], in_offset=None, compute_op=ALU.add).then_inc(G["added"].sem, 16)
                return add

            pipeline(pool, STEPS, edges((0, stage_x1), *[st for j in range(J) for st in ((3, add_sums(j)), (0, gather_x1(j)))]))

            L = flow["x2"]
            pool.wait_ge(G["added"].sem, G["added"].at(STEPS))

            def gather_sums(g):
                wait_free(pool, L["pre"], g)
                stage_indices(L, g, (dst_safe_i,))
                gather(L, g, 0, gat_sums[:, :], sums, ACC_W)

            pipeline(pool, STEPS, edges((0, gather_sums)))

            def gather_sources(L, tab):
                def gather_tab(g):
                    wait_free(pool, L["accd"], g)
                    stage_indices(L, g, (table_index,))
                    gather(L, g, 0, tab, src_rows)
                return gather_tab

            L = flow["sage1"]
            wait_all(pool, flow["x2"]["stored"])
            wait_all(pool, flow["nodes2"]["n_out"])
            pipeline(pool, STEPS, edges((0, gather_sources(L, x2_table[:, :]))))
            n = fix_gather(L, x2_table[:, :], fix_read, L["tr_b"])
            fix_scatter(L, h1_table[:, :], fix_write, SLOTS, n)
            L = flow["sage2"]
            wait_all(pool, flow["nodes2"]["n_h1"])
            pipeline(pool, STEPS, edges((0, gather_sources(L, h1_table[:, :]))))
            n = fix_gather(L, h1_table[:, :], fix_read, L["pre"], more=(x2_table[:, :],))
            fix_scatter(L, x3_table[:, :], fix_write, SLOTS, n)

            L = flow["att1"]
            wait_all(pool, flow["nodes3"]["n_out"])

            def gather_x3(g):
                wait_free(pool, L["tr_b"], g)
                stage_indices(L, g, (table_index, canon_slot_i))
                gather(L, g, 0, x3_table[:, :], src_rows)
                gather(L, g, 1, x3_table[:, :], own_rows)

            pipeline(pool, STEPS, edges((0, gather_x3)))

            L = flow["att2"]
            wait_all(pool, flow["nodes4"]["n_out"])

            def scatter_rows(g):
                wait_drained(pool, L["scattered"], g)
                g_.tensor_copy(out_stage[:, g.b, :], fours(out_index, g)).then_inc(L["idxd"].sem, 1)
                wait_done(pool, L["idxd"], g)
                wait_done(pool, L["newd"], g)
                settle(pool)
                for j in range(J):
                    g_.indirect_dma_start(
                        out=out[:, :], out_offset=bass.IndirectOffsetOnAxis(ap=out_stage[:, g.b, j:j + 1], axis=0),
                        in_=new_rows[:, g.b, j, :], in_offset=None,
                        bounds_check=N_NODES - 1, oob_is_err=False).then_inc(L["scattered"].sems[g.b], 16)

            pipeline(pool, STEPS, edges((7, scatter_rows), (5, inverse_root(L, "a")), (1, inverse_root(L, "e"))))
            n = fix_gather(L, x3_table[:, :], fix_read, L["pre3"])
            inverse_root(L, "e")(FIX, 1)
            inverse_root(L, "a")(FIX, 1)
            fix_scatter(L, out[:, :], fix_out, N_NODES, n, "scattered")

        @block.tensor
        def _(pe):
            te = nc.tensor
            pe.wait_ge(consts_made, 3)
            pe.wait_ge(weights_in, 16 * 12)
            w0s, w0d, w0e = w0_sb[:, 0:F], w0_sb[:, F:2 * F], w0_sb[:, 2 * F:2 * F + FE]
            for i, w in enumerate((w0s, w0d, natural["w_gat"][:, :], natural["w1l"][:, :],
                                   natural["w1r"][:, :], natural["w2l"][:, :], natural["w2r"][:, :])):
                te.transpose(ps[i // 4][0][:, (i % 4) * F:(i % 4 + 1) * F], w, ident[:, :])
            te.transpose(ps[1][0][0:FE, 3 * F:4 * F], w0e, ident[:, :]).then_inc(pe_prep, 1)
            pe.wait_ge(fix_ready, 1)
            for i in range(2):
                last = te.matmul(ps[2][0][:, i * P:(i + 1) * P], ones[:, :], diag[:, i, :], start=True, stop=True)
            last.then_inc(pe_prep, 1)
            pe.wait_ge(spread_at, 1)
            te.matmul(ps[2][0][:, 256:257], back_carry[:, :], fix_f[:, 0:1], start=True, stop=True).then_inc(carried, 1)
            pe.wait_ge(fix_ready, 2)
            te.matmul(ps[3][0][:, 0:F], col_bc[:, 0, :], wgat_t[:, :], start=True, stop=True)
            te.matmul(ps[3][0][:, F:2 * F], col_bc[:, 1, :], wgat_t[:, :], start=True, stop=True)
            te.matmul(ps[3][0][:, 2 * F:3 * F], col_bc[:, 2, :], outw_sb[:, :], start=True, stop=True).then_inc(pe_prep, 1)
            pe.wait_ge(dve_prep, 1)

            def transpose_step(L, g, bank, rows, done, copied, jn=J):
                wait_free(pe, L[copied], g)
                for j in range(jn):
                    last = te.transpose(ps[bank][g.b][:, j * F:(j + 1) * F], rows[:, g.b, j, 0:F], ident[:, :])
                last.then_inc(L[done].sem, 1)

            def carry(L, width, used):
                pe.wait_ge(L["accd"].sem, L["accd"].at(STEPS))
                pe.wait_ge(used.sem, used.at(STEPS))
                te.matmul(ps[0][0][:, 0:width], sum_carry[:, :], acc[:, 1, J - 1, 0:width],
                          start=True, stop=True).then_inc(carried, 1)

            L = flow["msg"]

            def transpose_ends(g):
                wait_landed(pe, L["gathered"], g)
                transpose_step(L, g, 0, src_rows, "tr_a", "cp_a")
                transpose_step(L, g, 1, own_rows, "tr_b", "cp_b")
                wait_landed(pe, L["eain"], g)
                wait_free(pe, L["cp_e"], g)
                settle(pe)
                for j in range(J):
                    last = te.transpose(ps[2][g.b][0:FE, j * P:(j + 1) * P], ea_rows[:, g.b, j, :], ident[:, :])
                last.then_inc(L["tr_e"].sem, 1)

            def messages(g):
                wait_done(pe, L["cp_a"], g)
                wait_done(pe, L["cp_b"], g)
                wait_done(pe, L["cp_e"], g)
                wait_free(pe, L["msg0"], g)
                for j in range(J):
                    c = slice(j * F, (j + 1) * F)
                    te.matmul(ps[3][g.b][:, c], t_a[:, g.b, c], w0s_t[:, :], start=True, stop=False)
                    te.matmul(ps[3][g.b][:, c], t_b[:, g.b, c], w0d_t[:, :], start=False, stop=False)
                    last = te.matmul(ps[3][g.b][:, c], t_e[:, g.b, c], w0e_t[:, :], start=False, stop=True)
                last.then_inc(L["mm"].sem, 1)

            pipeline(pe, STEPS, edges((1, messages), (0, transpose_ends)))
            carry(L, F, L["cp_a"])

            L = flow["gat"]

            def gat_keys(g):
                wait_done(pe, L["bcd"], g)
                transpose_step(L, g, 0, bc, "tr_a", "samed")

            def gat_tile_sums(g):
                wait_done(pe, L["samed"], g)
                wait_done(pe, L["msgd"], g)
                wait_free(pe, L["cp_a"], g)
                for j in range(J):
                    last = te.matmul(ps[2][g.b][:, :], msg[:, g.b, j, 0:F], same[g.b][:, j, :], start=j == 0, stop=j == J - 1)
                wait_free(pe, L["cp_b"], g)
                wait_done(pe, L["w_lo"], g)
                wait_done(pe, L["same_bf"], g)
                settle(pe)
                for i in range(J):
                    for j in range(J):
                        last = te.matmul(ps[1][g.b][:, 3 * i:3 * i + 3], same_bf[:, g.b, j, i * P:(i + 1) * P], w_parts[:, g.b, :, j],
                                         start=j == 0, stop=j == J - 1)
                last.then_inc(L["mm"].sem, 1)

            def gat_project(g):
                wait_done(pe, L["cp_a"], g)
                wait_free(pe, L["cp_b"], g)
                for j in range(J):
                    c = slice(j * F, (j + 1) * F)
                    last = te.matmul(ps[3][g.b][:, c], t_c[:, g.b, c], natural["w_gat"][:, :], start=True, stop=True)
                last.then_inc(L["mm2"].sem, 1)

            pipeline(pe, STEPS, edges((2, gat_project), (1, gat_tile_sums), (0, gat_keys)))
            for n in ("samed", "cp_a", "cp_b"):
                pe.wait_ge(L[n].sem, L[n].at(STEPS))

            D = flow["nodes2"]

            def by_bank(pn):
                return [(j, j // J, j % J, slice(j % J * F, j % J * F + pn)) for j in range(DJ)]

            def nodes_transpose_x2(g):
                pn = dense_p(g)
                wait_done(pe, D["n_row"], g)
                wait_previous(pe, D["x2tc"], g)
                for j, bank, _, c in by_bank(pn):
                    last = te.transpose(ps[0][bank][:, c], node_out[0:pn, g.b, j, :], ident[0:pn, 0:pn])
                last.then_inc(D["x2tp"].sem, 1)

            def nodes_h1(g):
                wait_done(pe, D["x2tc"], g)
                wait_previous(pe, D["h1tc"], g)
                for h in range(2):
                    last = te.matmul(ps[1][h][:, :], w1r_t[:, :], node_x2t[:, g.b, h * J * F:(h + 1) * J * F], start=True, stop=True)
                last.then_inc(D["h1p"].sem, 1)

            def nodes_y(g):
                pn = dense_p(g)
                wait_done(pe, D["h1tc"], g)
                wait_previous(pe, D["y"], g)
                for j, bank, i, _ in by_bank(pn):
                    if i == 0:
                        te.matmul(ps[3][bank][0:pn, :], ones_bf[:, 0:pn], b2_parts[:, :, :].rearrange("p j f -> p (j f)"),
                                  start=True, stop=False)
                    last = te.matmul(ps[3][bank][0:pn, i * F:(i + 1) * F], node_h1t[:, g.b, j * F:j * F + pn], w2r_t[:, :],
                                     start=False, stop=i == J - 1)
                last.then_inc(D["yp"].sem, 1)

            def nodes_h1_rows(g):
                pn = dense_p(g)
                wait_previous(pe, D["h1c"], g)
                for j, bank, i, _ in by_bank(pn):
                    last = te.transpose(ps[2][bank][0:pn, i * F:(i + 1) * F], node_h1t[:, g.b, j * F:j * F + pn], ident[:, :])
                last.then_inc(D["h1tp"].sem, 1)

            pipeline(pe, DENSE_FULL, [nodes(4, nodes_y), nodes(3, nodes_transpose_x2), nodes(4, nodes_h1_rows), nodes(3, nodes_h1)])
            for n in ("x2tc", "h1tc", "h1c", "y"):
                pe.wait_ge(D[n].sem, D[n].at(DENSE_STEPS))

            L = flow["sage1"]

            def sage_transpose(g, jn=J):
                wait_done(pe, L["msgd"], g)
                transpose_step(L, g, 0, msg, "tr_a", "cp_a", jn)
                if g is FIX:
                    pe.wait_ge(fix_in, 48 * (LAYER_NO["sage1" if L is flow["sage1"] else "sage2"] + 1))
                else:
                    wait_landed(pe, L["own"], g)
                transpose_step(L, g, 1, own_rows, "tr_b", "cp_b", jn)

            def sage_h1(g, jn=J):
                wait_done(pe, L["cp_a"], g)
                wait_done(pe, L["cp_b"], g)
                wait_free(pe, L["cp_c"], g)
                c = slice(0, jn * F)
                te.matmul(ps[2][g.b][:, c], w1l_t[:, :], t_a[:, g.b, c], start=True, stop=False)
                te.matmul(ps[2][g.b][:, c], w1r_t[:, :], t_b[:, g.b, c], start=False, stop=True).then_inc(L["mm"].sem, 1)

            def sage_h1_rows(g, jn=J):
                wait_done(pe, L["cp_c"], g)
                wait_free(pe, L["newd"], g)
                for j in range(jn):
                    c = slice(j * F, (j + 1) * F)
                    last = te.transpose(ps[3][g.b][:, c], t_c[:, g.b, c], ident[:, :])
                last.then_inc(L["mm2"].sem, 1)

            pipeline(pe, STEPS, edges((2, sage_h1_rows), (1, sage_h1), (0, sage_transpose)))
            carry(L, F + 1, L["cp_a"])
            sage_transpose(FIX, 1)
            sage_h1(FIX, 1)
            sage_h1_rows(FIX, 1)

            L = flow["sage2"]

            def sage_out(g, jn=J):
                wait_done(pe, L["cp_a"], g)
                wait_done(pe, L["cp_b"], g)
                wait_free(pe, L["pre"], g)
                te.matmul(ps[3][g.b][:, 0:jn * F], ones_bf[:, :], b2_parts[:, 0:jn, :].rearrange("p j f -> p (j f)"),
                          start=True, stop=False)
                for j in range(jn):
                    c = slice(j * F, (j + 1) * F)
                    te.matmul(ps[3][g.b][:, c], t_a[:, g.b, c], w2l_t[:, :], start=False, stop=False)
                    last = te.matmul(ps[3][g.b][:, c], t_b[:, g.b, c], w2r_t[:, :], start=False, stop=j == jn - 1)
                last.then_inc(L["mm"].sem, 1)

            pipeline(pe, STEPS, edges((1, sage_out), (0, sage_transpose)))
            carry(L, F + 1, L["cp_a"])
            sage_transpose(FIX, 1)
            sage_out(FIX, 1)

            L = flow["att1"]

            def att_transpose(g):
                wait_landed(pe, L["gathered"], g)
                transpose_step(L, g, 0, src_rows, "tr_a", "cp_a")
                transpose_step(L, g, 1, own_rows, "tr_b", "cp_b")

            def queries_keys(g):
                wait_done(pe, L["cp_a"], g)
                wait_free(pe, L["newd"], g)
                for j in range(J):
                    c = slice(j * F, (j + 1) * F)
                    last = te.matmul(ps[2][g.b][:, c], t_a[:, g.b, c], qw_sb[:, :, :].rearrange("f h d -> f (h d)"), start=True, stop=True)
                last.then_inc(L["mm"].sem, 1)
                wait_done(pe, L["cp_b"], g)
                wait_free(pe, L["cp_c"], g)
                for j in range(J):
                    c = slice(j * F, (j + 1) * F)
                    last = te.matmul(ps[3][g.b][:, c], t_b[:, g.b, c], kw_sb[:, :, :].rearrange("f h d -> f (h d)"), start=True, stop=True)
                last.then_inc(L["mm2"].sem, 1)

            pipeline(pe, STEPS, edges((1, queries_keys), (0, att_transpose)))
            pe.wait_ge(max_at, 1)
            for i in range(2):
                last = te.matmul(ps[i][0][:, :], ones[:, :],
                                 diag[:, 2 + i * HEADS:2 + (i + 1) * HEADS, :].rearrange("p h q -> p (h q)"), start=True, stop=True)
            last.then_inc(max_at, 1)

            L = flow["att2"]
            pe.wait_ge(max_at, 3)

            def att_back_transpose(g, jn=J):
                wait_done(pe, L["msg0"], g)
                transpose_step(L, g, 0, gate, "tr_a", "cp_a", jn)

            def att_project(g, jn=J):
                wait_done(pe, L["cp_a"], g)
                wait_free(pe, L["pre2"], g)
                for j in range(jn):
                    c = slice(j * F, (j + 1) * F)
                    last = te.matmul(ps[3][g.b][:, c], t_a[:, g.b, c], outw_sb[:, :], start=True, stop=True)
                last.then_inc(L["mm"].sem, 1)

            pipeline(pe, STEPS, edges((1, att_project), (0, att_back_transpose)))
            pe.wait_ge(L["accd"].sem, L["accd"].at(STEPS))
            carry(L, ACC_W, L["cp_a"])
            att_back_transpose(FIX, 1)
            att_project(FIX, 1)

        @block.scalar
        def _(act):
            sc = nc.scalar
            act.wait_ge(cols_in, 16 * 5)
            sc.activation(sbeta_col, beta_col, ACT.Silu).then_inc(act_prep, 1)

            def roots(L, k):
                def root(g, jn=None):
                    pn, jn = (dense_p(g), DJ) if k == "n" else (P, jn or J)
                    wait_done(act, L[f"{k}_ve"], g)
                    at = NORM[k][2][0:pn, g.b, 0:jn]
                    sc.activation(at, at, ACT.Sqrt).then_inc(L[f"{k}_rt"].sem, 1)
                return root

            def normed_rows(L, k, rows, to, made, out_ring=None, used=()):
                def make(g, jn=None):
                    pn, jn = (dense_p(g), DJ) if k == "n" else (P, jn or J)
                    if out_ring:
                        wait_drained(act, L[out_ring], g)
                    for signal in used:
                        wait_free(act, L[signal], g)
                    wait_done(act, L[f"{k}_nm"], g)
                    for j in range(jn):
                        last = sc.activation(to[0:pn, g.b, j, :], rows[0:pn, g.b, j, 0:F], ACT.Identity,
                                             bias=NORM[k][3][0:pn, g.b, j:j + 1], scale=NORM[k][2][0:pn, g.b, j:j + 1])
                    last.then_inc(L[made].sem, 1)
                return make

            D = flow["nodes1"]
            pipeline(act, DENSE_FULL, [nodes(1, normed_rows(D, "n", node_in, node_out, "n_row", "n_out")), nodes(0, roots(D, "n"))])

            def copy_out(L, g, bank, to, produced, copied, free, jn=J):
                wait_done(act, L[produced], g)
                wait_free(act, L[free], g)
                sc.activation(to[:, g.b, 0:jn * F], ps[bank][g.b][:, 0:jn * F], ACT.Copy).then_inc(L[copied].sem, 1)

            L = flow["msg"]

            def copy_ends(g):
                copy_out(L, g, 0, t_a, "tr_a", "cp_a", "mm")
                copy_out(L, g, 1, t_b, "tr_b", "cp_b", "mm")
                wait_done(act, L["tr_e"], g)
                sc.activation(t_e[0:FE, g.b, :], ps[2][g.b][0:FE, :], ACT.Copy).then_inc(L["cp_e"].sem, 1)

            def sigmoid(g):
                wait_done(act, L["mm"], g)
                wait_free(act, L["msg0"], g)
                sc.activation(gate[:, g.b, :, :].rearrange("p j f -> p (j f)"), ps[3][g.b][:, :], ACT.Sigmoid)\
                    .then_inc(L["sig"].sem, 1)

            new_x1 = normed_rows(L, "e", pre, new_rows, "newd", "stored")
            pipeline(act, STEPS, edges((3, new_x1), (1, sigmoid), (0, copy_ends)))
            new_x1(FIX, 1)

            L = flow["gat"]

            def exp_scores(g):
                wait_done(act, L["e2"], g)
                wait_free(act, L["msgd"], g)
                sc.activation(edge4[:, g.b, 4, :], edge4[:, g.b, 3, :], ACT.Exp).then_inc(L["expd"].sem, 1)

            def gat_copy_sums(g):
                wait_done(act, L["mm"], g)
                wait_free(act, L["mm2"], g)
                sc.activation(t_c[:, g.b, :], ps[2][g.b][:, :], ACT.Copy).then_inc(L["cp_a"].sem, 1)

            def gat_copy_projected(g):
                if not g.first_use():
                    act.wait_ge(L["added"].sem, L["added"].per * (g.index() - 1))
                wait_done(act, L["mm2"], g)
                sc.activation(sums[:, g.b, :, F:F + 3], ps[1][g.b][:, 0:3 * J].rearrange("p (j w) -> p j w", w=3), ACT.Copy)
                sc.activation(sums[:, g.b, :, 0:F], ps[3][g.b][:, :].rearrange("p (j f) -> p j f", f=F), ACT.Copy)\
                    .then_inc(L["cp_b"].sem, 1)

            def same_to_bf16(g):
                wait_done(act, L["samed"], g)
                wait_free(act, L["mm"], g)
                sc.activation(same_bf[:, g.b, :, :].rearrange("p j i -> p (j i)"), same[g.b].rearrange("p j i -> p (j i)"), ACT.Copy)\
                    .then_inc(L["same_bf"].sem, 1)

            pipeline(act, STEPS, edges((2, gat_copy_projected), (1, same_to_bf16), (1, gat_copy_sums), (0, exp_scores)))

            L, D = flow["x2"], flow["nodes2"]
            banks = [(h, slice(h * J * F, (h + 1) * J * F)) for h in range(2)]

            def nodes_copy_x2t(g):
                wait_done(act, D["x2tp"], g)
                wait_free(act, D["h1p"], g)
                for h, c in banks:
                    last = sc.activation(node_x2t[:, g.b, c], ps[0][h][:, :], ACT.Copy)
                last.then_inc(D["x2tc"].sem, 1)

            def nodes_relu(g):
                wait_done(act, D["h1p"], g)
                wait_free(act, D["h1tp"], g)
                for h, c in banks:
                    last = sc.activation(node_h1t[:, g.b, c], ps[1][h][:, :], ACT.Relu, bias=b1_col)
                last.then_inc(D["h1tc"].sem, 1)

            def nodes_copy_h1(g):
                pn = dense_p(g)
                wait_done(act, D["h1tp"], g)
                wait_drained(act, D["n_h1"], g)
                for h, _ in banks:
                    last = sc.activation(node_h1[0:pn, g.b, h * J:(h + 1) * J, :].rearrange("p j f -> p (j f)"),
                                         ps[2][h][0:pn, :], ACT.Copy)
                last.then_inc(D["h1c"].sem, 1)

            pipeline(act, DENSE_FULL, [
                nodes(3, nodes_copy_x2t), nodes(4, nodes_copy_h1), nodes(3, nodes_relu),
                nodes(2, normed_rows(D, "n", node_in, node_out, "n_row", "n_out", ("x2tp", "y")))]
                + edges((2, normed_rows(L, "e", pre, new_rows, "newd", "stored")))
                + [nodes(1, roots(D, "n"))] + edges((1, roots(L, "e"))))

            L = flow["sage1"]

            def sage_copies(g, jn=J):
                copy_out(L, g, 0, t_a, "tr_a", "cp_a", "mm", jn)
                copy_out(L, g, 1, t_b, "tr_b", "cp_b", "mm", jn)

            def sage_relu(g, jn=J):
                wait_done(act, L["mm"], g)
                wait_free(act, L["mm2"], g)
                sc.activation(t_c[:, g.b, 0:jn * F], ps[2][g.b][:, 0:jn * F], ACT.Relu, bias=b1_col).then_inc(L["cp_c"].sem, 1)

            def h1_rows(g, jn=J):
                wait_done(act, L["mm2"], g)
                wait_drained(act, L["stored"], g)
                sc.activation(new_rows[:, g.b, 0:jn, :].rearrange("p j f -> p (j f)"), ps[3][g.b][:, 0:jn * F], ACT.Copy)\
                    .then_inc(L["newd"].sem, 1)

            D = flow["nodes3"]
            pipeline(act, DENSE_FULL, edges((2, h1_rows), (1, sage_relu))
                     + [nodes(1, normed_rows(D, "n", node_in, node_out, "n_row", "n_out"))]
                     + edges((0, sage_copies)) + [nodes(0, roots(D, "n"))])
            sage_copies(FIX, 1)
            sage_relu(FIX, 1)
            h1_rows(FIX, 1)

            L = flow["sage2"]
            new_x3, root = normed_rows(L, "e", pre, new_rows, "newd", "stored"), roots(L, "e")
            pipeline(act, STEPS, edges((3, new_x3), (2, root), (0, sage_copies)))
            sage_copies(FIX, 1)
            root(FIX, 1)
            new_x3(FIX, 1)

            L, D = flow["att1"], flow["nodes4"]

            def att_copies(g):
                copy_out(L, g, 0, t_a, "tr_a", "cp_a", "mm")
                copy_out(L, g, 1, t_b, "tr_b", "cp_b", "mm2")

            def queries_keys_out(g):
                wait_done(act, L["mm"], g)
                wait_drained(act, L["stored"], g)
                wait_free(act, L["pre"], g)
                sc.activation(new_rows[:, g.b, :, :].rearrange("p j f -> p (j f)"), ps[2][g.b][:, :], ACT.Copy)\
                    .then_inc(L["newd"].sem, 1)
                wait_done(act, L["mm2"], g)
                sc.activation(gate[:, g.b, :, :].rearrange("p j f -> p (j f)"), ps[3][g.b][:, :], ACT.Copy,
                              scale=float(HID) ** -0.5).then_inc(L["cp_c"].sem, 1)

            pipeline(act, DENSE_FULL, edges((1, queries_keys_out)) + [nodes(1, normed_rows(D, "n", node_in, node_out, "n_row", "n_out"))]
                     + edges((0, att_copies)) + [nodes(0, roots(D, "n"))])
            act.wait_ge(max_at, 4)
            sc.activation(alpha[:, :, :].rearrange("p t h -> p (t h)"), tmp_a[:, :, :].rearrange("p t h -> p (t h)"),
                          ACT.Exp).then_inc(max_at, 1)

            L = flow["att2"]

            def silu(g, jn=J):
                wait_done(act, L["tr_a"], g)
                wait_free(act, L["mm"], g)
                sc.activation(t_a[:, g.b, 0:jn * F], ps[0][g.b][:, 0:jn * F], ACT.Silu, bias=beta_col, scale=gamma_col)\
                    .then_inc(L["cp_a"].sem, 1)

            normed = normed_rows(L, "e", pre, gate, "msg0", None, ("tr_a",))
            new_x4 = normed_rows(L, "a", ny, new_rows, "newd", "scattered")
            pipeline(act, STEPS, edges((6, new_x4), (3, silu), (2, normed)))
            normed(FIX, 1)
            silu(FIX, 1)
            new_x4(FIX, 1)

        @block.vector
        def _(dve):
            v = nc.vector
            linked = [0]

            def link(ins):
                linked[0] += 1
                ins.then_inc(slots_made, 1)
                dve.wait_ge(slots_made, linked[0])

            first, last_ = d[:, 1:2], d[:, T:T + 1]
            dve.wait_ge(consts_made, 3)
            dve.wait_ge(dst_in, 48)
            dve.wait_ge(src_in, 16)
            v.memset(t_e[FE:FE + 1, :, :], 1.0)
            v.memset(earlier[:, 0:(J - 1) * P], 1.0)
            v.tensor_copy(earlier[:, (J - 1) * P:], lower[:, :])
            link(v.tensor_copy(d[:, :], dst_i[:, :]))
            v.tensor_copy(slot[:, :], slot_i[:, :])
            v.tensor_tensor(keep[:, :], d[:, 1:T + 1], d[:, 0:T], ALU.is_equal)
            v.tensor_tensor(canon[:, :], d[:, 1:T + 1], d[:, 2:T + 2], ALU.not_equal)
            v.tensor_scalar(in_first[:, :], d[:, 1:T + 1], first, None, ALU.is_equal)
            v.tensor_scalar(in_open[:, :], d[:, 1:T + 1], last_, None, ALU.is_equal)
            link(v.tensor_scalar_min(dst_safe_i[:, :], d[:, 1:T + 1], float(N_NODES - 1)))
            v.memset(keep[:, 0:1], 0.0)
            link(v.tensor_scalar(tmp_t[:, :], canon[:, :], -float(FAR), float(FAR), ALU.mult, ALU.add))
            link(v.tensor_tensor(map_index[:, :], tmp_t[:, :], d[:, 1:T + 1], ALU.add))
            v.tensor_scalar(open_last, canon[:, T - 1:T], -1.0, 1.0, ALU.mult, ALU.add).then_inc(map_index_made, 1)
            link(v.tensor_tensor(first_done[:, :], in_first[:, :], canon[:, :], ALU.mult))
            link(v.reduce_sum(has_first, first_done[:, :], axis=AX))
            link(v.tensor_tensor(tmp_t[:, :], first_done[:, :], slot[:, :], ALU.mult))
            link(v.reduce_sum(fix_slot, tmp_t[:, :], axis=AX))
            v.tensor_copy(fix_f[:, 0:1], fix_slot)
            link(v.tensor_copy(fix_read, fix_slot))
            link(v.tensor_scalar(fix_f[:, 1:2], has_first, -float(FAR), float(FAR), ALU.mult, ALU.add))
            link(v.tensor_tensor(fix_write, fix_f[:, 1:2], fix_slot, ALU.add))
            v.tensor_tensor(fix_out, fix_f[:, 1:2], first, ALU.add)
            v.tensor_copy(fix_node, dst_safe_i[:, 0:1])
            link(v.tensor_tensor(canon_inner[:, :], canon[:, :], first_done[:, :], ALU.subtract))
            link(v.tensor_scalar(tmp_t[:, :], canon_inner[:, :], -float(FAR), float(FAR), ALU.mult, ALU.add))
            link(v.tensor_tensor(out_index[:, :], tmp_t[:, :], d[:, 1:T + 1], ALU.add))
            link(v.tensor_scalar(tmp_t[:, 0:1], first, float(N_NODES - 1), None, ALU.is_gt))
            link(v.tensor_tensor(dummy_row[:, 1:2], tmp_t[:, 0:1], dummy_row[:, 0:1], ALU.mult))
            link(v.tensor_scalar(source_key[:, :], src_i[:, :], dummy_row[:, 1:2], None, ALU.add))
            link(v.tensor_scalar(in_open[:, :], in_open[:, :], open_last, None, ALU.mult))
            link(v.tensor_scalar(first_done[:, :], in_first[:, :], has_first, None, ALU.mult))
            v.tensor_scalar(diag[:, 0, :], ident[:, :], first, None, ALU.mult)
            v.tensor_scalar(diag[:, 1, :], ident[:, :], last_, None, ALU.mult).then_inc(fix_ready, 1)
            dve.wait_ge(pe_prep, 2)
            first_row, last_row = ps[2][0][:, 0:P], ps[2][0][:, P:2 * P]
            link(v.scalar_tensor_tensor(sum_carry[:, :], first_row, last_, upper[:, :], ALU.is_equal, ALU.mult))
            link(v.scalar_tensor_tensor(back_carry[:, :], last_row, first, lower[:, :], ALU.is_equal, ALU.mult))
            link(v.tensor_scalar(back_carry[:, :], back_carry[:, :], has_first, None, ALU.mult))
            for i, (row, col) in enumerate(((first_row, first), (last_row, first), (first_row, last_), (last_row, last_))):
                link(v.tensor_scalar(max_pen[:, i, :], row, col, None, ALU.is_equal))
            link(v.tensor_scalar(max_pen[:, :, :], max_pen[:, :, :], 1.0, LOW, ALU.subtract, ALU.mult))
            link(v.tensor_scalar(undone[:, 0, :], canon[:, :], -1.0, 1.0, ALU.mult, ALU.add))
            for k in range(1, len(DOUBLINGS)):
                s = DOUBLINGS[k - 1]
                v.tensor_copy(undone[:, k, T - s:T], undone[:, k - 1, T - s:T])
                link(v.tensor_tensor(undone[:, k, 0:T - s], undone[:, k - 1, 0:T - s], undone[:, k - 1, s:T], ALU.mult))

            def spread_back(value, fix, times):
                link(v.tensor_tensor(spread[:, :], value, canon_inner[:, :], ALU.mult))
                for k, s in enumerate(DOUBLINGS):
                    link(v.tensor_tensor(tmp_t[:, 0:T - s], spread[:, s:T], undone[:, k, 0:T - s], ALU.mult))
                    link(v.tensor_tensor(spread[:, 0:T - s], spread[:, 0:T - s], tmp_t[:, 0:T - s], ALU.add))
                link(v.scalar_tensor_tensor(spread[:, :], first_done[:, :], fix, spread[:, :], ALU.mult, ALU.add))
                dve.wait_ge(carried, times)
                link(v.tensor_copy(carry_p, ps[2][0][:, 256:257]))
                link(v.scalar_tensor_tensor(spread[:, :], in_open[:, :], carry_p, spread[:, :], ALU.mult, ALU.add))

            v.memset(junk[:, 0, 0, 0:1], 0.0).then_inc(spread_at, 1)
            spread_back(slot[:, :], fix_slot, 1)
            v.tensor_copy(canon_slot_i[:, :], spread[:, :]).then_inc(index_made, 1)
            dve.wait_ge(weights_in, 16 * 12)
            link(v.tensor_copy(b2_hi[:, :], b2_rows[:, :]))
            link(v.tensor_tensor(b2_rows[:, :], b2_rows[:, :], b2_hi[:, :], ALU.subtract))
            link(v.tensor_copy(b2_mid[:, :], b2_rows[:, :]))
            link(v.tensor_tensor(b2_rows[:, :], b2_rows[:, :], b2_mid[:, :], ALU.subtract))
            link(v.tensor_copy(b2_lo[:, :], b2_rows[:, :]))
            v.tensor_copy(ones_bf[:, :], ones[0:3, :])
            link(v.tensor_scalar(b2_hi[:, :], b2_hi[:, :], ident[0:3, 0:1], None, ALU.mult))
            link(v.scalar_tensor_tensor(b2_mid[:, :], b2_mid[:, :], ident[0:3, 1:2], b2_hi[:, :], ALU.mult, ALU.add))
            for j in range(J):
                v.scalar_tensor_tensor(b2_parts[:, j, :], b2_lo[:, :], ident[0:3, 2:3], b2_mid[:, :], ALU.mult, ALU.add)
            dve.wait_ge(pe_prep, 1)
            for i, w in enumerate((w0s_t, w0d_t, wgat_t, w1l_t, w1r_t, w2l_t, w2r_t)):
                v.tensor_copy(w[:, :], ps[i // 4][0][:, (i % 4) * F:(i % 4 + 1) * F])
            v.tensor_copy(w0e_t[0:FE, :], ps[1][0][0:FE, 3 * F:4 * F])
            dve.wait_ge(cols_in, 16 * 5)
            dve.wait_ge(act_prep, 1)
            for i, col in enumerate((adst_col, asrc_col, sbeta_col)):
                last = v.tensor_scalar(col_bc[:, i, :], ones[:, :], col, None, ALU.mult)
            last.then_inc(fix_ready, 1)
            dve.wait_ge(pe_prep, 3)
            dve.wait_ge(weights_in, 16 * 12)
            v.tensor_copy(vdst_bc[:, :], ps[3][0][:, 0:F])
            v.tensor_copy(vsrc_bc[:, :], ps[3][0][:, F:2 * F])
            v.tensor_tensor(local3_bc[:, :], ps[3][0][:, 2 * F:3 * F], outb_bc[:, :], ALU.add).then_inc(dve_prep, 1)
            dve.wait_ge(dve_prep, 1)

            def moments(L, k, g, rows, pn=P, jn=J):
                stats, mv, root, _ = NORM[k]
                for j in range(jn):
                    last = v.bn_stats(stats[0:pn, g.b, j, :], rows[0:pn, g.b, j, 0:F])
                last.then_inc(L[f"{k}_bn"].sem, 1)
                wait_free(dve, L[f"{k}_nm"], g)
                wait_done(dve, L[f"{k}_bn"], g)
                settle(dve)
                for j in range(jn):
                    last = v.bn_aggr(mv[0:pn, g.b, j, :], stats[0:pn, g.b, j, :])
                last.then_inc(L[f"{k}_ag"].sem, 1)
                wait_done(dve, L[f"{k}_ag"], g)
                v.tensor_scalar_add(root[0:pn, g.b, 0:jn], mv[0:pn, g.b, 0:jn, 1], EPS).then_inc(L[f"{k}_ve"].sem, 1)

            def shifts(L, k, inverted=True):
                def make(g, jn=None):
                    pn, jn = (dense_p(g), DJ) if k == "n" else (P, jn or J)
                    _, mv, root, shift = NORM[k]
                    at = root[0:pn, g.b, 0:jn]
                    wait_done(dve, L[f"{k}_rt"], g)
                    if inverted:
                        v.reciprocal(at, at).then_inc(L[f"{k}_rc"].sem, 1)
                        wait_done(dve, L[f"{k}_rc"], g)
                    v.scalar_tensor_tensor(shift[0:pn, g.b, 0:jn], mv[0:pn, g.b, 0:jn, 0], -1.0, at, ALU.mult, ALU.mult)\
                        .then_inc(L[f"{k}_nm"].sem, 1)
                return make

            def node_moments(D):
                def make(g):
                    wait_landed(dve, D["n_in"], g)
                    wait_free(dve, D["n_row"], g)
                    moments(D, "n", g, node_in, dense_p(g), DJ)
                return make

            D = flow["nodes1"]
            pipeline(dve, DENSE_FULL, [nodes(1, shifts(D, "n")), nodes(0, node_moments(D))])

            def running_sums(L, g, rows, width):
                wait_drained(dve, L["dumped"], g)
                for j in range(J):
                    wait_part(dve, L["accd"], g, j)
                    before = acc[:, g.b, j - 1, 0:width] if j else acc[:, 1 - g.b, J - 1, 0:width]
                    v.scalar_tensor_tensor(acc[:, g.b, j, 0:width], before, keep[:, bass.ds(g.index() * J + j, 1)],
                                           rows[:, g.b, j, 0:width], ALU.mult, ALU.add).then_inc(L["accd"].sem, 1)

            def fix_sums(L, width, times):
                n = LAYER_NO[next(k for k in flow if flow[k] is L)]
                dve.wait_ge(fix_in, 48 * (n + 1))
                dve.wait_ge(carried, times)
                v.tensor_tensor(acc[:, 0, 0, 0:width], fix_acc[:, 0:width], ps[0][0][:, 0:width], ALU.add)\
                    .then_inc(L["accd"].sem, J)

            L = flow["msg"]

            def message_sums(g):
                wait_done(dve, L["sig"], g)
                v.tensor_tensor(msg[:, g.b, :, 0:F], ps[3][g.b][:, :].rearrange("p (j f) -> p j f", f=F), gate[:, g.b, :, :], ALU.mult)\
                    .then_inc(L["msg0"].sem, 1)
                wait_done(dve, L["msg0"], g)
                v.scalar_tensor_tensor(msg[:, g.b, :, 0:F], msg[:, g.b, :, 0:F], 0.01, msg[:, g.b, :, 0:F], ALU.mult, ALU.max)\
                    .then_inc(L["msgd"].sem, 1)
                wait_done(dve, L["msgd"], g)
                running_sums(L, g, msg, F)

            def x1_sums(g, jn=J):
                wait_free(dve, L["newd"], g)
                wait_done(dve, L["accd"], g)
                v.tensor_tensor(pre[:, g.b, 0:jn, :], own_rows[:, g.b, 0:jn, :], acc[:, g.b, 0:jn, 0:F], ALU.add).then_inc(L["pre"].sem, 1)
                wait_done(dve, L["pre"], g)
                moments(L, "e", g, pre, P, jn)

            x1_shifts = shifts(L, "e", False)
            pipeline(dve, STEPS, edges((3, x1_shifts), (1, message_sums), (1, x1_sums)))
            fix_sums(L, F, 2)
            x1_sums(FIX, 1)
            x1_shifts(FIX, 1)
            L = flow["gat"]

            def edge_scores(g):
                wait_landed(dve, L["gathered"], g)
                for i, (rows, vec) in enumerate(((own_rows, vdst_bc), (src_rows, vsrc_bc))):
                    for j in range(J):
                        last = v.tensor_tensor_reduce(out=junk[:, i, j, :], in0=rows[:, g.b, j, 0:F], in1=vec[:, :], scale=1.0,
                                                      scalar=0.0, op0=ALU.mult, op1=ALU.add, accum_out=edge4[:, g.b, i, j:j + 1])
                last.then_inc(L["score"].sem, 1)
                wait_done(dve, L["score"], g)
                v.tensor_tensor(edge4[:, g.b, 2, :], edge4[:, g.b, 0, :], edge4[:, g.b, 1, :], ALU.add).then_inc(L["e0"].sem, 1)
                wait_done(dve, L["e0"], g)
                v.scalar_tensor_tensor(edge4[:, g.b, 5, :], edge4[:, g.b, 2, :], 0.2, edge4[:, g.b, 2, :], ALU.mult, ALU.max)\
                    .then_inc(L["e1"].sem, 1)
                wait_free(dve, L["expd"], g)
                wait_done(dve, L["e1"], g)
                v.tensor_scalar(edge4[:, g.b, 3, :], edge4[:, g.b, 5, :], -2.0, 2.0, ALU.max, ALU.min).then_inc(L["e2"].sem, 1)

            def edge_keys(g):
                v.tensor_copy(key4[:, g.b, 0, :], fours(source_key, g)).then_inc(L["keyd"].sem, 1)
                wait_free(dve, L["tr_a"], g)
                wait_done(dve, L["keyd"], g)
                for j in range(J):
                    last = v.tensor_scalar(bc[:, g.b, j, :], ones[:, :], key4[:, g.b, 0, j:j + 1], None, ALU.mult)
                last.then_inc(L["bcd"].sem, 1)

            def same_sources(g):
                wait_done(dve, L["tr_a"], g)
                wait_free(dve, L["mm"], g)
                for j in range(J):
                    last = v.tensor_scalar(same[g.b][:, j, :], ps[0][g.b][:, :], key4[:, g.b, 0, j:j + 1], None, ALU.is_equal)
                last.then_inc(L["samed"].sem, 1)
                wait_done(dve, L["samed"], g)
                for j in range(J):
                    n = (j + 1) * P
                    last = v.tensor_tensor_reduce(out=junk2[:, j, 0:n], in0=same[g.b][:, j, 0:n], in1=earlier[:, J * P - n:], scale=1.0,
                                                  scalar=0.0, op0=ALU.mult, op1=ALU.add, accum_out=key4[:, g.b, 1, j:j + 1])
                last.then_inc(L["rep0"].sem, 1)
                v.tensor_tensor(key4[:, g.b, 2, :], key4[:, g.b, 0, :], dummy_rows[:, :], ALU.subtract)
                wait_done(dve, L["rep0"], g)
                v.tensor_scalar(key4[:, g.b, 3, :], key4[:, g.b, 1, :], 0.0, None, ALU.is_equal).then_inc(L["rep1"].sem, 1)
                wait_free(dve, L["rep2"], g)
                wait_done(dve, L["rep1"], g)
                v.tensor_tensor(key4[:, g.b, 4, :], key4[:, g.b, 2, :], key4[:, g.b, 3, :], ALU.mult).then_inc(L["rep3"].sem, 1)

            def add_indices(g):
                if not g.first_use():
                    dve.wait_ge(L["added"].sem, L["added"].per * (g.index() - 1))
                wait_done(dve, L["rep3"], g)
                v.tensor_tensor(add_idx[:, g.b, :], key4[:, g.b, 4, :], dummy_rows[:, :], ALU.add).then_inc(L["rep2"].sem, 1)

            def weighted_rows(g):
                wait_done(dve, L["expd"], g)
                wait_free(dve, L["mm"], g)
                for j in range(J):
                    last = v.tensor_scalar(msg[:, g.b, j, 0:F], src_rows[:, g.b, j, 0:F], edge4[:, g.b, 4, j:j + 1], None, ALU.mult)
                last.then_inc(L["msgd"].sem, 1)

            def weight_parts(g):
                left = edge4[:, g.b, 4, :]
                v.tensor_copy(w_parts[:, g.b, 0, :], left).then_inc(L["w_hi"].sem, 1)
                for i, (part, rest, after) in enumerate((("w_hi", "w_r1", "w_mid"), ("w_mid", "w_r2", "w_lo"))):
                    wait_done(dve, L[part], g)
                    v.tensor_tensor(w_left[:, g.b, i, :], left, w_parts[:, g.b, i, :], ALU.subtract).then_inc(L[rest].sem, 1)
                    left = w_left[:, g.b, i, :]
                    wait_done(dve, L[rest], g)
                    v.tensor_copy(w_parts[:, g.b, i + 1, :], left).then_inc(L[after].sem, 1)

            pipeline(dve, STEPS, edges((2, add_indices), (1, weighted_rows), (1, weight_parts), (1, same_sources), (0, edge_keys), (0, edge_scores)))

            L, D = flow["x2"], flow["nodes2"]

            def add_means(M, names, g, rows, row_sums, recips, to, pn, jn):
                rcs, rc0, rc1, made = names
                at = recips[0:pn, g.b, 0, 0:jn]
                v.tensor_reduce(at, row_sums[0:pn, g.b, 0:jn, F:F + 3], axis=AX, op=ALU.add).then_inc(M[rcs].sem, 1)
                wait_done(dve, M[rcs], g)
                v.tensor_scalar_max(at, at, 1e-30).then_inc(M[rc0].sem, 1)
                wait_done(dve, M[rc0], g)
                v.reciprocal(recips[0:pn, g.b, 1, 0:jn], recips[0:pn, g.b, 0, 0:jn]).then_inc(M[rc1].sem, 1)
                wait_done(dve, M[rc1], g)
                for j in range(jn):
                    last = v.scalar_tensor_tensor(to[0:pn, g.b, j, :], row_sums[0:pn, g.b, j, 0:F], recips[0:pn, g.b, 1, j:j + 1],
                                                  rows[0:pn, g.b, j, :], ALU.mult, ALU.add)
                last.then_inc(M[made].sem, 1)
                wait_done(dve, M[made], g)

            def slots_x2(g):
                wait_landed(dve, L["own"], g)
                wait_landed(dve, L["gathered"], g)
                wait_free(dve, L["newd"], g)
                add_means(L, ("rcs", "rc0", "rc1", "pre"), g, own_rows, sums, edge4, pre, P, J)
                moments(L, "e", g, pre)

            def nodes_x2(g):
                wait_landed(dve, D["n_in"], g)
                wait_free(dve, D["n_row"], g)
                add_means(D, ("n_rcs", "n_rc0", "n_rc1", "n_pre"), g, node_in, node_sums, node_recip, node_in, dense_p(g), DJ)
                moments(D, "n", g, node_in, dense_p(g), DJ)

            def nodes_y(g):
                pn = dense_p(g)
                wait_done(dve, D["yp"], g)
                wait_drained(dve, D["n_y"], g)
                for h in range(2):
                    rows = slice(h * J, (h + 1) * J)
                    last = v.tensor_tensor(node_y[0:pn, g.b, rows, :].rearrange("p j f -> p (j f)"), ps[3][h][0:pn, :],
                                           node_out[0:pn, g.b, rows, :].rearrange("p j f -> p (j f)"), ALU.add)
                last.then_inc(D["y"].sem, 1)

            pipeline(dve, DENSE_FULL, [nodes(2, shifts(D, "n"))] + edges((2, shifts(L, "e"))) + [nodes(4, nodes_y)]
                     + [nodes(1, nodes_x2)] + edges((1, slots_x2)))

            def plain_sums(g):
                wait_landed(dve, L["gathered"], g)
                running_sums(L, g, src_rows, F + 1)

            def means(g, jn=J):
                wait_done(dve, L["accd"], g)
                v.reciprocal(edge4[:, g.b, 5, 0:jn], acc[:, g.b, 0:jn, F]).then_inc(L["rcp"].sem, 1)
                wait_free(dve, L["tr_a"], g)
                wait_done(dve, L["rcp"], g)
                for j in range(jn):
                    last = v.tensor_scalar(msg[:, g.b, j, 0:F], acc[:, g.b, j, 0:F], edge4[:, g.b, 5, j:j + 1], None, ALU.mult)
                last.then_inc(L["msgd"].sem, 1)

            def sums_and_means(g):
                plain_sums(g)
                means(g)

            L = flow["sage1"]

            D = flow["nodes3"]
            pipeline(dve, DENSE_FULL, [nodes(1, shifts(D, "n"))] + edges((0, sums_and_means)) + [nodes(0, node_moments(D))])
            fix_sums(L, F + 1, 3)
            means(FIX, 1)

            L = flow["sage2"]

            def x3_sums(g, jn=J):
                if g is FIX:
                    dve.wait_ge(fix_in, 48 * 3)
                else:
                    wait_landed(dve, L["own2"], g)
                wait_done(dve, L["mm"], g)
                wait_free(dve, L["newd"], g)
                v.tensor_tensor(pre[:, g.b, 0:jn, :].rearrange("p j f -> p (j f)"), ps[3][g.b][:, 0:jn * F],
                                own2_rows[:, g.b, 0:jn, :].rearrange("p j f -> p (j f)"), ALU.add).then_inc(L["pre"].sem, 1)
                wait_done(dve, L["pre"], g)
                moments(L, "e", g, pre, P, jn)

            x3_shifts = shifts(L, "e")
            pipeline(dve, STEPS, edges((3, x3_shifts), (2, x3_sums), (0, sums_and_means)))
            fix_sums(L, F + 1, 4)
            means(FIX, 1)
            x3_sums(FIX, 1)
            x3_shifts(FIX, 1)

            L, D = flow["att1"], flow["nodes4"]

            def products(g):
                wait_done(dve, L["newd"], g)
                wait_done(dve, L["cp_c"], g)
                wait_free(dve, L["score"], g)
                v.tensor_tensor(pre[:, g.b, :, :], new_rows[:, g.b, :, :], gate[:, g.b, :, :], ALU.mult).then_inc(L["pre"].sem, 1)
                wait_done(dve, L["pre"], g)
                v.tensor_reduce(alpha[:, bass.ds(g.index() * J, J), :], pre[:, g.b, :, :].rearrange("p j (h e) -> p j h e", e=HID),
                                axis=AX, op=ALU.add).then_inc(L["score"].sem, 1)

            def nodes_x3_more(g):
                pn = dense_p(g)
                wait_landed(dve, D["n_in"], g)
                v.tensor_tensor(node_in[0:pn, g.b, :, :], node_in[0:pn, g.b, :, :],
                                local3_bc[0:pn, None, :].to_broadcast([pn, DJ, F]), ALU.add).then_inc(D["n_pre"].sem, 1)
                wait_done(dve, D["n_pre"], g)
                wait_free(dve, D["n_row"], g)
                moments(D, "n", g, node_in, pn, DJ)

            pipeline(dve, DENSE_FULL, edges((2, products)) + [nodes(1, shifts(D, "n")), nodes(0, nodes_x3_more)])
            dve.wait_ge(L["score"].sem, L["score"].at(STEPS))
            link(v.tensor_copy(seg_max[:, :, :], alpha[:, :, :]))

            def hop(s, ahead):
                n = T - s
                a, b = (seg_max[:, s:T, :], seg_max[:, 0:n, :]) if ahead else (seg_max[:, 0:n, :], seg_max[:, s:T, :])
                link(v.tensor_tensor(tmp_t[:, 0:n], d[:, 1:1 + n], d[:, 1 + s:1 + T], ALU.is_equal))
                link(v.tensor_scalar(tmp_t[:, 0:n], tmp_t[:, 0:n], 1.0, LOW, ALU.subtract, ALU.mult))
                link(v.tensor_tensor(tmp_a[:, 0:n, :], a, tmp_t[:, 0:n, None].to_broadcast([P, n, HEADS]), ALU.add))
                link(v.tensor_tensor(b, b, tmp_a[:, 0:n, :], ALU.max))

            for s in DOUBLINGS:
                hop(s, False)
            for s in DOUBLINGS:
                hop(s, True)
            for i, t in enumerate((0, T - 1)):
                for h in range(HEADS):
                    last = v.tensor_scalar(diag[:, 2 + i * HEADS + h, :], ident[:, :], seg_max[:, t, h:h + 1], None, ALU.mult)
            last.then_inc(max_at, 1)
            dve.wait_ge(max_at, 2)
            for i in range(4):
                row = ps[i % 2][0][:, :].rearrange("p (h q) -> p h q", q=P)
                link(v.tensor_tensor(max_row[:, 0, :, :], row, max_pen[:, i:i + 1, :].to_broadcast([P, HEADS, P]), ALU.add))
                link(v.tensor_reduce(max_extra[:, i, :], max_row[:, 0, :, :], axis=AX, op=ALU.max))
            v.tensor_tensor(max_extra[:, 0, :], max_extra[:, 0, :], max_extra[:, 1, :], ALU.max)
            link(v.tensor_tensor(max_extra[:, 2, :], max_extra[:, 2, :], max_extra[:, 3, :], ALU.max))
            for i, at in ((0, first), (2, last_)):
                link(v.tensor_scalar(tmp_t[:, :], d[:, 1:T + 1], at, None, ALU.is_equal))
                link(v.tensor_scalar(tmp_t[:, :], tmp_t[:, :], 1.0, LOW, ALU.subtract, ALU.mult))
                link(v.tensor_tensor(tmp_a[:, :, :], tmp_t[:, :, None].to_broadcast([P, T, HEADS]),
                                     max_extra[:, i:i + 1, :].to_broadcast([P, T, HEADS]), ALU.add))
                link(v.tensor_tensor(seg_max[:, :, :], seg_max[:, :, :], tmp_a[:, :, :], ALU.max))
            v.tensor_tensor(tmp_a[:, :, :], alpha[:, :, :], seg_max[:, :, :], ALU.subtract).then_inc(max_at, 2)
            dve.wait_ge(max_at, 5)

            L = flow["att2"]

            def attended_sums(g):
                wait_landed(dve, L["qin"], g)
                a = fours(alpha, g)
                v.tensor_tensor(msg[:, g.b, :, 0:F].rearrange("p j (h e) -> p j h e", e=HID),
                                src_rows[:, g.b, :, 0:F].rearrange("p j (h e) -> p j h e", e=HID),
                                a[:, :, :, None].to_broadcast([P, J, HEADS, HID]), ALU.mult)
                v.tensor_copy(msg[:, g.b, :, F:F + HEADS], a).then_inc(L["msgd"].sem, 1)
                wait_done(dve, L["msgd"], g)
                running_sums(L, g, msg, ACC_W)

            def attended(g, jn=J):
                wait_done(dve, L["accd"], g)
                v.tensor_scalar_max(recip[:, g.b, 0:jn, :], acc[:, g.b, 0:jn, F:ACC_W], 1e-30).then_inc(L["rcp"].sem, 1)
                wait_done(dve, L["rcp"], g)
                v.reciprocal(recip[:, g.b, 0:jn, :], recip[:, g.b, 0:jn, :]).then_inc(L["rcp2"].sem, 1)
                wait_done(dve, L["rcp2"], g)
                wait_free(dve, L["msg0"], g)
                v.tensor_tensor(pre[:, g.b, 0:jn, :].rearrange("p j (h e) -> p j h e", e=HID),
                                acc[:, g.b, 0:jn, 0:F].rearrange("p j (h e) -> p j h e", e=HID),
                                recip[:, g.b, 0:jn, :, None].to_broadcast([P, jn, HEADS, HID]), ALU.mult).then_inc(L["pre"].sem, 1)
                wait_done(dve, L["pre"], g)
                moments(L, "e", g, pre, P, jn)

            def x4_sums(g, jn=J):
                wait_done(dve, L["mm"], g)
                rows = ps[3][g.b][:, 0:jn * F].rearrange("p (j f) -> p j f", f=F)
                wait_free(dve, L["newd"], g)
                v.tensor_tensor(ny[:, g.b, 0:jn, :], rows, outb_bc[:, None, :].to_broadcast([P, jn, F]), ALU.add).then_inc(L["pre2"].sem, 1)
                if g is FIX:
                    dve.wait_ge(fix_in, 48 * 4)
                else:
                    wait_landed(dve, L["own"], g)
                wait_done(dve, L["pre2"], g)
                v.tensor_tensor(ny[:, g.b, 0:jn, :], ny[:, g.b, 0:jn, :], own_rows[:, g.b, 0:jn, :], ALU.add).then_inc(L["pre3"].sem, 1)
                wait_done(dve, L["pre3"], g)
                moments(L, "a", g, ny, P, jn)

            att_shifts, x4_shifts = shifts(L, "e", False), shifts(L, "a", False)
            pipeline(dve, STEPS, edges((6, x4_shifts), (2, att_shifts), (0, attended_sums), (4, x4_sums), (0, attended)))
            fix_sums(L, ACC_W, 5)
            attended(FIX, 1)
            att_shifts(FIX, 1)
            x4_sums(FIX, 1)
            x4_shifts(FIX, 1)


_INS = ["x", "src", "dst", "edge_attr_64", "L0_gnn_W", "L0_gnn_b", "L1_gnn_kernel", "L1_gnn_kernel_attention",
        "L2_gnn_W1l", "L2_gnn_b1", "L2_gnn_W1r", "L2_gnn_W2l", "L2_gnn_b2", "L2_gnn_W2r", "L3_gnn_qw", "L3_gnn_kw",
        "L3_gnn_ln_gamma", "L3_gnn_ln_beta", "L3_gnn_out_w", "L3_gnn_out_b"]


def kernel(**inputs):
    import numpy as _np
    import concourse.bacc as _bacc
    from concourse import mybir as _mybir
    from concourse.bass_utils import run_bass_kernel_spmd as _run

    nc = _bacc.Bacc("TRN2", target_bir_lowering=False, num_devices=1)
    arrays, args = {}, []
    for name in _INS:
        a = _np.ascontiguousarray(inputs[name])
        arrays[f"in_{name}_dram"] = a
        args.append(nc.dram_tensor(f"in_{name}_dram", a.shape, _mybir.dt.from_np(a.dtype), kind="ExternalInput").ap())
    out = nc.dram_tensor("out_0_dram", (N_NODES, F), _mybir.dt.float32, kind="ExternalOutput").ap()
    gnn_program(nc, *args, out)
    r = _run(nc, [arrays], core_ids=[0])
    return r.results[0]["out_0_dram"]
```

```python
import concourse.bass as bass
from concourse import mybir
from contextlib import ExitStack

P = 128
F = 128
FE = 64
N_NODES = 50000
N_EDGES = 25000
EP = 125
T = N_EDGES // EP
SLOTS = P * T
J = 4
STEPS = T // J
DJ = 8
DENSE_FULL = N_NODES // (P * DJ)
TAIL_P = (N_NODES - DENSE_FULL * P * DJ) // DJ
DENSE_STEPS = DENSE_FULL + 1
MAP_P = 125
HEADS, HID = 4, 32
EPS = 1e-5
FAR = 1 << 20
PAD_NODE = 65535
LOW = 1e30
DOUBLINGS = [1, 2, 4, 8, 16, 32, 64, 128]

assert EP * T == N_EDGES and T % J == 0 and DENSE_FULL * P * DJ + TAIL_P * DJ == N_NODES


class Step:

    def __init__(self, k, b):
        self.k, self.b = k, b

    def first_use(self):
        return isinstance(self.k, int) and self.k == 0

    def index(self):
        return 2 * self.k + self.b


class Back(Step):

    def index(self):
        return (2 * self.k + self.b) * -1 + (STEPS - 1)


def back(g):
    return Back(g.k, g.b)


class Signal:

    def __init__(self, sem, base, per):
        self.sem, self.base, self.per = sem, base, per

    def at(self, steps):
        return self.base + self.per * steps


class Ring:

    def __init__(self, sems, base, n, steps):
        self.sems, self.base, self.n = sems, base, n
        self.end = [base[0] + 16 * n * ((steps + 1) // 2), base[1] + 16 * n * (steps // 2)]


def wait_done(eng, signal, g):
    eng.wait_ge(signal.sem, signal.per * g.index() + (signal.base + signal.per))


def wait_part(eng, signal, g, part):
    eng.wait_ge(signal.sem, signal.per * g.index() + (signal.base + part))


def wait_free(eng, signal, g):
    if not g.first_use():
        eng.wait_ge(signal.sem, signal.per * g.index() + (signal.base - signal.per))
    elif signal.base:
        eng.wait_ge(signal.sem, signal.base)


def wait_previous(eng, signal, g):
    if not (isinstance(g.k, int) and g.index() == 0 and signal.base == 0):
        eng.wait_ge(signal.sem, signal.per * g.index() + signal.base)


def wait_landed(eng, ring, g):
    eng.wait_ge(ring.sems[g.b], 16 * ring.n * g.k + (ring.base[g.b] + 16 * ring.n))


def wait_drained(eng, ring, g):
    if not g.first_use() or ring.base[g.b]:
        eng.wait_ge(ring.sems[g.b], 16 * ring.n * g.k + ring.base[g.b])


def wait_all(eng, ring):
    for b in range(2):
        eng.wait_ge(ring.sems[b], ring.end[b])


def settle(eng):
    eng.nop(nofuse=True)


def pipeline(eng, looped, stages):
    longest = max(lag for lag, _, _ in stages)

    def at(s):
        for lag, stage, count in stages:
            if 0 <= s - lag < count:
                stage(Step((s - lag) // 2, (s - lag) % 2))

    first = (longest + 3) // 2 * 2
    loops = (looped - first) // 2
    for s in range(first):
        at(s)
    with eng.Fori(0, loops) as i:
        for h in range(2):
            for lag, stage, _ in stages:
                stage(Step(i + (first + h - lag) // 2, (h - lag) % 2))
    for s in range(first + 2 * loops, max(lag + count for lag, _, count in stages)):
        at(s)


def edges(*stages):
    return [(lag, stage, STEPS) for lag, stage in stages]


def nodes(lag, stage):
    return (lag, stage, DENSE_STEPS)


def gnn_program(nc, x, src, dst, edge_attr, w0, b0, w_gat, att, w1l, b1, w1r, w2l, b2, w2r,
                qw, kw, gamma, beta, out_w, out_b, out):
    fp32 = mybir.dt.float32
    bf16 = mybir.dt.bfloat16
    i32 = mybir.dt.int32
    ALU = mybir.AluOpType
    ACT = mybir.ActivationFunctionType
    AX = mybir.AxisListType.X

    ctx = ExitStack()
    with ctx:
        def sb(name, shape, dt=fp32):
            return ctx.enter_context(nc.sbuf_tensor(name, shape, dt))

        def sem(name):
            return ctx.enter_context(nc.semaphore(name))

        def sem2(name):
            return [sem(f"{name}{b}") for b in range(2)]

        def table(name, rows):
            return nc.dram_tensor(name, (rows, F), fp32, kind="Internal").ap()

        x1_table, x2_table, h1_table, x3_table = (table(f"{n}_table", SLOTS + N_NODES) for n in ("x1", "x2", "h1", "x3"))
        y_nodes = table("y_nodes", N_NODES)
        q_rows = table("q_rows", SLOTS)
        ACC_W = F + HEADS
        gat_sums = nc.dram_tensor("gat_sums", (DENSE_STEPS * P * DJ + J * P, ACC_W), fp32, kind="Internal").ap()
        acc_dump = nc.dram_tensor("acc_dump", (SLOTS, ACC_W), fp32, kind="Internal").ap()
        node_map = nc.dram_tensor("node_map", (N_NODES, 1), i32, kind="Internal").ap()

        def slot_rows(tab, g):
            v = tab[0:SLOTS, :].rearrange("(p t) f -> p (t f)", p=P)
            return v[:, bass.ds(g.index() * (J * F), J * F)]

        def acc_rows(g):
            v = acc_dump.rearrange("(p t) f -> p (t f)", p=P)
            return v[:, bass.ds(g.index() * (J * ACC_W), J * ACC_W)]

        def is_tail(g):
            return isinstance(g.k, int) and g.index() == DENSE_FULL

        def dense_p(g):
            return TAIL_P if is_tail(g) else P

        def node_rows(tab, base, g):
            pn = dense_p(g)
            rows = tab[bass.ds(g.index() * (P * DJ) + base, pn * DJ), :]
            return rows.rearrange("(p j) f -> p j f", p=pn)

        def sums_rows(g):
            rows = gat_sums[bass.ds(g.index() * (P * DJ), P * DJ), :]
            return rows.rearrange("(p j) f -> p (j f)", p=P)

        ident = sb("ident", [P, P])
        ones = sb("ones", [P, P])
        upper = sb("upper", [P, P])
        lower = sb("lower", [P, P])
        w0_sb = sb("w0_sb", [P, 2 * F + FE])
        natural = {n: sb(f"{n}_sb", [P, F]) for n in ("w_gat", "w1l", "w1r", "w2l", "w2r")}
        w0s_t, w0d_t, wgat_t, w1l_t, w1r_t, w2l_t, w2r_t = (sb(n, [P, F]) for n in ("w0s_t", "w0d_t", "wgat_t", "w1l_t", "w1r_t", "w2l_t", "w2r_t"))
        w0e_t = sb("w0e_t", [FE + 1, F])
        qw_sb, kw_sb = sb("qw_sb", [P, HEADS, HID]), sb("kw_sb", [P, HEADS, HID])
        outw_sb = sb("outw_sb", [P, F])
        outb_bc = sb("outb_bc", [P, F])
        bias_rows = sb("bias_rows", [3, 2, F])
        bias_hi, bias_mid, bias_lo = (sb(n, [3, 2, F], bf16) for n in ("bias_hi", "bias_mid", "bias_lo"))
        b2_parts, outb_parts = sb("b2_parts", [3, J, F], bf16), sb("outb_parts", [3, J, F], bf16)
        ones_bf = sb("ones_bf", [3, P], bf16)
        cols = sb("cols", [P, 8])
        b1_col, gamma_col, beta_col, adst_col, asrc_col, sbeta_col = (cols[:, i:i + 1] for i in range(6))
        col_bc = sb("col_bc", [P, 3, P])
        vdst_bc, vsrc_bc, local3_bc = sb("vdst_bc", [P, F]), sb("vsrc_bc", [P, F]), sb("local3_bc", [P, F])

        dst_i = sb("dst_i", [P, T + 2], i32)
        d = sb("d", [P, T + 2])
        src_i = sb("src_i", [P, T], i32)
        dst_safe_i = sb("dst_safe_i", [P, T], i32)
        table_index = sb("table_index", [P, T], i32)
        map_index = sb("map_index", [P, T], i32)
        out_index = sb("out_index", [P, T], i32)
        slot_i = sb("slot_i", [P, T], i32)
        slot = sb("slot", [P, T])
        keep, canon, in_first, first_done = (sb(n, [P, T]) for n in ("keep", "canon", "in_first", "first_done"))
        canon_inner = sb("canon_inner", [P, T])
        undone = sb("undone", [P, T])
        apart = sb("apart", [P, len(DOUBLINGS), T])
        tmp_t = sb("tmp_t", [P, T])
        source_key = sb("source_key", [P, T])
        dummy_row = sb("dummy_row", [P, 2])
        dummy_rows = sb("dummy_rows", [P, J])
        alpha = sb("alpha", [P, T, HEADS])
        seg_max = sb("seg_max", [P, T, HEADS])
        tmp_a = sb("tmp_a", [P, T, HEADS])
        neg_half = sb("neg_half", [P, J])
        one_p = sb("one_p", [P, 2])
        has_first, fix_slot = (one_p[:, i:i + 1] for i in range(2))
        fix_idx = sb("fix_idx", [P, 4], i32)
        fix_read, fix_write, fix_out, fix_node = (fix_idx[:, i:i + 1] for i in range(4))
        fix_skip = sb("fix_skip", [P, 1])
        diag = sb("diag", [P, 2 + 2 * HEADS, P])
        sum_carry = sb("sum_carry", [P, P])
        back_carry = sb("back_carry", [P, P])
        max_pen = sb("max_pen", [P, 4, P])
        max_row = sb("max_row", [P, 2, HEADS, P])
        max_extra = sb("max_extra", [P, 4, HEADS])

        def ring(name, width=F, dt=fp32):
            return sb(name, [P, 2, J, width], dt)

        def dense_ring(name, width=F):
            return sb(name, [P, 2, DJ, width])

        zeros = sb("zeros", [P, DJ * ACC_W])
        node_in, node_sums, node_out, node_h1, node_y = (dense_ring(f"node_{n}", w) for n, w in (
            ("in", F), ("sums", ACC_W), ("out", F), ("h1", F), ("y", F)))
        node_x2t, node_h1t = sb("node_x2t", [P, 2, DJ * F]), sb("node_h1t", [P, 2, DJ * F])
        node_recip = sb("node_recip", [P, 2, 2, DJ])
        src_rows = ring("src_rows", ACC_W)
        own_rows, own2_rows, ny = ring("own_rows"), ring("own2_rows"), ring("att_pre")
        ea_rows = ring("ea_rows", FE)
        msg = ring("msg", ACC_W)
        acc = ring("acc", ACC_W)
        gate = ring("gate")
        bc = ring("bc")
        pre = ring("pre")
        new_rows = ring("new_rows")
        same = [t[:, :, :, :].rearrange("p b j f -> p (b j f)").rearrange("p (j i) -> p j i", j=J) for t in (node_h1, node_y)]
        junk2 = node_x2t[:, :, :].rearrange("p b c -> p (b c)").rearrange("p (j i) -> p j i", j=J)
        same_bf = sb("same_bf", [P, 2, J, J * P], bf16)
        w_parts = sb("w_parts", [P, 2, 3, J], bf16)
        w_left = sb("w_left", [P, 2, 2, J])
        earlier = sb("earlier", [P, (J - 1) * P + P])
        sums = ring("sums", ACC_W)
        key4 = sb("key4", [P, 2, 5, J])
        add_idx = sb("add_idx", [P, 2, J], i32)
        junk = sb("junk", [P, 2, J, F])
        t_a, t_b, t_c = (sb(n, [P, 2, J * F]) for n in ("t_a", "t_b", "t_c"))
        t_e = sb("t_e", [FE + 1, 2, J * P])
        NORM = {k: (sb(f"{k}_stats", [P, 2, n, 6]), sb(f"{k}_moments", [P, 2, n, 2]), sb(f"{k}_root", [P, 2, n]),
                    sb(f"{k}_shift", [P, 2, n])) for k, n in (("e", J), ("a", J), ("n", DJ))}
        edge4 = sb("edge4", [P, 2, 6, J])
        recip = sb("recip", [P, 2, J, HEADS])
        out_stage = sb("out_stage", [P, 2, J], i32)
        idx_stage = sb("idx_stage", [P, 2, 2, J], i32)
        val_stage = sb("val_stage", [P, 2, J], i32)
        map_init = sb("map_init", [MAP_P, N_NODES // MAP_P], i32)
        open_row = sb("open_row", [P, F])
        fix_acc = sb("fix_acc", [P, ACC_W])

        ps = [[ctx.enter_context(nc.psum_tensor(f"ps{i}{b}", [P, J * F], fp32)) for b in range(2)] for i in range(4)]

        weights_in, cols_in, dst_in, src_in = sem("weights_in"), sem("cols_in"), sem("dst_in"), sem("src_in")
        consts_made, dst_set, slots_made = sem("consts_made"), sem("dst_set"), sem("slots_made")
        pe_prep, dve_prep, act_prep = sem("pe_prep"), sem("dve_prep"), sem("act_prep")
        map_start, map_index_made, slots_set, apart_made = (sem(n) for n in ("map_start", "map_index_made", "slots_set", "apart_made"))
        carried, max_at, fix_in, fix_out_sem = (sem(n) for n in ("carried", "max_at", "fix_in", "fix_out_sem"))
        opened = sem("opened")
        fix_ready, dummies_zero = sem("fix_ready"), sem("dummies_zero")

        PER = {"accd": J, "spread": J}

        def norm(k, inverted=True):
            return [f"{k}_{n}" for n in ("bn", "ag", "ve", "rt", "nm")] + [f"{k}_rc"] * inverted

        LAYERS = {
            "map": dict(front=["idxd", "idx2", "mapd"], rings=dict(marked=J, mapped=J)),
            "nodes1": dict(front=norm("n") + ["n_row"], rings=dict(n_in=1, n_out=1, n_zero=1), steps=DENSE_STEPS),
            "msg": dict(front=["idxd", "tr_a", "cp_a", "tr_b", "cp_b", "tr_e", "cp_e", "mm", "sig", "msg0", "msgd"],
                        back=["accd", "pre", "newd", "e_cn"] + norm("e", False),
                        rings=dict(gathered=2 * J, eain=2, dumped=1, stored=1)),
            "gat": dict(front=["idxd", "score", "e0", "e1", "e2", "expd", "msgd", "keyd", "bcd", "tr_a", "samed", "rep0", "rep1",
                               "rep2", "rep3", "mm", "cp_a", "mm2", "cp_b", "w_hi", "w_r1", "w_mid", "w_r2", "w_lo", "same_bf",
                               "spread"],
                        rings=dict(gathered=J, own=1), parts=dict(added=16 * J)),
            "x2": dict(front=["idxd", "rcs", "rc0", "rc1", "pre", "newd"] + norm("e"), rings=dict(gathered=J, own=1, stored=1)),
            "nodes2": dict(front=["n_rcs", "n_rc0", "n_rc1", "n_pre", "x2tp", "x2tc", "h1p", "h1tc", "h1tp", "h1c", "yp", "y", "n_row"] + norm("n"),
                           rings=dict(n_in=2, n_out=1, n_h1=1, n_y=1), steps=DENSE_STEPS),
            "sage1": dict(front=["idxd"], back=["accd", "rcp", "msgd", "tr_a", "cp_a", "tr_b", "cp_b", "mm", "cp_c", "mm2", "newd"],
                          rings=dict(gathered=J, own=1, dumped=1, stored=1)),
            "nodes3": dict(front=norm("n") + ["n_row"], rings=dict(n_in=1, n_out=1), steps=DENSE_STEPS),
            "sage2": dict(front=["idxd"], back=["accd", "rcp", "msgd", "tr_a", "cp_a", "tr_b", "cp_b", "mm", "pre", "newd", "e_cn"] + norm("e"),
                          rings=dict(gathered=J, own=1, own2=1, dumped=1, stored=1)),
            "att1": dict(front=["idxd", "spread", "tr_a", "cp_a", "tr_b", "cp_b", "mm", "mm2", "newd", "cp_c", "pre", "score"],
                         rings=dict(gathered=J, own=1, stored=1)),
            "nodes4": dict(front=norm("n") + ["n_pre", "n_row"], rings=dict(n_in=1, n_out=1), steps=DENSE_STEPS),
            "att2": dict(front=["idxd", "msgd"],
                         back=["accd", "rcp", "rcp2", "pre", "msg0", "tr_a", "cp_a", "mm", "pre2", "newd"]
                         + norm("e", False) + norm("a", False),
                         rings=dict(qin=1, own=1, dumped=1, scattered=J)),
        }
        sems, counts, flow = {}, {}, {}
        for layer, use in LAYERS.items():
            flow[layer] = {}
            steps = use.get("steps", STEPS)
            for kind, total in (("front", steps), ("back", steps + 1)):
                for n in use.get(kind, []):
                    if n not in sems:
                        sems[n], counts[n] = sem(n), 0
                    per = PER.get(n, 1)
                    flow[layer][n] = Signal(sems[n], counts[n], per)
                    counts[n] += per * total
            for n, m in use["rings"].items():
                if n not in sems:
                    sems[n], counts[n] = sem2(n), [0, 0]
                flow[layer][n] = Ring(sems[n], counts[n], m, steps)
                counts[n] = flow[layer][n].end
            for n, per in use.get("parts", {}).items():
                flow[layer][n] = Signal(sem(n), 0, per)
        LAYER_NO = {n: i for i, n in enumerate(("msg", "sage1", "sage2", "att2"))}
        FIX = Step(STEPS // 2, 0)

        block = ctx.enter_context(nc.Block())

        def fours(ap, g):
            return ap[:, bass.ds(g.index() * J, J)]

        @block.sync
        def _(sp):
            sp.wait_ge(dst_set, 1)
            by_p = dst.rearrange("(p t) -> p t", t=T)
            sp.dma_start(dst_i[0:EP, 1:T + 1], by_p).then_inc(dst_in, 16)
            with nc.allow_non_contiguous_dma(reason="one value a partition"):
                sp.dma_start(dst_i[1:EP, 0:1], by_p[0:EP - 1, T - 1:T]).then_inc(dst_in, 16)
                sp.dma_start(dst_i[0:EP - 1, T + 1:T + 2], by_p[1:EP, 0:1]).then_inc(dst_in, 16)
            sp.dma_start(src_i[0:EP, :], src.rearrange("(p t) -> p t", t=T)).then_inc(src_in, 16)
            sp.dma_start(w0_sb[:, :], w0).then_inc(weights_in, 16)
            for n, a in (("w_gat", w_gat), ("w1l", w1l), ("w1r", w1r), ("w2l", w2l), ("w2r", w2r)):
                sp.dma_start(natural[n][:, :], a).then_inc(weights_in, 16)
            sp.dma_start(outw_sb[:, :], out_w).then_inc(weights_in, 16)
            sp.dma_start(w0e_t[FE:FE + 1, :], b0.rearrange("(a n) -> a n", a=1)).then_inc(weights_in, 16)
            sp.dma_start(qw_sb[:, :, :], qw.rearrange("h f d -> f h d")).then_inc(weights_in, 16)
            sp.dma_start(kw_sb[:, :, :], kw.rearrange("h f d -> f h d")).then_inc(weights_in, 16)
            sp.dma_start(bias_rows[:, 0, :], b2.partition_broadcast(3)).then_inc(weights_in, 16)
            sp.dma_start(bias_rows[:, 1, :], out_b.partition_broadcast(3)).then_inc(weights_in, 16)
            sp.dma_start(outb_bc[:, :], out_b.partition_broadcast(P)).then_inc(weights_in, 16)
            with nc.allow_non_contiguous_dma(reason="one value a partition"):
                for i, a in enumerate((b1, gamma, beta)):
                    sp.dma_start(cols[:, i:i + 1], a.rearrange("(n a) -> n a", a=1)).then_inc(cols_in, 16)
                sp.dma_start(cols[:, 3:4], att[0:F, :]).then_inc(cols_in, 16)
                sp.dma_start(cols[:, 4:5], att[F:2 * F, :]).then_inc(cols_in, 16)

            def dump_and_store(L, tab):
                def dump(g):
                    wait_done(sp, L["accd"], g)
                    sp.dma_start(acc_rows(g), acc[:, g.b, :, :]).then_inc(L["dumped"].sems[g.b], 16)

                def store(g):
                    wait_done(sp, L["newd"], g)
                    sp.dma_start(slot_rows(tab, g), new_rows[:, g.b, :, :]).then_inc(L["stored"].sems[g.b], 16)

                return dump, store

            def load_nodes(D, tab, base, used):
                def load(g):
                    wait_free(sp, D[used], g)
                    sp.dma_start(node_in[0:dense_p(g), g.b, :, :], node_rows(tab, base, g)).then_inc(D["n_in"].sems[g.b], 16)
                return load

            def store_nodes(D, tab, base):
                def store(g):
                    wait_done(sp, D["n_row"], g)
                    sp.dma_start(node_rows(tab, base, g), node_out[0:dense_p(g), g.b, :, :]).then_inc(D["n_out"].sems[g.b], 16)
                return store

            D = flow["nodes1"]

            def zero_sums(g):
                wait_drained(sp, D["n_zero"], g)
                sp.dma_start(sums_rows(g), zeros[:, :]).then_inc(D["n_zero"].sems[g.b], 16)

            sp.wait_ge(consts_made, 3)
            sp.dma_start(gat_sums[DENSE_STEPS * P * DJ:, :].rearrange("(p j) f -> p (j f)", p=P), zeros[:, 0:J * ACC_W])\
                .then_inc(dummies_zero, 16)
            pipeline(sp, DENSE_FULL, [nodes(2, store_nodes(D, x1_table, SLOTS)), nodes(0, load_nodes(D, x, 0, "n_row")), nodes(0, zero_sums)])

            L = flow["msg"]
            ea_v = edge_attr.rearrange("(p t) f -> p (t f)", p=EP)

            def load_ea(g):
                wait_free(sp, L["tr_e"], g)
                for lo, hi in ((0, 112), (112, EP)):
                    sp.dma_start(ea_rows[lo:hi, g.b, :, :],
                                 ea_v[lo:hi, bass.ds(g.index() * (J * FE), J * FE)]).then_inc(L["eain"].sems[g.b], 16)

            dump, store = dump_and_store(L, x1_table)
            pipeline(sp, STEPS, edges((0, load_ea), (1, dump), (4, store)))

            def load_own(L, signal, tab, to, ring):
                def load(g):
                    wait_free(sp, signal, g)
                    sp.dma_start(to[:, g.b, :, :], slot_rows(tab, g)).then_inc(ring.sems[g.b], 16)
                return load

            L = flow["gat"]
            wait_all(sp, flow["msg"]["stored"])
            sp.wait_ge(fix_out_sem, 16 * 1)

            def load_own_back(L, tab, to):
                def load(g):
                    wait_free(sp, L["spread"], g)
                    sp.dma_start(to[:, g.b, :, :], slot_rows(tab, back(g))).then_inc(L["own"].sems[g.b], 16)
                return load

            pipeline(sp, STEPS, edges((0, load_own_back(L, x1_table, own2_rows))))
            L, D = flow["x2"], flow["nodes2"]
            wait_all(sp, flow["nodes1"]["n_out"])
            sp.wait_ge(flow["gat"]["added"].sem, flow["gat"]["added"].at(STEPS))
            load_x1 = load_nodes(D, x1_table, SLOTS, "n_row")

            def load_x1_sums(g):
                wait_free(sp, D["n_pre"], g)
                sp.dma_start(node_sums[0:dense_p(g), g.b, :, :], node_rows(gat_sums, 0, g)).then_inc(D["n_in"].sems[g.b], 16)
                load_x1(g)

            def store_h1(g):
                wait_done(sp, D["h1c"], g)
                sp.dma_start(node_rows(h1_table, SLOTS, g), node_h1[0:dense_p(g), g.b, :, :]).then_inc(D["n_h1"].sems[g.b], 16)

            def store_y(g):
                wait_done(sp, D["y"], g)
                sp.dma_start(node_rows(y_nodes, 0, g), node_y[0:dense_p(g), g.b, :, :]).then_inc(D["n_y"].sems[g.b], 16)

            _, store = dump_and_store(L, x2_table)
            pipeline(sp, DENSE_FULL, [nodes(5, store_h1), nodes(5, store_y), nodes(3, store_nodes(D, x2_table, SLOTS))]
                     + edges((3, store), (0, load_own(L, L["pre"], x1_table, own_rows, L["own"]))) + [nodes(0, load_x1_sums)])

            L, D = flow["sage1"], flow["nodes3"]
            wait_all(sp, flow["x2"]["stored"])
            wait_all(sp, flow["nodes2"]["n_out"])
            wait_all(sp, flow["nodes2"]["n_y"])
            dump, store = dump_and_store(L, h1_table)
            pipeline(sp, DENSE_FULL, edges((0, load_own(L, L["tr_b"], x2_table, own_rows, L["own"])))
                     + [nodes(0, load_nodes(D, y_nodes, 0, "n_row"))] + edges((1, dump))
                     + [nodes(2, store_nodes(D, x3_table, SLOTS))] + edges((3, store)))
            L = flow["sage2"]
            wait_all(sp, flow["sage1"]["stored"])
            sp.wait_ge(fix_out_sem, 16 * 2)
            dump, store = dump_and_store(L, x3_table)
            h1_own = load_own(L, L["tr_b"], h1_table, own_rows, L["own"])
            x2_own = load_own(L, L["pre"], x2_table, own2_rows, L["own2"])

            def both(g):
                h1_own(g)
                x2_own(g)

            pipeline(sp, STEPS, edges((0, both), (1, dump), (4, store)))
            L, D = flow["att1"], flow["nodes4"]
            wait_all(sp, flow["nodes3"]["n_out"])
            wait_all(sp, flow["sage2"]["stored"])
            sp.wait_ge(fix_out_sem, 16 * 3)

            def store_q(g):
                wait_done(sp, L["newd"], g)
                sp.dma_start(slot_rows(q_rows, back(g)), new_rows[:, g.b, :, :]).then_inc(L["stored"].sems[g.b], 16)

            pipeline(sp, DENSE_FULL, edges((0, load_own_back(L, x3_table, own_rows))) + [nodes(0, load_nodes(D, x3_table, SLOTS, "n_row"))]
                     + edges((2, store_q)) + [nodes(2, store_nodes(D, out, 0))])
            L = flow["att2"]
            wait_all(sp, flow["att1"]["stored"])

            def load_q(g):
                wait_free(sp, L["msgd"], g)
                sp.dma_start(src_rows[:, g.b, :, 0:F], slot_rows(q_rows, g).rearrange("p (j f) -> p j f", f=F))\
                    .then_inc(L["qin"].sems[g.b], 16)

            dump, _ = dump_and_store(L, None)
            pipeline(sp, STEPS, edges((0, load_q), (1, dump), (3, load_own(L, L["pre2"], x3_table, own_rows, L["own"]))))
            sp.wait_ge(fix_out_sem, 16 * 4)
            wait_all(sp, L["scattered"])

        @block.gpsimd
        def _(pool):
            g_ = nc.gpsimd
            g_.memset(dst_i[:, :], PAD_NODE)
            g_.memset(src_i[:, :], 0)
            g_.memset(ident[:, :], 0.0)
            g_.memset(ones[:, :], 1.0)
            g_.memset(upper[:, :], 1.0)
            g_.memset(neg_half[:, :], -0.5)
            g_.memset(lower[:, :], 1.0).then_inc(consts_made, 1)
            pool.wait_ge(consts_made, 1)
            g_.memset(dst_i[:, 0:1], -1)
            g_.memset(dst_i[:, T + 1:T + 2], -1).then_inc(dst_set, 1)
            g_.affine_select(out=ident[:, :], in_=ident[:, :], compare_op=ALU.not_equal, fill=1.0, base=0,
                             pattern=[[-1, P]], channel_multiplier=1)
            g_.affine_select(out=upper[:, :], in_=upper[:, :], compare_op=ALU.is_gt, fill=0.0, base=0,
                             pattern=[[1, P]], channel_multiplier=-1)
            g_.affine_select(out=lower[:, :], in_=lower[:, :], compare_op=ALU.is_gt, fill=0.0, base=0,
                             pattern=[[-1, P]], channel_multiplier=1)
            g_.iota(slot_i[:, :], pattern=[[1, T]], base=0, channel_multiplier=T)
            g_.iota(map_init[:, :], pattern=[[1, N_NODES // MAP_P]], base=SLOTS, channel_multiplier=N_NODES // MAP_P)
            g_.memset(src_rows[:, :, :, :], 0.0)
            g_.memset(msg[:, :, :, :], 0.0)
            g_.memset(acc[:, :, :, :], 0.0)
            g_.memset(zeros[:, :], 0.0)
            g_.memset(sums[:, :, :, :], 0.0)
            g_.iota(dummy_rows[:, :], pattern=[[P, J]], base=DENSE_STEPS * P * DJ, channel_multiplier=1,
                    allow_small_or_imprecise_dtypes=True)
            g_.iota(dummy_row[:, 0:1], pattern=[[0, 1]], base=N_NODES, channel_multiplier=1,
                    allow_small_or_imprecise_dtypes=True)
            g_.memset(ea_rows[:, :, :, :], 0.0).then_inc(consts_made, 1)
            pool.wait_ge(consts_made, 2)
            g_.memset(src_rows[:, :, :, F:F + 1], 1.0).then_inc(consts_made, 1)

            def mark_and_look_up():
                pool.dma_start(node_map.rearrange("(p t) a -> p (t a)", p=MAP_P), map_init[:, :]).then_inc(map_start, 16)
                pool.wait_ge(map_start, 16)
                L = flow["map"]
                pool.wait_ge(map_index_made, 1)

                def mark(g):
                    wait_drained(pool, L["marked"], g)
                    g_.tensor_copy(idx_stage[:, g.b, 0, :], fours(map_index, g))
                    g_.tensor_copy(val_stage[:, g.b, :], fours(slot_i, g)).then_inc(L["idxd"].sem, 1)
                    wait_done(pool, L["idxd"], g)
                    settle(pool)
                    for j in range(J):
                        g_.indirect_dma_start(
                            out=node_map[:, :], out_offset=bass.IndirectOffsetOnAxis(ap=idx_stage[:, g.b, 0, j:j + 1], axis=0),
                            in_=val_stage[:, g.b, j:j + 1], in_offset=None,
                            bounds_check=N_NODES - 1, oob_is_err=False).then_inc(L["marked"].sems[g.b], 16)

                pipeline(pool, STEPS, edges((0, mark)))
                wait_all(pool, L["marked"])

                def look_up(g):
                    wait_free(pool, L["mapd"], g)
                    g_.tensor_copy(idx_stage[:, g.b, 1, :], fours(src_i, g)).then_inc(L["idx2"].sem, 1)
                    wait_done(pool, L["idx2"], g)
                    settle(pool)
                    for j in range(J):
                        g_.indirect_dma_start(
                            out=val_stage[:, g.b, j:j + 1], out_offset=None, in_=node_map[:, :],
                            in_offset=bass.IndirectOffsetOnAxis(ap=idx_stage[:, g.b, 1, j:j + 1], axis=0))\
                            .then_inc(L["mapped"].sems[g.b], 16)

                def keep_looked_up(g):
                    wait_landed(pool, L["mapped"], g)
                    g_.tensor_copy(fours(table_index, g), val_stage[:, g.b, :]).then_inc(L["mapd"].sem, 1)

                pipeline(pool, STEPS, edges((0, look_up), (1, keep_looked_up)))
                pool.wait_ge(L["mapd"].sem, L["mapd"].at(STEPS))

            def inverse_root(L, k):
                def root(g, jn=J):
                    wait_done(pool, L[f"{k}_ve"], g)
                    at = NORM[k][2][:, g.b, 0:jn]
                    g_.tensor_tensor(at, at, neg_half[:, 0:jn], ALU.pow).then_inc(L[f"{k}_rt"].sem, 1)
                return root

            def stage_indices(L, g, arrays, order=lambda g: g):
                for i, a in enumerate(arrays):
                    last = g_.tensor_copy(idx_stage[:, g.b, i, :], fours(a, order(g)))
                last.then_inc(L["idxd"].sem, 1)
                wait_done(pool, L["idxd"], g)
                settle(pool)

            def gather(L, g, i, tab, to, width=F):
                for j in range(J):
                    g_.indirect_dma_start(
                        out=to[:, g.b, j, 0:width], out_offset=None, in_=tab,
                        in_offset=bass.IndirectOffsetOnAxis(ap=idx_stage[:, g.b, i, j:j + 1], axis=0))\
                        .then_inc(L["gathered"].sems[g.b], 16)

            def fix_gather(L, own, idx, own_used, more=()):
                n = LAYER_NO["att2" if L is flow["att2"] else next(k for k in flow if flow[k] is L)]
                wait_all(pool, L["dumped"])
                pool.wait_ge(own_used.sem, own_used.at(STEPS))
                g_.indirect_dma_start(out=fix_acc[:, :], out_offset=None, in_=acc_dump[:, :],
                                      in_offset=bass.IndirectOffsetOnAxis(ap=fix_read, axis=0)).then_inc(fix_in, 16)
                g_.indirect_dma_start(out=own_rows[:, 0, 0, :], out_offset=None, in_=own,
                                      in_offset=bass.IndirectOffsetOnAxis(ap=idx, axis=0)).then_inc(fix_in, 16)
                g_.indirect_dma_start(out=own2_rows[:, 0, 0, :], out_offset=None, in_=more[0] if more else own,
                                      in_offset=bass.IndirectOffsetOnAxis(ap=idx, axis=0)).then_inc(fix_in, 16)
                pool.wait_ge(fix_in, 48 * (n + 1))
                return n

            def fix_scatter(L, tab, idx, rows, n, out_ring="stored"):
                wait_all(pool, L[out_ring])
                pool.wait_ge(L["newd"].sem, L["newd"].at(STEPS + 1))
                g_.indirect_dma_start(out=tab, out_offset=bass.IndirectOffsetOnAxis(ap=idx, axis=0),
                                      in_=new_rows[:, 0, 0, :], in_offset=None,
                                      bounds_check=rows - 1, oob_is_err=False).then_inc(fix_out_sem, 16)
                pool.wait_ge(fix_out_sem, 16 * (n + 1))

            mark_and_look_up()
            pool.wait_ge(slots_set, 1)
            L = flow["msg"]

            def gather_ends(g):
                wait_free(pool, L["tr_b"], g)
                stage_indices(L, g, (src_i, dst_safe_i))
                gather(L, g, 0, x[:, :], src_rows)
                wait_free(pool, L["pre"], g)
                settle(pool)
                gather(L, g, 1, x[:, :], own_rows)

            def scatter_rows(L, tab, stage):
                def scatter(g):
                    wait_drained(pool, L["scattered"], g)
                    g_.tensor_copy(out_stage[:, g.b, :], fours(out_index, g)).then_inc(L[stage].sem, 1)
                    wait_done(pool, L[stage], g)
                    wait_done(pool, L["newd"], g)
                    settle(pool)
                    for j in range(J):
                        g_.indirect_dma_start(
                            out=tab, out_offset=bass.IndirectOffsetOnAxis(ap=out_stage[:, g.b, j:j + 1], axis=0),
                            in_=new_rows[:, g.b, j, :], in_offset=None,
                            bounds_check=N_NODES - 1, oob_is_err=False).then_inc(L["scattered"].sems[g.b], 16)
                return scatter

            pipeline(pool, STEPS, edges((0, gather_ends), (2, inverse_root(L, "e"))))
            n = fix_gather(L, x[:, :], fix_node, L["pre"])
            inverse_root(L, "e")(FIX, 1)
            fix_scatter(L, x1_table[:, :], fix_write, SLOTS, n)

            G = flow["gat"]
            wait_all(pool, flow["nodes1"]["n_out"])
            wait_all(pool, flow["nodes1"]["n_zero"])
            pool.wait_ge(dummies_zero, 16)

            def gather_x1(g):
                wait_free(pool, G["score"], g)
                stage_indices(G, g, (table_index,), back)
                gather(G, g, 0, x1_table[:, :], own_rows)

            def add_sums(g):
                wait_done(pool, G["cp_b"], g)
                wait_done(pool, G["rep2"], g)
                if not (isinstance(g.k, int) and g.index() == 0):
                    pool.wait_ge(G["added"].sem, G["added"].per * g.index())
                settle(pool)
                for j in range(J):
                    g_.indirect_dma_start(
                        out=gat_sums[:, :], out_offset=bass.IndirectOffsetOnAxis(ap=add_idx[:, g.b, j:j + 1], axis=0),
                        in_=sums[:, g.b, j, :], in_offset=None, compute_op=ALU.add).then_inc(G["added"].sem, 16)

            pipeline(pool, STEPS, edges((0, gather_x1), (3, add_sums)))

            L = flow["x2"]
            pool.wait_ge(G["added"].sem, G["added"].at(STEPS))

            def gather_sums(g):
                wait_free(pool, L["pre"], g)
                stage_indices(L, g, (dst_safe_i,))
                gather(L, g, 0, gat_sums[:, :], sums, ACC_W)

            pipeline(pool, STEPS, edges((0, gather_sums)))

            def gather_sources(L, tab):
                def gather_tab(g):
                    wait_free(pool, L["accd"], g)
                    stage_indices(L, g, (table_index,))
                    gather(L, g, 0, tab, src_rows)
                return gather_tab

            L = flow["sage1"]
            wait_all(pool, flow["x2"]["stored"])
            wait_all(pool, flow["nodes2"]["n_out"])
            pipeline(pool, STEPS, edges((0, gather_sources(L, x2_table[:, :]))))
            n = fix_gather(L, x2_table[:, :], fix_read, L["tr_b"])
            fix_scatter(L, h1_table[:, :], fix_write, SLOTS, n)
            L = flow["sage2"]
            wait_all(pool, flow["nodes2"]["n_h1"])
            pipeline(pool, STEPS, edges((0, gather_sources(L, h1_table[:, :]))))
            n = fix_gather(L, h1_table[:, :], fix_read, L["pre"], more=(x2_table[:, :],))
            fix_scatter(L, x3_table[:, :], fix_write, SLOTS, n)

            L = flow["att1"]
            wait_all(pool, flow["nodes3"]["n_out"])

            def gather_x3(g):
                wait_free(pool, L["tr_a"], g)
                stage_indices(L, g, (table_index,), back)
                gather(L, g, 0, x3_table[:, :], src_rows)

            pipeline(pool, STEPS, edges((0, gather_x3)))

            L = flow["att2"]
            wait_all(pool, flow["nodes4"]["n_out"])

            def scatter_rows(g):
                wait_drained(pool, L["scattered"], g)
                g_.tensor_copy(out_stage[:, g.b, :], fours(out_index, g)).then_inc(L["idxd"].sem, 1)
                wait_done(pool, L["idxd"], g)
                wait_done(pool, L["newd"], g)
                settle(pool)
                for j in range(J):
                    g_.indirect_dma_start(
                        out=out[:, :], out_offset=bass.IndirectOffsetOnAxis(ap=out_stage[:, g.b, j:j + 1], axis=0),
                        in_=new_rows[:, g.b, j, :], in_offset=None,
                        bounds_check=N_NODES - 1, oob_is_err=False).then_inc(L["scattered"].sems[g.b], 16)

            pipeline(pool, STEPS, edges((7, scatter_rows), (5, inverse_root(L, "a")), (1, inverse_root(L, "e"))))
            n = fix_gather(L, x3_table[:, :], fix_read, L["pre2"])
            inverse_root(L, "e")(FIX, 1)
            inverse_root(L, "a")(FIX, 1)
            fix_scatter(L, out[:, :], fix_out, N_NODES, n, "scattered")

        @block.tensor
        def _(pe):
            te = nc.tensor
            pe.wait_ge(consts_made, 3)
            pe.wait_ge(weights_in, 16 * 13)
            w0s, w0d, w0e = w0_sb[:, 0:F], w0_sb[:, F:2 * F], w0_sb[:, 2 * F:2 * F + FE]
            for i, w in enumerate((w0s, w0d, natural["w_gat"][:, :], natural["w1l"][:, :],
                                   natural["w1r"][:, :], natural["w2l"][:, :], natural["w2r"][:, :])):
                te.transpose(ps[i // 4][0][:, (i % 4) * F:(i % 4 + 1) * F], w, ident[:, :])
            te.transpose(ps[1][0][0:FE, 3 * F:4 * F], w0e, ident[:, :]).then_inc(pe_prep, 1)
            pe.wait_ge(fix_ready, 1)
            for i in range(2):
                last = te.matmul(ps[2][0][:, i * P:(i + 1) * P], ones[:, :], diag[:, i, :], start=True, stop=True)
            last.then_inc(pe_prep, 1)
            pe.wait_ge(fix_ready, 2)
            te.matmul(ps[3][0][:, 0:F], col_bc[:, 0, :], wgat_t[:, :], start=True, stop=True)
            te.matmul(ps[3][0][:, F:2 * F], col_bc[:, 1, :], wgat_t[:, :], start=True, stop=True)
            te.matmul(ps[3][0][:, 2 * F:3 * F], col_bc[:, 2, :], outw_sb[:, :], start=True, stop=True).then_inc(pe_prep, 1)
            pe.wait_ge(dve_prep, 1)

            def transpose_step(L, g, bank, rows, done, copied, jn=J):
                wait_free(pe, L[copied], g)
                for j in range(jn):
                    last = te.transpose(ps[bank][g.b][:, j * F:(j + 1) * F], rows[:, g.b, j, 0:F], ident[:, :])
                last.then_inc(L[done].sem, 1)

            def open_rows(L, times, used):
                pe.wait_ge(L["newd"].sem, L["newd"].at(STEPS + 1))
                if used:
                    pe.wait_ge(used.sem, used.at(STEPS + 1))
                te.matmul(ps[1][0][:, 0:F], back_carry[:, :], new_rows[:, 0, 0, :], start=True, stop=True).then_inc(opened, 1)
                pe.wait_ge(opened, times)

            def carry(L, width, used):
                pe.wait_ge(L["accd"].sem, L["accd"].at(STEPS))
                pe.wait_ge(used.sem, used.at(STEPS))
                te.matmul(ps[0][0][:, 0:width], sum_carry[:, :], acc[:, 1, J - 1, 0:width],
                          start=True, stop=True).then_inc(carried, 1)

            L = flow["msg"]

            def transpose_ends(g):
                wait_landed(pe, L["gathered"], g)
                transpose_step(L, g, 0, src_rows, "tr_a", "cp_a")
                transpose_step(L, g, 1, own_rows, "tr_b", "cp_b")
                wait_landed(pe, L["eain"], g)
                wait_free(pe, L["cp_e"], g)
                settle(pe)
                for j in range(J):
                    last = te.transpose(ps[2][g.b][0:FE, j * P:(j + 1) * P], ea_rows[:, g.b, j, :], ident[:, :])
                last.then_inc(L["tr_e"].sem, 1)

            def messages(g):
                wait_done(pe, L["cp_a"], g)
                wait_done(pe, L["cp_b"], g)
                wait_done(pe, L["cp_e"], g)
                wait_free(pe, L["msg0"], g)
                for j in range(J):
                    c = slice(j * F, (j + 1) * F)
                    te.matmul(ps[3][g.b][:, c], t_a[:, g.b, c], w0s_t[:, :], start=True, stop=False)
                    te.matmul(ps[3][g.b][:, c], t_b[:, g.b, c], w0d_t[:, :], start=False, stop=False)
                    last = te.matmul(ps[3][g.b][:, c], t_e[:, g.b, c], w0e_t[:, :], start=False, stop=True)
                last.then_inc(L["mm"].sem, 1)

            pipeline(pe, STEPS, edges((1, messages), (0, transpose_ends)))
            carry(L, F, L["cp_a"])
            pe.wait_ge(L["cp_b"].sem, L["cp_b"].at(STEPS))
            open_rows(L, 2, None)

            L = flow["gat"]

            def gat_keys(g):
                wait_done(pe, L["bcd"], g)
                transpose_step(L, g, 0, bc, "tr_a", "samed")

            def gat_tile_sums(g):
                wait_done(pe, L["samed"], g)
                wait_done(pe, L["msgd"], g)
                wait_free(pe, L["cp_a"], g)
                for j in reversed(range(J)):
                    n = (j + 1) * P
                    te.matmul(ps[2][g.b][:, 0:n], msg[:, g.b, j, 0:F], same[g.b][:, j, 0:n], start=j == J - 1, stop=j == 0)
                wait_free(pe, L["cp_b"], g)
                wait_done(pe, L["w_lo"], g)
                wait_done(pe, L["same_bf"], g)
                settle(pe)
                for i in range(J):
                    for j in range(i, J):
                        last = te.matmul(ps[1][g.b][:, 3 * i:3 * i + 3], same_bf[:, g.b, j, i * P:(i + 1) * P], w_parts[:, g.b, :, j],
                                         start=j == i, stop=j == J - 1)
                last.then_inc(L["mm"].sem, 1)

            def gat_project(g):
                wait_done(pe, L["cp_a"], g)
                wait_free(pe, L["cp_b"], g)
                for j in range(J):
                    c = slice(j * F, (j + 1) * F)
                    last = te.matmul(ps[3][g.b][:, c], t_c[:, g.b, c], natural["w_gat"][:, :], start=True, stop=True)
                last.then_inc(L["mm2"].sem, 1)

            pipeline(pe, STEPS, edges((2, gat_project), (1, gat_tile_sums), (0, gat_keys)))
            for n in ("samed", "cp_a", "cp_b"):
                pe.wait_ge(L[n].sem, L[n].at(STEPS))

            D = flow["nodes2"]

            def by_bank(pn):
                return [(j, j // J, j % J, slice(j % J * F, j % J * F + pn)) for j in range(DJ)]

            def nodes_transpose_x2(g):
                pn = dense_p(g)
                wait_done(pe, D["n_row"], g)
                wait_previous(pe, D["x2tc"], g)
                for j, bank, _, c in by_bank(pn):
                    last = te.transpose(ps[0][bank][:, c], node_out[0:pn, g.b, j, :], ident[0:pn, 0:pn])
                last.then_inc(D["x2tp"].sem, 1)

            def nodes_h1(g):
                wait_done(pe, D["x2tc"], g)
                wait_previous(pe, D["h1tc"], g)
                for h in range(2):
                    last = te.matmul(ps[1][h][:, :], w1r_t[:, :], node_x2t[:, g.b, h * J * F:(h + 1) * J * F], start=True, stop=True)
                last.then_inc(D["h1p"].sem, 1)

            def nodes_y(g):
                pn = dense_p(g)
                wait_done(pe, D["h1tc"], g)
                wait_previous(pe, D["y"], g)
                for j, bank, i, _ in by_bank(pn):
                    if i == 0:
                        te.matmul(ps[3][bank][0:pn, :], ones_bf[:, 0:pn], b2_parts[:, :, :].rearrange("p j f -> p (j f)"),
                                  start=True, stop=False)
                    last = te.matmul(ps[3][bank][0:pn, i * F:(i + 1) * F], node_h1t[:, g.b, j * F:j * F + pn], w2r_t[:, :],
                                     start=False, stop=i == J - 1)
                last.then_inc(D["yp"].sem, 1)

            def nodes_h1_rows(g):
                pn = dense_p(g)
                wait_previous(pe, D["h1c"], g)
                for j, bank, i, _ in by_bank(pn):
                    last = te.transpose(ps[2][bank][0:pn, i * F:(i + 1) * F], node_h1t[:, g.b, j * F:j * F + pn], ident[:, :])
                last.then_inc(D["h1tp"].sem, 1)

            pipeline(pe, DENSE_FULL, [nodes(4, nodes_y), nodes(3, nodes_transpose_x2), nodes(4, nodes_h1_rows), nodes(3, nodes_h1)])
            for n in ("x2tc", "h1tc", "h1c", "y"):
                pe.wait_ge(D[n].sem, D[n].at(DENSE_STEPS))

            L = flow["sage1"]

            def sage_transpose(g, jn=J):
                wait_done(pe, L["msgd"], g)
                transpose_step(L, g, 0, msg, "tr_a", "cp_a", jn)
                if g is FIX:
                    pe.wait_ge(fix_in, 48 * (LAYER_NO["sage1" if L is flow["sage1"] else "sage2"] + 1))
                else:
                    wait_landed(pe, L["own"], g)
                transpose_step(L, g, 1, own_rows, "tr_b", "cp_b", jn)

            def sage_h1(g, jn=J):
                wait_done(pe, L["cp_a"], g)
                wait_done(pe, L["cp_b"], g)
                wait_free(pe, L["cp_c"], g)
                c = slice(0, jn * F)
                te.matmul(ps[2][g.b][:, c], w1l_t[:, :], t_a[:, g.b, c], start=True, stop=False)
                te.matmul(ps[2][g.b][:, c], w1r_t[:, :], t_b[:, g.b, c], start=False, stop=True).then_inc(L["mm"].sem, 1)

            def sage_h1_rows(g, jn=J):
                wait_done(pe, L["cp_c"], g)
                wait_free(pe, L["newd"], g)
                for j in range(jn):
                    c = slice(j * F, (j + 1) * F)
                    last = te.transpose(ps[3][g.b][:, c], t_c[:, g.b, c], ident[:, :])
                last.then_inc(L["mm2"].sem, 1)

            pipeline(pe, STEPS, edges((2, sage_h1_rows), (1, sage_h1), (0, sage_transpose)))
            carry(L, F + 1, L["cp_a"])
            sage_transpose(FIX, 1)
            sage_h1(FIX, 1)
            sage_h1_rows(FIX, 1)

            L = flow["sage2"]

            def sage_out(g, jn=J):
                wait_done(pe, L["cp_a"], g)
                wait_done(pe, L["cp_b"], g)
                wait_free(pe, L["pre"], g)
                te.matmul(ps[3][g.b][:, 0:jn * F], ones_bf[:, :], b2_parts[:, 0:jn, :].rearrange("p j f -> p (j f)"),
                          start=True, stop=False)
                for j in range(jn):
                    c = slice(j * F, (j + 1) * F)
                    te.matmul(ps[3][g.b][:, c], t_a[:, g.b, c], w2l_t[:, :], start=False, stop=False)
                    last = te.matmul(ps[3][g.b][:, c], t_b[:, g.b, c], w2r_t[:, :], start=False, stop=j == jn - 1)
                last.then_inc(L["mm"].sem, 1)

            pipeline(pe, STEPS, edges((1, sage_out), (0, sage_transpose)))
            carry(L, F + 1, L["cp_a"])
            sage_transpose(FIX, 1)
            sage_out(FIX, 1)
            open_rows(L, 4, L["cp_b"])

            L = flow["att1"]

            def att_transpose(g):
                wait_landed(pe, L["gathered"], g)
                transpose_step(L, g, 0, src_rows, "tr_a", "cp_a")
                wait_part(pe, L["spread"], g, J)
                transpose_step(L, g, 1, msg, "tr_b", "cp_b")

            def queries_keys(g):
                wait_done(pe, L["cp_a"], g)
                wait_free(pe, L["newd"], g)
                for j in range(J):
                    c = slice(j * F, (j + 1) * F)
                    last = te.matmul(ps[2][g.b][:, c], t_a[:, g.b, c], qw_sb[:, :, :].rearrange("f h d -> f (h d)"), start=True, stop=True)
                last.then_inc(L["mm"].sem, 1)
                wait_done(pe, L["cp_b"], g)
                wait_free(pe, L["cp_c"], g)
                for j in range(J):
                    c = slice(j * F, (j + 1) * F)
                    last = te.matmul(ps[3][g.b][:, c], t_b[:, g.b, c], kw_sb[:, :, :].rearrange("f h d -> f (h d)"), start=True, stop=True)
                last.then_inc(L["mm2"].sem, 1)

            pipeline(pe, STEPS, edges((1, queries_keys), (0, att_transpose)))
            pe.wait_ge(max_at, 1)
            for i in range(2):
                last = te.matmul(ps[i][0][:, :], ones[:, :],
                                 diag[:, 2 + i * HEADS:2 + (i + 1) * HEADS, :].rearrange("p h q -> p (h q)"), start=True, stop=True)
            last.then_inc(max_at, 1)

            L = flow["att2"]
            pe.wait_ge(max_at, 3)

            def att_back_transpose(g, jn=J):
                wait_done(pe, L["msg0"], g)
                transpose_step(L, g, 0, gate, "tr_a", "cp_a", jn)

            def att_project(g, jn=J):
                wait_done(pe, L["cp_a"], g)
                wait_free(pe, L["pre2"], g)
                te.matmul(ps[3][g.b][:, 0:jn * F], ones_bf[:, :], outb_parts[:, 0:jn, :].rearrange("p j f -> p (j f)"),
                          start=True, stop=False)
                for j in range(jn):
                    c = slice(j * F, (j + 1) * F)
                    last = te.matmul(ps[3][g.b][:, c], t_a[:, g.b, c], outw_sb[:, :], start=False, stop=j == jn - 1)
                last.then_inc(L["mm"].sem, 1)

            pipeline(pe, STEPS, edges((1, att_project), (0, att_back_transpose)))
            pe.wait_ge(L["accd"].sem, L["accd"].at(STEPS))
            carry(L, ACC_W, L["cp_a"])
            att_back_transpose(FIX, 1)
            att_project(FIX, 1)

        @block.scalar
        def _(act):
            sc = nc.scalar
            act.wait_ge(cols_in, 16 * 5)
            sc.activation(sbeta_col, beta_col, ACT.Silu).then_inc(act_prep, 1)

            def roots(L, k):
                def root(g, jn=None):
                    pn, jn = (dense_p(g), DJ) if k == "n" else (P, jn or J)
                    wait_done(act, L[f"{k}_ve"], g)
                    at = NORM[k][2][0:pn, g.b, 0:jn]
                    sc.activation(at, at, ACT.Sqrt).then_inc(L[f"{k}_rt"].sem, 1)
                return root

            def normed_rows(L, k, rows, to, made, out_ring=None, used=()):
                def make(g, jn=None):
                    pn, jn = (dense_p(g), DJ) if k == "n" else (P, jn or J)
                    if out_ring:
                        wait_drained(act, L[out_ring], g)
                    for signal in used:
                        wait_free(act, L[signal], g)
                    wait_done(act, L[f"{k}_nm"], g)
                    for j in range(jn):
                        last = sc.activation(to[0:pn, g.b, j, :], rows[0:pn, g.b, j, 0:F], ACT.Identity,
                                             bias=NORM[k][3][0:pn, g.b, j:j + 1], scale=NORM[k][2][0:pn, g.b, j:j + 1])
                    last.then_inc(L[made].sem, 1)
                return make

            D = flow["nodes1"]
            pipeline(act, DENSE_FULL, [nodes(1, normed_rows(D, "n", node_in, node_out, "n_row", "n_out")), nodes(0, roots(D, "n"))])

            def copy_out(L, g, bank, to, produced, copied, free, jn=J):
                wait_done(act, L[produced], g)
                wait_free(act, L[free], g)
                sc.activation(to[:, g.b, 0:jn * F], ps[bank][g.b][:, 0:jn * F], ACT.Copy).then_inc(L[copied].sem, 1)

            L = flow["msg"]

            def copy_ends(g):
                copy_out(L, g, 0, t_a, "tr_a", "cp_a", "mm")
                copy_out(L, g, 1, t_b, "tr_b", "cp_b", "mm")
                wait_done(act, L["tr_e"], g)
                sc.activation(t_e[0:FE, g.b, :], ps[2][g.b][0:FE, :], ACT.Copy).then_inc(L["cp_e"].sem, 1)

            def sigmoid(g):
                wait_done(act, L["mm"], g)
                wait_free(act, L["msg0"], g)
                sc.activation(gate[:, g.b, :, :].rearrange("p j f -> p (j f)"), ps[3][g.b][:, :], ACT.Sigmoid)\
                    .then_inc(L["sig"].sem, 1)

            new_x1 = normed_rows(L, "e", pre, new_rows, "newd", "stored")
            pipeline(act, STEPS, edges((3, new_x1), (1, sigmoid), (0, copy_ends)))
            new_x1(FIX, 1)

            L = flow["gat"]

            def exp_scores(g):
                wait_done(act, L["e2"], g)
                wait_free(act, L["msgd"], g)
                wait_free(act, L["w_lo"], g)
                sc.activation(edge4[:, g.b, 4, :], edge4[:, g.b, 3, :], ACT.Exp).then_inc(L["expd"].sem, 1)

            def broadcast_keys(g):
                wait_done(act, L["keyd"], g)
                wait_free(act, L["tr_a"], g)
                for j in range(J):
                    last = sc.activation(bc[:, g.b, j, :], ones[:, :], ACT.Copy, scale=key4[:, g.b, 0, j:j + 1])
                last.then_inc(L["bcd"].sem, 1)

            def weighted_rows(g):
                wait_free(act, L["mm"], g)
                wait_done(act, L["expd"], g)
                wait_part(act, L["spread"], g, J)
                for j in range(J):
                    last = sc.activation(msg[:, g.b, j, 0:F], acc[:, g.b, j, 0:F], ACT.Copy, scale=edge4[:, g.b, 4, j:j + 1])
                last.then_inc(L["msgd"].sem, 1)

            def gat_copy_sums(g):
                wait_done(act, L["mm"], g)
                wait_free(act, L["mm2"], g)
                sc.activation(t_c[:, g.b, :], ps[2][g.b][:, :], ACT.Copy).then_inc(L["cp_a"].sem, 1)

            def gat_copy_projected(g):
                if not g.first_use():
                    act.wait_ge(L["added"].sem, L["added"].per * (g.index() - 1))
                wait_done(act, L["mm2"], g)
                sc.activation(sums[:, g.b, :, F:F + 3], ps[1][g.b][:, 0:3 * J].rearrange("p (j w) -> p j w", w=3), ACT.Copy)
                sc.activation(sums[:, g.b, :, 0:F], ps[3][g.b][:, :].rearrange("p (j f) -> p j f", f=F), ACT.Copy)\
                    .then_inc(L["cp_b"].sem, 1)

            def same_to_bf16(g):
                wait_done(act, L["samed"], g)
                wait_free(act, L["mm"], g)
                for j in range(J):
                    n = (j + 1) * P
                    last = sc.activation(same_bf[:, g.b, j, 0:n], same[g.b][:, j, 0:n], ACT.Copy)
                last.then_inc(L["same_bf"].sem, 1)

            pipeline(act, STEPS, edges((2, gat_copy_projected), (1, weighted_rows), (1, same_to_bf16), (0, broadcast_keys), (1, gat_copy_sums), (0, exp_scores)))

            L, D = flow["x2"], flow["nodes2"]
            banks = [(h, slice(h * J * F, (h + 1) * J * F)) for h in range(2)]

            def nodes_copy_x2t(g):
                wait_done(act, D["x2tp"], g)
                wait_free(act, D["h1p"], g)
                for h, c in banks:
                    last = sc.activation(node_x2t[:, g.b, c], ps[0][h][:, :], ACT.Copy)
                last.then_inc(D["x2tc"].sem, 1)

            def nodes_relu(g):
                wait_done(act, D["h1p"], g)
                wait_free(act, D["h1tp"], g)
                for h, c in banks:
                    last = sc.activation(node_h1t[:, g.b, c], ps[1][h][:, :], ACT.Relu, bias=b1_col)
                last.then_inc(D["h1tc"].sem, 1)

            def nodes_copy_h1(g):
                pn = dense_p(g)
                wait_done(act, D["h1tp"], g)
                wait_drained(act, D["n_h1"], g)
                for h, _ in banks:
                    last = sc.activation(node_h1[0:pn, g.b, h * J:(h + 1) * J, :].rearrange("p j f -> p (j f)"),
                                         ps[2][h][0:pn, :], ACT.Copy)
                last.then_inc(D["h1c"].sem, 1)

            pipeline(act, DENSE_FULL, [
                nodes(3, nodes_copy_x2t), nodes(4, nodes_copy_h1), nodes(3, nodes_relu),
                nodes(2, normed_rows(D, "n", node_in, node_out, "n_row", "n_out", ("x2tp", "y")))]
                + edges((2, normed_rows(L, "e", pre, new_rows, "newd", "stored")))
                + [nodes(1, roots(D, "n"))] + edges((1, roots(L, "e"))))

            L = flow["sage1"]

            def sage_copies(g, jn=J):
                copy_out(L, g, 0, t_a, "tr_a", "cp_a", "mm", jn)
                copy_out(L, g, 1, t_b, "tr_b", "cp_b", "mm", jn)

            def sage_relu(g, jn=J):
                wait_done(act, L["mm"], g)
                wait_free(act, L["mm2"], g)
                sc.activation(t_c[:, g.b, 0:jn * F], ps[2][g.b][:, 0:jn * F], ACT.Relu, bias=b1_col).then_inc(L["cp_c"].sem, 1)

            def h1_rows(g, jn=J):
                wait_done(act, L["mm2"], g)
                wait_drained(act, L["stored"], g)
                sc.activation(new_rows[:, g.b, 0:jn, :].rearrange("p j f -> p (j f)"), ps[3][g.b][:, 0:jn * F], ACT.Copy)\
                    .then_inc(L["newd"].sem, 1)

            D = flow["nodes3"]
            pipeline(act, DENSE_FULL, edges((2, h1_rows), (1, sage_relu))
                     + [nodes(1, normed_rows(D, "n", node_in, node_out, "n_row", "n_out"))]
                     + edges((0, sage_copies)) + [nodes(0, roots(D, "n"))])
            sage_copies(FIX, 1)
            sage_relu(FIX, 1)
            h1_rows(FIX, 1)

            L = flow["sage2"]
            new_x3, root = normed_rows(L, "e", pre, new_rows, "newd", "stored"), roots(L, "e")
            pipeline(act, STEPS, edges((3, new_x3), (2, root), (0, sage_copies)))
            sage_copies(FIX, 1)
            root(FIX, 1)
            new_x3(FIX, 1)

            L, D = flow["att1"], flow["nodes4"]

            def att_copies(g):
                copy_out(L, g, 0, t_a, "tr_a", "cp_a", "mm")
                copy_out(L, g, 1, t_b, "tr_b", "cp_b", "mm2")

            def queries_keys_out(g):
                wait_done(act, L["mm"], g)
                wait_drained(act, L["stored"], g)
                wait_free(act, L["pre"], g)
                if g.first_use():
                    act.wait_ge(opened, 4)
                sc.activation(new_rows[:, g.b, :, :].rearrange("p j f -> p (j f)"), ps[2][g.b][:, :], ACT.Copy)\
                    .then_inc(L["newd"].sem, 1)
                wait_done(act, L["mm2"], g)
                sc.activation(gate[:, g.b, :, :].rearrange("p j f -> p (j f)"), ps[3][g.b][:, :], ACT.Copy,
                              scale=float(HID) ** -0.5).then_inc(L["cp_c"].sem, 1)

            pipeline(act, DENSE_FULL, [nodes(1, roots(D, "n"))] + edges((1, queries_keys_out), (0, att_copies))
                     + [nodes(1, normed_rows(D, "n", node_in, node_out, "n_row", "n_out"))])
            act.wait_ge(max_at, 4)
            sc.activation(alpha[:, :, :].rearrange("p t h -> p (t h)"), tmp_a[:, :, :].rearrange("p t h -> p (t h)"),
                          ACT.Exp).then_inc(max_at, 1)

            L = flow["att2"]

            def silu(g, jn=J):
                wait_done(act, L["tr_a"], g)
                wait_free(act, L["mm"], g)
                sc.activation(t_a[:, g.b, 0:jn * F], ps[0][g.b][:, 0:jn * F], ACT.Silu, bias=beta_col, scale=gamma_col)\
                    .then_inc(L["cp_a"].sem, 1)

            normed = normed_rows(L, "e", pre, gate, "msg0", None, ("tr_a",))
            new_x4 = normed_rows(L, "a", ny, new_rows, "newd", "scattered")
            pipeline(act, STEPS, edges((6, new_x4), (3, silu), (2, normed)))
            normed(FIX, 1)
            silu(FIX, 1)
            new_x4(FIX, 1)

        @block.vector
        def _(dve):
            v = nc.vector
            linked = [0]

            def link(ins):
                linked[0] += 1
                ins.then_inc(slots_made, 1)
                dve.wait_ge(slots_made, linked[0])

            first, last_ = d[:, 1:2], d[:, T:T + 1]
            dve.wait_ge(consts_made, 3)
            dve.wait_ge(dst_in, 48)
            dve.wait_ge(src_in, 16)
            v.memset(t_e[FE:FE + 1, :, :], 1.0)
            v.memset(earlier[:, 0:(J - 1) * P], 1.0)
            v.tensor_copy(earlier[:, (J - 1) * P:], lower[:, :])
            link(v.tensor_copy(d[:, :], dst_i[:, :]))
            v.tensor_copy(slot[:, :], slot_i[:, :])
            v.tensor_tensor(keep[:, :], d[:, 1:T + 1], d[:, 0:T], ALU.is_equal)
            v.tensor_tensor(canon[:, :], d[:, 1:T + 1], d[:, 2:T + 2], ALU.not_equal)
            v.tensor_scalar(in_first[:, :], d[:, 1:T + 1], first, None, ALU.is_equal)
            link(v.tensor_scalar_min(dst_safe_i[:, :], d[:, 1:T + 1], float(N_NODES - 1)))
            v.memset(keep[:, 0:1], 0.0)
            link(v.tensor_scalar(tmp_t[:, :], canon[:, :], -float(FAR), float(FAR), ALU.mult, ALU.add))
            v.tensor_tensor(map_index[:, :], tmp_t[:, :], d[:, 1:T + 1], ALU.add).then_inc(map_index_made, 1)
            link(v.tensor_tensor(first_done[:, :], in_first[:, :], canon[:, :], ALU.mult))
            link(v.reduce_sum(has_first, first_done[:, :], axis=AX))
            link(v.tensor_tensor(tmp_t[:, :], first_done[:, :], slot[:, :], ALU.mult))
            link(v.reduce_sum(fix_slot, tmp_t[:, :], axis=AX))
            link(v.tensor_copy(fix_read, fix_slot))
            link(v.tensor_scalar(fix_skip[:, :], has_first, -float(FAR), float(FAR), ALU.mult, ALU.add))
            link(v.tensor_tensor(fix_write, fix_skip[:, :], fix_slot, ALU.add))
            v.tensor_tensor(fix_out, fix_skip[:, :], first, ALU.add)
            v.tensor_copy(fix_node, dst_safe_i[:, 0:1])
            link(v.tensor_tensor(canon_inner[:, :], canon[:, :], first_done[:, :], ALU.subtract))
            link(v.tensor_scalar(tmp_t[:, :], canon_inner[:, :], -float(FAR), float(FAR), ALU.mult, ALU.add))
            link(v.tensor_tensor(out_index[:, :], tmp_t[:, :], d[:, 1:T + 1], ALU.add))
            link(v.tensor_scalar(tmp_t[:, 0:1], first, float(N_NODES - 1), None, ALU.is_gt))
            link(v.tensor_tensor(dummy_row[:, 1:2], tmp_t[:, 0:1], dummy_row[:, 0:1], ALU.mult))
            v.tensor_scalar(source_key[:, :], src_i[:, :], dummy_row[:, 1:2], None, ALU.add).then_inc(slots_set, 1)
            v.tensor_scalar(diag[:, 0, :], ident[:, :], first, None, ALU.mult)
            v.tensor_scalar(diag[:, 1, :], ident[:, :], last_, None, ALU.mult).then_inc(fix_ready, 1)
            dve.wait_ge(pe_prep, 2)
            first_row, last_row = ps[2][0][:, 0:P], ps[2][0][:, P:2 * P]
            link(v.scalar_tensor_tensor(sum_carry[:, :], first_row, last_, upper[:, :], ALU.is_equal, ALU.mult))
            link(v.scalar_tensor_tensor(back_carry[:, :], last_row, first, lower[:, :], ALU.is_equal, ALU.mult))
            link(v.tensor_scalar(back_carry[:, :], back_carry[:, :], has_first, None, ALU.mult))
            for i, (row, col) in enumerate(((first_row, first), (last_row, first), (first_row, last_), (last_row, last_))):
                link(v.tensor_scalar(max_pen[:, i, :], row, col, None, ALU.is_equal))
            link(v.tensor_scalar(max_pen[:, :, :], max_pen[:, :, :], 1.0, LOW, ALU.subtract, ALU.mult))
            link(v.tensor_scalar(undone[:, :], canon[:, :], -1.0, 1.0, ALU.mult, ALU.add))
            for k, s in enumerate(DOUBLINGS):
                v.tensor_tensor(apart[:, k, 0:T - s], d[:, 1:1 + T - s], d[:, 1 + s:1 + T], ALU.is_equal).then_inc(apart_made, 1)
            dve.wait_ge(apart_made, len(DOUBLINGS))
            for k, s in enumerate(DOUBLINGS):
                v.tensor_scalar(apart[:, k, 0:T - s], apart[:, k, 0:T - s], 1.0, LOW, ALU.subtract, ALU.mult)
            dve.wait_ge(weights_in, 16 * 13)
            link(v.tensor_copy(bias_hi[:, :, :], bias_rows[:, :, :]))
            link(v.tensor_tensor(bias_rows[:, :, :], bias_rows[:, :, :], bias_hi[:, :, :], ALU.subtract))
            link(v.tensor_copy(bias_mid[:, :, :], bias_rows[:, :, :]))
            link(v.tensor_tensor(bias_rows[:, :, :], bias_rows[:, :, :], bias_mid[:, :, :], ALU.subtract))
            link(v.tensor_copy(bias_lo[:, :, :], bias_rows[:, :, :]))
            v.tensor_copy(ones_bf[:, :], ones[0:3, :])
            link(v.tensor_scalar(bias_hi[:, :, :], bias_hi[:, :, :], ident[0:3, 0:1], None, ALU.mult))
            link(v.scalar_tensor_tensor(bias_mid[:, :, :], bias_mid[:, :, :], ident[0:3, 1:2], bias_hi[:, :, :], ALU.mult, ALU.add))
            for i, parts in enumerate((b2_parts, outb_parts)):
                for j in range(J):
                    v.scalar_tensor_tensor(parts[:, j, :], bias_lo[:, i, :], ident[0:3, 2:3], bias_mid[:, i, :], ALU.mult, ALU.add)
            dve.wait_ge(pe_prep, 1)
            for i, w in enumerate((w0s_t, w0d_t, wgat_t, w1l_t, w1r_t, w2l_t, w2r_t)):
                v.tensor_copy(w[:, :], ps[i // 4][0][:, (i % 4) * F:(i % 4 + 1) * F])
            v.tensor_copy(w0e_t[0:FE, :], ps[1][0][0:FE, 3 * F:4 * F])
            dve.wait_ge(cols_in, 16 * 5)
            dve.wait_ge(act_prep, 1)
            for i, col in enumerate((adst_col, asrc_col, sbeta_col)):
                last = v.tensor_scalar(col_bc[:, i, :], ones[:, :], col, None, ALU.mult)
            last.then_inc(fix_ready, 1)
            dve.wait_ge(pe_prep, 3)
            dve.wait_ge(weights_in, 16 * 13)
            v.tensor_copy(vdst_bc[:, :], ps[3][0][:, 0:F])
            v.tensor_copy(vsrc_bc[:, :], ps[3][0][:, F:2 * F])
            v.tensor_tensor(local3_bc[:, :], ps[3][0][:, 2 * F:3 * F], outb_bc[:, :], ALU.add).then_inc(dve_prep, 1)
            dve.wait_ge(dve_prep, 1)

            def moments(*works):
                for L, k, g, rows, pn, jn in works:
                    for j in range(jn):
                        last = v.bn_stats(NORM[k][0][0:pn, g.b, j, :], rows[0:pn, g.b, j, 0:F])
                    last.then_inc(L[f"{k}_bn"].sem, 1)
                for L, k, g, rows, pn, jn in works:
                    wait_free(dve, L[f"{k}_nm"], g)
                    wait_done(dve, L[f"{k}_bn"], g)
                    settle(dve)
                    for j in range(jn):
                        last = v.bn_aggr(NORM[k][1][0:pn, g.b, j, :], NORM[k][0][0:pn, g.b, j, :])
                    last.then_inc(L[f"{k}_ag"].sem, 1)
                for L, k, g, rows, pn, jn in works:
                    wait_done(dve, L[f"{k}_ag"], g)
                    v.tensor_scalar_add(NORM[k][2][0:pn, g.b, 0:jn], NORM[k][1][0:pn, g.b, 0:jn, 1], EPS).then_inc(L[f"{k}_ve"].sem, 1)

            def shifts(L, k, inverted=True, only_canon=False):
                def make(g, jn=None):
                    pn, jn = (dense_p(g), DJ) if k == "n" else (P, jn or J)
                    _, mv, root, shift = NORM[k]
                    at = root[0:pn, g.b, 0:jn]
                    wait_done(dve, L[f"{k}_rt"], g)
                    if inverted:
                        v.reciprocal(at, at).then_inc(L[f"{k}_rc"].sem, 1)
                        wait_done(dve, L[f"{k}_rc"], g)
                    if only_canon:
                        of_slots = fours(canon, g) if g is not FIX else ones[:, 0:jn]
                        v.tensor_tensor(at, at, of_slots, ALU.mult).then_inc(L[f"{k}_cn"].sem, 1)
                        wait_done(dve, L[f"{k}_cn"], g)
                    v.scalar_tensor_tensor(shift[0:pn, g.b, 0:jn], mv[0:pn, g.b, 0:jn, 0], -1.0, at, ALU.mult, ALU.mult)\
                        .then_inc(L[f"{k}_nm"].sem, 1)
                return make

            def node_moments(D):
                def make(g):
                    wait_landed(dve, D["n_in"], g)
                    wait_free(dve, D["n_row"], g)
                    moments((D, "n", g, node_in, dense_p(g), DJ))
                return make

            D = flow["nodes1"]
            pipeline(dve, DENSE_FULL, [nodes(1, shifts(D, "n")), nodes(0, node_moments(D))])

            def running_sum(L, j, rows, width):
                def add(g):
                    if j == 0:
                        wait_drained(dve, L["dumped"], g)
                    wait_part(dve, L["accd"], g, j)
                    before = acc[:, g.b, j - 1, 0:width] if j else acc[:, 1 - g.b, J - 1, 0:width]
                    v.scalar_tensor_tensor(acc[:, g.b, j, 0:width], before, keep[:, bass.ds(g.index() * J + j, 1)],
                                           rows[:, g.b, j, 0:width], ALU.mult, ALU.add).then_inc(L["accd"].sem, 1)
                return add

            def running_sums(L, g, rows, width):
                for j in range(J):
                    running_sum(L, j, rows, width)(g)

            def fix_sums(L, width, times):
                n = LAYER_NO[next(k for k in flow if flow[k] is L)]
                dve.wait_ge(fix_in, 48 * (n + 1))
                dve.wait_ge(carried, times)
                v.tensor_tensor(acc[:, 0, 0, 0:width], fix_acc[:, 0:width], ps[0][0][:, 0:width], ALU.add)\
                    .then_inc(L["accd"].sem, J)

            L = flow["msg"]

            def message_sums(g):
                wait_done(dve, L["sig"], g)
                v.tensor_tensor(msg[:, g.b, :, 0:F], ps[3][g.b][:, :].rearrange("p (j f) -> p j f", f=F), gate[:, g.b, :, :], ALU.mult)\
                    .then_inc(L["msg0"].sem, 1)
                wait_done(dve, L["msg0"], g)
                v.scalar_tensor_tensor(msg[:, g.b, :, 0:F], msg[:, g.b, :, 0:F], 0.01, msg[:, g.b, :, 0:F], ALU.mult, ALU.max)\
                    .then_inc(L["msgd"].sem, 1)
                wait_done(dve, L["msgd"], g)
                running_sums(L, g, msg, F)

            def x1_sums(g, jn=J):
                wait_free(dve, L["newd"], g)
                wait_done(dve, L["accd"], g)
                v.tensor_tensor(pre[:, g.b, 0:jn, :], own_rows[:, g.b, 0:jn, :], acc[:, g.b, 0:jn, 0:F], ALU.add).then_inc(L["pre"].sem, 1)
                wait_done(dve, L["pre"], g)
                moments((L, "e", g, pre, P, jn))

            x1_shifts = shifts(L, "e", False, True)
            pipeline(dve, STEPS, edges((3, x1_shifts), (1, message_sums), (1, x1_sums)))
            fix_sums(L, F, 1)
            x1_sums(FIX, 1)
            x1_shifts(FIX, 1)
            def take_open_rows(times):
                dve.wait_ge(opened, times)
                v.tensor_copy(open_row[:, :], ps[1][0][:, 0:F]).then_inc(opened, 1)

            def spread_row(L, i, rows, to, used):
                def add(g):
                    if i == 0:
                        wait_landed(dve, L["own"], g)
                        wait_free(dve, L[used], g)
                    j = J - 1 - i
                    if isinstance(g.k, int) and g.index() == 0 and i == 0:
                        after = open_row[:, :]
                    else:
                        wait_part(dve, L["spread"], g, i)
                        after = to[:, g.b, j + 1, 0:F] if i else to[:, 1 - g.b, 0, 0:F]
                    v.scalar_tensor_tensor(to[:, g.b, j, 0:F], after, undone[:, bass.ds(back(g).index() * J + j, 1)],
                                           rows[:, g.b, j, :], ALU.mult, ALU.add).then_inc(L["spread"].sem, 1)
                return add

            L = flow["gat"]
            take_open_rows(1)
            dve.wait_ge(opened, 2)

            def edge_scores(g):
                wait_landed(dve, L["gathered"], g)
                wait_part(dve, L["spread"], g, J)
                for i, (rows, vec) in enumerate(((own_rows, vdst_bc), (acc, vsrc_bc))):
                    for j in range(J):
                        last = v.tensor_tensor_reduce(out=junk[:, i, j, :], in0=rows[:, g.b, j, 0:F], in1=vec[:, :], scale=1.0,
                                                      scalar=0.0, op0=ALU.mult, op1=ALU.add, accum_out=edge4[:, g.b, i, j:j + 1])
                last.then_inc(L["score"].sem, 1)

            def add_scores(g):
                wait_done(dve, L["score"], g)
                v.tensor_tensor(edge4[:, g.b, 2, :], edge4[:, g.b, 0, :], edge4[:, g.b, 1, :], ALU.add).then_inc(L["e0"].sem, 1)

            def leaky_scores(g):
                wait_done(dve, L["e0"], g)
                v.scalar_tensor_tensor(edge4[:, g.b, 5, :], edge4[:, g.b, 2, :], 0.2, edge4[:, g.b, 2, :], ALU.mult, ALU.max)\
                    .then_inc(L["e1"].sem, 1)

            def clip_scores(g):
                wait_free(dve, L["expd"], g)
                wait_done(dve, L["e1"], g)
                v.tensor_scalar(edge4[:, g.b, 3, :], edge4[:, g.b, 5, :], -2.0, 2.0, ALU.max, ALU.min).then_inc(L["e2"].sem, 1)

            def edge_keys(g):
                wait_free(dve, L["bcd"], g)
                v.tensor_copy(key4[:, g.b, 0, :], fours(source_key, back(g))).then_inc(L["keyd"].sem, 1)

            def same_sources(g):
                wait_done(dve, L["tr_a"], g)
                wait_free(dve, L["mm"], g)
                for j in range(J):
                    n = (j + 1) * P
                    last = v.tensor_scalar(same[g.b][:, j, 0:n], ps[0][g.b][:, 0:n], key4[:, g.b, 0, j:j + 1], None, ALU.is_equal)
                last.then_inc(L["samed"].sem, 1)
                wait_done(dve, L["samed"], g)
                for j in range(J):
                    n = (j + 1) * P
                    last = v.tensor_tensor_reduce(out=junk2[:, j, 0:n], in0=same[g.b][:, j, 0:n], in1=earlier[:, J * P - n:], scale=1.0,
                                                  scalar=0.0, op0=ALU.mult, op1=ALU.add, accum_out=key4[:, g.b, 1, j:j + 1])
                last.then_inc(L["rep0"].sem, 1)

            def keys_apart(g):
                v.tensor_tensor(key4[:, g.b, 2, :], key4[:, g.b, 0, :], dummy_rows[:, :], ALU.subtract)
                wait_done(dve, L["rep0"], g)
                v.tensor_scalar(key4[:, g.b, 3, :], key4[:, g.b, 1, :], 0.0, None, ALU.is_equal).then_inc(L["rep1"].sem, 1)

            def keys_of_first(g):
                wait_free(dve, L["rep2"], g)
                wait_done(dve, L["rep1"], g)
                v.tensor_tensor(key4[:, g.b, 4, :], key4[:, g.b, 2, :], key4[:, g.b, 3, :], ALU.mult).then_inc(L["rep3"].sem, 1)

            def add_indices(g):
                if not g.first_use():
                    dve.wait_ge(L["added"].sem, L["added"].per * (g.index() - 1))
                wait_done(dve, L["rep3"], g)
                v.tensor_tensor(add_idx[:, g.b, :], key4[:, g.b, 4, :], dummy_rows[:, :], ALU.add).then_inc(L["rep2"].sem, 1)

            def weight_part(i):
                def make(g):
                    if i == 0:
                        wait_done(dve, L["expd"], g)
                        wait_free(dve, L["mm"], g)
                    if i:
                        wait_done(dve, L[("w_r1", "w_r2")[i - 1]], g)
                    left = w_left[:, g.b, i - 1, :] if i else edge4[:, g.b, 4, :]
                    v.tensor_copy(w_parts[:, g.b, i, :], left).then_inc(L[("w_hi", "w_mid", "w_lo")[i]].sem, 1)
                return make

            def weight_rest(i):
                def make(g):
                    wait_done(dve, L[("w_hi", "w_mid")[i]], g)
                    left = w_left[:, g.b, i - 1, :] if i else edge4[:, g.b, 4, :]
                    v.tensor_tensor(w_left[:, g.b, i, :], left, w_parts[:, g.b, i, :], ALU.subtract).then_inc(L[("w_r1", "w_r2")[i]].sem, 1)
                return make

            spread = [(0, spread_row(L, i, own2_rows, acc, "msgd")) for i in range(J)]
            pipeline(dve, STEPS, edges(
                (2, add_indices), (0, edge_keys), (1, weight_part(0)), spread[0], (1, weight_rest(0)), spread[1], (1, weight_part(1)), spread[2],
                (1, weight_rest(1)), spread[3], (1, weight_part(2)), (1, same_sources), (0, edge_scores),
                (1, keys_apart), (0, add_scores), (0, leaky_scores), (1, keys_of_first), (0, clip_scores)))

            L, D = flow["x2"], flow["nodes2"]

            def add_means(*works):
                for M, (rcs, rc0, rc1, made), g, rows, row_sums, recips, to, pn, jn in works:
                    v.tensor_reduce(recips[0:pn, g.b, 0, 0:jn], row_sums[0:pn, g.b, 0:jn, F:F + 3], axis=AX, op=ALU.add)\
                        .then_inc(M[rcs].sem, 1)
                for M, (rcs, rc0, rc1, made), g, rows, row_sums, recips, to, pn, jn in works:
                    wait_done(dve, M[rcs], g)
                    at = recips[0:pn, g.b, 0, 0:jn]
                    v.tensor_scalar_max(at, at, 1e-30).then_inc(M[rc0].sem, 1)
                for M, (rcs, rc0, rc1, made), g, rows, row_sums, recips, to, pn, jn in works:
                    wait_done(dve, M[rc0], g)
                    v.reciprocal(recips[0:pn, g.b, 1, 0:jn], recips[0:pn, g.b, 0, 0:jn]).then_inc(M[rc1].sem, 1)
                for M, (rcs, rc0, rc1, made), g, rows, row_sums, recips, to, pn, jn in works:
                    wait_done(dve, M[rc1], g)
                    for j in range(jn):
                        last = v.scalar_tensor_tensor(to[0:pn, g.b, j, :], row_sums[0:pn, g.b, j, 0:F], recips[0:pn, g.b, 1, j:j + 1],
                                                      rows[0:pn, g.b, j, :], ALU.mult, ALU.add)
                    last.then_inc(M[made].sem, 1)
                for M, (rcs, rc0, rc1, made), g, *_ in works:
                    wait_done(dve, M[made], g)

            def make_x2(g):
                sums_works, norm_works = [], []
                if not (isinstance(g.k, int) and g.index() >= DENSE_STEPS):
                    wait_landed(dve, D["n_in"], g)
                    wait_free(dve, D["n_row"], g)
                    sums_works.append((D, ("n_rcs", "n_rc0", "n_rc1", "n_pre"), g, node_in, node_sums, node_recip, node_in, dense_p(g), DJ))
                    norm_works.append((D, "n", g, node_in, dense_p(g), DJ))
                wait_landed(dve, L["own"], g)
                wait_landed(dve, L["gathered"], g)
                wait_free(dve, L["newd"], g)
                sums_works.append((L, ("rcs", "rc0", "rc1", "pre"), g, own_rows, sums, edge4, pre, P, J))
                norm_works.append((L, "e", g, pre, P, J))
                add_means(*sums_works)
                moments(*norm_works)

            def nodes_y(g):
                pn = dense_p(g)
                wait_done(dve, D["yp"], g)
                wait_drained(dve, D["n_y"], g)
                for h in range(2):
                    rows = slice(h * J, (h + 1) * J)
                    last = v.tensor_tensor(node_y[0:pn, g.b, rows, :].rearrange("p j f -> p (j f)"), ps[3][h][0:pn, :],
                                           node_out[0:pn, g.b, rows, :].rearrange("p j f -> p (j f)"), ALU.add)
                last.then_inc(D["y"].sem, 1)

            pipeline(dve, DENSE_FULL, [nodes(2, shifts(D, "n"))] + edges((2, shifts(L, "e"))) + [nodes(4, nodes_y)]
                     + edges((1, make_x2)))

            def plain_sums(g):
                wait_landed(dve, L["gathered"], g)
                running_sums(L, g, src_rows, F + 1)

            def means(g, jn=J):
                wait_done(dve, L["accd"], g)
                v.reciprocal(edge4[:, g.b, 5, 0:jn], acc[:, g.b, 0:jn, F]).then_inc(L["rcp"].sem, 1)
                wait_free(dve, L["tr_a"], g)
                wait_done(dve, L["rcp"], g)
                for j in range(jn):
                    last = v.tensor_scalar(msg[:, g.b, j, 0:F], acc[:, g.b, j, 0:F], edge4[:, g.b, 5, j:j + 1], None, ALU.mult)
                last.then_inc(L["msgd"].sem, 1)

            def sums_and_means(g):
                plain_sums(g)
                means(g)

            L = flow["sage1"]

            D = flow["nodes3"]
            pipeline(dve, DENSE_FULL, [nodes(1, shifts(D, "n"))] + edges((0, sums_and_means)) + [nodes(0, node_moments(D))])
            fix_sums(L, F + 1, 2)
            means(FIX, 1)

            L = flow["sage2"]

            def x3_sums(g, jn=J):
                if g is FIX:
                    dve.wait_ge(fix_in, 48 * 3)
                else:
                    wait_landed(dve, L["own2"], g)
                wait_done(dve, L["mm"], g)
                wait_free(dve, L["newd"], g)
                v.tensor_tensor(pre[:, g.b, 0:jn, :].rearrange("p j f -> p (j f)"), ps[3][g.b][:, 0:jn * F],
                                own2_rows[:, g.b, 0:jn, :].rearrange("p j f -> p (j f)"), ALU.add).then_inc(L["pre"].sem, 1)

            def x3_moments(g, jn=J):
                wait_done(dve, L["pre"], g)
                moments((L, "e", g, pre, P, jn))

            x3_shifts = shifts(L, "e", True, True)
            def sources_landed(g):
                wait_landed(dve, L["gathered"], g)

            run = [(0, running_sum(L, j, src_rows, F + 1)) for j in range(J)]
            pipeline(dve, STEPS, edges((3, x3_shifts), (0, sources_landed), run[0], (2, x3_sums), run[1], (2, x3_moments), run[2], run[3],
                                       (0, means)))
            fix_sums(L, F + 1, 3)
            means(FIX, 1)
            x3_sums(FIX, 1)
            x3_moments(FIX, 1)
            x3_shifts(FIX, 1)

            L, D = flow["att1"], flow["nodes4"]

            spread = [(0, spread_row(L, i, own_rows, msg, "tr_b")) for i in range(J)]
            take_open_rows(3)
            dve.wait_ge(opened, 4)

            def products(g):
                wait_done(dve, L["newd"], g)
                wait_done(dve, L["cp_c"], g)
                wait_free(dve, L["score"], g)
                v.tensor_tensor(pre[:, g.b, :, :], new_rows[:, g.b, :, :], gate[:, g.b, :, :], ALU.mult).then_inc(L["pre"].sem, 1)

            def score_sums(g):
                wait_done(dve, L["pre"], g)
                v.tensor_reduce(alpha[:, bass.ds(back(g).index() * J, J), :], pre[:, g.b, :, :].rearrange("p j (h e) -> p j h e", e=HID),
                                axis=AX, op=ALU.add).then_inc(L["score"].sem, 1)

            def nodes_x3_more(g):
                pn = dense_p(g)
                wait_landed(dve, D["n_in"], g)
                v.tensor_tensor(node_in[0:pn, g.b, :, :], node_in[0:pn, g.b, :, :],
                                local3_bc[0:pn, None, :].to_broadcast([pn, DJ, F]), ALU.add).then_inc(D["n_pre"].sem, 1)
                wait_done(dve, D["n_pre"], g)
                wait_free(dve, D["n_row"], g)
                moments((D, "n", g, node_in, pn, DJ))

            pipeline(dve, DENSE_FULL, edges(
                spread[0], spread[1], (1, products), spread[2], (1, score_sums), spread[3])
                + [nodes(1, shifts(D, "n")), nodes(0, nodes_x3_more)])
            dve.wait_ge(L["score"].sem, L["score"].at(STEPS))
            link(v.tensor_copy(seg_max[:, :, :], alpha[:, :, :]))

            def hop(k, ahead):
                n = T - DOUBLINGS[k]
                a, b = (seg_max[:, T - n:T, :], seg_max[:, 0:n, :]) if ahead else (seg_max[:, 0:n, :], seg_max[:, T - n:T, :])
                link(v.tensor_tensor(tmp_a[:, 0:n, :], a, apart[:, k, 0:n, None].to_broadcast([P, n, HEADS]), ALU.add))
                link(v.tensor_tensor(b, b, tmp_a[:, 0:n, :], ALU.max))

            for ahead in (False, True):
                for k in range(len(DOUBLINGS)):
                    hop(k, ahead)
            for i, t in enumerate((0, T - 1)):
                for h in range(HEADS):
                    last = v.tensor_scalar(diag[:, 2 + i * HEADS + h, :], ident[:, :], seg_max[:, t, h:h + 1], None, ALU.mult)
            last.then_inc(max_at, 1)
            dve.wait_ge(max_at, 2)
            for i in range(4):
                row = ps[i % 2][0][:, :].rearrange("p (h q) -> p h q", q=P)
                link(v.tensor_tensor(max_row[:, 0, :, :], row, max_pen[:, i:i + 1, :].to_broadcast([P, HEADS, P]), ALU.add))
                link(v.tensor_reduce(max_extra[:, i, :], max_row[:, 0, :, :], axis=AX, op=ALU.max))
            v.tensor_tensor(max_extra[:, 0, :], max_extra[:, 0, :], max_extra[:, 1, :], ALU.max)
            link(v.tensor_tensor(max_extra[:, 2, :], max_extra[:, 2, :], max_extra[:, 3, :], ALU.max))
            for i, at in ((0, first), (2, last_)):
                link(v.tensor_scalar(tmp_t[:, :], d[:, 1:T + 1], at, None, ALU.is_equal))
                link(v.tensor_scalar(tmp_t[:, :], tmp_t[:, :], 1.0, LOW, ALU.subtract, ALU.mult))
                link(v.tensor_tensor(tmp_a[:, :, :], tmp_t[:, :, None].to_broadcast([P, T, HEADS]),
                                     max_extra[:, i:i + 1, :].to_broadcast([P, T, HEADS]), ALU.add))
                link(v.tensor_tensor(seg_max[:, :, :], seg_max[:, :, :], tmp_a[:, :, :], ALU.max))
            v.tensor_tensor(tmp_a[:, :, :], alpha[:, :, :], seg_max[:, :, :], ALU.subtract).then_inc(max_at, 2)
            dve.wait_ge(max_at, 5)

            L = flow["att2"]

            def attended_sums(g):
                wait_landed(dve, L["qin"], g)
                a = fours(alpha, g)
                v.tensor_tensor(msg[:, g.b, :, 0:F].rearrange("p j (h e) -> p j h e", e=HID),
                                src_rows[:, g.b, :, 0:F].rearrange("p j (h e) -> p j h e", e=HID),
                                a[:, :, :, None].to_broadcast([P, J, HEADS, HID]), ALU.mult)
                v.tensor_copy(msg[:, g.b, :, F:F + HEADS], a).then_inc(L["msgd"].sem, 1)
                wait_done(dve, L["msgd"], g)

            def attended(g, jn=J):
                wait_done(dve, L["accd"], g)
                v.tensor_scalar_max(recip[:, g.b, 0:jn, :], acc[:, g.b, 0:jn, F:ACC_W], 1e-30).then_inc(L["rcp"].sem, 1)
                wait_done(dve, L["rcp"], g)
                v.reciprocal(recip[:, g.b, 0:jn, :], recip[:, g.b, 0:jn, :]).then_inc(L["rcp2"].sem, 1)
                wait_done(dve, L["rcp2"], g)
                wait_free(dve, L["msg0"], g)
                v.tensor_tensor(pre[:, g.b, 0:jn, :].rearrange("p j (h e) -> p j h e", e=HID),
                                acc[:, g.b, 0:jn, 0:F].rearrange("p j (h e) -> p j h e", e=HID),
                                recip[:, g.b, 0:jn, :, None].to_broadcast([P, jn, HEADS, HID]), ALU.mult).then_inc(L["pre"].sem, 1)
                wait_done(dve, L["pre"], g)
                moments((L, "e", g, pre, P, jn))

            def x4_sums(g, jn=J):
                wait_done(dve, L["mm"], g)
                wait_free(dve, L["newd"], g)
                if g is FIX:
                    dve.wait_ge(fix_in, 48 * 4)
                else:
                    wait_landed(dve, L["own"], g)
                v.tensor_tensor(ny[:, g.b, 0:jn, :].rearrange("p j f -> p (j f)"), ps[3][g.b][:, 0:jn * F],
                                own_rows[:, g.b, 0:jn, :].rearrange("p j f -> p (j f)"), ALU.add).then_inc(L["pre2"].sem, 1)

            def x4_moments(g, jn=J):
                wait_done(dve, L["pre2"], g)
                moments((L, "a", g, ny, P, jn))

            att_shifts, x4_shifts = shifts(L, "e", False), shifts(L, "a", False)
            pipeline(dve, STEPS, edges(
                (6, x4_shifts), (2, att_shifts), (0, attended_sums),
                (0, running_sum(L, 0, msg, ACC_W)), (4, x4_sums), (0, running_sum(L, 1, msg, ACC_W)), (4, x4_moments),
                (0, running_sum(L, 2, msg, ACC_W)), (0, running_sum(L, 3, msg, ACC_W)), (0, attended)))
            fix_sums(L, ACC_W, 4)
            attended(FIX, 1)
            att_shifts(FIX, 1)
            x4_sums(FIX, 1)
            x4_moments(FIX, 1)
            x4_shifts(FIX, 1)


_INS = ["x", "src", "dst", "edge_attr_64", "L0_gnn_W", "L0_gnn_b", "L1_gnn_kernel", "L1_gnn_kernel_attention",
        "L2_gnn_W1l", "L2_gnn_b1", "L2_gnn_W1r", "L2_gnn_W2l", "L2_gnn_b2", "L2_gnn_W2r", "L3_gnn_qw", "L3_gnn_kw",
        "L3_gnn_ln_gamma", "L3_gnn_ln_beta", "L3_gnn_out_w", "L3_gnn_out_b"]


def kernel(**inputs):
    import numpy as _np
    import concourse.bacc as _bacc
    from concourse import mybir as _mybir
    from concourse.bass_utils import run_bass_kernel_spmd as _run

    nc = _bacc.Bacc("TRN2", target_bir_lowering=False, num_devices=1)
    arrays, args = {}, []
    for name in _INS:
        a = _np.ascontiguousarray(inputs[name])
        arrays[f"in_{name}_dram"] = a
        args.append(nc.dram_tensor(f"in_{name}_dram", a.shape, _mybir.dt.from_np(a.dtype), kind="ExternalInput").ap())
    out = nc.dram_tensor("out_0_dram", (N_NODES, F), _mybir.dt.float32, kind="ExternalOutput").ap()
    gnn_program(nc, *args, out)
    r = _run(nc, [arrays], core_ids=[0])
    return r.results[0]["out_0_dram"]
```
